# Optimizing a Trainium2 kernel written in Bass

```python
import numpy as np
import jax
import jax.numpy as jnp

def _softmax(x, axis=-1):
    return jax.nn.softmax(x, axis=axis)

def _gelu(x):
    return jax.nn.gelu(x, approximate=True)

def _silu(x):
    return jax.nn.silu(x)

def _sigmoid(x):
    return jax.nn.sigmoid(x)

def _layernorm(x, axis=-1, eps=1e-05):
    m = jnp.mean(x, axis=axis, keepdims=True)
    v = jnp.var(x, axis=axis, keepdims=True)
    return (x - m) / jnp.sqrt(v + eps)

def _scatter_add(tgt, idx, src, axis=0):
    return tgt.at[idx].add(src)

def _segment_sum(src, seg, n):
    return jax.ops.segment_sum(src, seg, n)
kernel_name = 'mk_hybrid_d1_jaxref_r4_9c7f5c'

def setup_inputs(seed: int=0):
    np.random.seed(seed)
    _w = jnp.asarray

    def _L0_attn_a_setup():
        import jax, jax.numpy as jnp
        import numpy as np
        DIM = 512
        HEAD_DIM = 128
        NH = DIM // HEAD_DIM
        CHUNK = 128

        def _forward(x, Wq, bq, Wk, bk, Wv, bv, Wbeta, bbeta, Walpha, balpha):
            B, T, D = x.shape
            H, S, C = (NH, HEAD_DIM, CHUNK)
            q = (x @ Wq + bq).reshape(B, T, H, S)
            k = (x @ Wk + bk).reshape(B, T, H, S)
            v = (x @ Wv + bv).reshape(B, T, H, S)
            k = k / jnp.maximum(jnp.linalg.norm(k, axis=-1, keepdims=True), 1e-12)
            alpha_val = jax.nn.sigmoid(x @ Walpha + balpha).reshape(B, T, H, 1)
            beta = jax.nn.softplus(x @ Wbeta + bbeta).reshape(B, T, H, 1)
            pad = -T % C

            def padt(t):
                return jnp.pad(t, ((0, 0), (0, pad), (0, 0), (0, 0))) if pad else t
            qp, kp, vp = (padt(q), padt(k), padt(v))
            ap, bp = (padt(alpha_val), padt(beta))
            Tp = T + pad
            n = Tp // C

            def ch(t):
                return t.reshape(B, n, C, H, t.shape[-1]).transpose(0, 1, 3, 2, 4)
            qc, kc, vc, bc = (ch(qp), ch(kp), ch(vp), ch(bp))
            cla = jnp.cumsum(jnp.log(ch(ap) + 1e-06), axis=3)
            decay = jnp.exp(cla - jnp.swapaxes(cla, -1, -2))
            causal = jnp.tril(jnp.ones((C, C), dtype=bool))
            decay = jnp.where(causal, decay, 0.0)
            attn = jnp.einsum('bnhcd,bnhed->bnhce', qc, kc) * jnp.swapaxes(bc, -1, -2) * decay
            y_local = jnp.einsum('bnhce,bnhed->bnhcd', attn, vc)
            chunk_decay = jnp.exp(cla)
            cla_end = cla[:, :, :, -1:, :]
            total_decay = jnp.exp(cla_end)
            decay_to_end = jnp.exp(cla_end - cla)
            kw = kc * bc * decay_to_end
            delta = jnp.einsum('bnhcd,bnhce->bnhde', vc, kw)
            state0 = jnp.zeros((B, H, S, S), x.dtype)

            def step(state, inp):
                q_i, yloc_i, cd_i, td_i, d_i = inp
                y_glob = jnp.einsum('bhce,bhde->bhcd', q_i, state) * cd_i
                new_state = state * td_i + d_i
                return (new_state, y_glob + yloc_i)
            xs = (jnp.moveaxis(qc, 1, 0), jnp.moveaxis(y_local, 1, 0), jnp.moveaxis(chunk_decay, 1, 0), jnp.moveaxis(total_decay, 1, 0), jnp.moveaxis(delta, 1, 0))
            final_state, y_chunks = jax.lax.scan(step, state0, xs)
            y = jnp.moveaxis(y_chunks, 0, 1)
            y = y.transpose(0, 1, 3, 2, 4).reshape(B, Tp, D)[:, :T, :]
            surprise = jnp.linalg.norm(y_local, axis=-1).mean(axis=-1)
            surprise = surprise.reshape(B, -1, 1).mean(axis=1, keepdims=True)
            return (y, final_state, surprise, alpha_val)

        def _reference_tuple_inner(x, Wq, bq, Wk, bk, Wv, bv, Wbeta, bbeta, Walpha, balpha):
            return _forward(x, Wq, bq, Wk, bk, Wv, bv, Wbeta, bbeta, Walpha, balpha)
        key = jax.random.key(seed)
        ks = jax.random.split(key, 6)
        B, T = (2, 1024)
        s = 1.0 / np.sqrt(DIM)

        def lin(k, out_dim):
            k1, k2 = jax.random.split(k)
            W = jax.random.uniform(k1, (DIM, out_dim), minval=-s, maxval=s, dtype=jnp.float32)
            b = jax.random.uniform(k2, (out_dim,), minval=-s, maxval=s, dtype=jnp.float32)
            return (W, b)
        Wq, bq = lin(ks[0], NH * HEAD_DIM)
        Wk, bk = lin(ks[1], NH * HEAD_DIM)
        Wv, bv = lin(ks[2], NH * HEAD_DIM)
        Wbeta, bbeta = lin(ks[3], NH)
        Walpha, _ = lin(ks[4], NH)
        balpha = jnp.full((NH,), 2.0, dtype=jnp.float32)
        x = jax.random.normal(ks[5], (B, T, DIM), dtype=jnp.float32)
        return {'x': x, 'Wq': Wq, 'bq': bq, 'Wk': Wk, 'bk': bk, 'Wv': Wv, 'bv': bv, 'Wbeta': Wbeta, 'bbeta': bbeta, 'Walpha': Walpha, 'balpha': balpha}
    _L0_attn_a_in = _L0_attn_a_setup()

    def _L0_attn_b_setup():
        import jax, jax.numpy as jnp
        import numpy as np
        D_MODEL = 512
        B, S = (2, 512)
        key = jax.random.key(seed)
        kx, kq, kk, kv, ko = jax.random.split(key, 5)
        std = 1.0 / np.sqrt(D_MODEL)
        return {'x': jax.random.normal(kx, (B, S, D_MODEL), dtype=jnp.float32), 'W_q': jax.random.normal(kq, (D_MODEL, D_MODEL), dtype=jnp.float32) * std, 'W_k': jax.random.normal(kk, (D_MODEL, D_MODEL), dtype=jnp.float32) * std, 'W_v': jax.random.normal(kv, (D_MODEL, D_MODEL), dtype=jnp.float32) * std, 'W_o': jax.random.normal(ko, (D_MODEL, D_MODEL), dtype=jnp.float32) * std}
    _L0_attn_b_in = _L0_attn_b_setup()

    def _L0_ffn_setup():
        import jax, jax.numpy as jnp
        import numpy as np
        DIM = 512
        HID = 1408
        ZERO_POINT = 128.0

        def _qlinear(x, wq, scale):
            W = (wq.astype(jnp.float32) - ZERO_POINT) * scale[:, None]
            return jnp.einsum('bsd,hd->bsh', x, W)
        key = jax.random.key(seed)
        ks = jax.random.split(key, 7)
        B, S = (4, 512)
        sg = jax.random.uniform(ks[1], (HID,)) * (0.02 / np.sqrt(DIM)) + 0.0001
        su = jax.random.uniform(ks[3], (HID,)) * (0.02 / np.sqrt(DIM)) + 0.0001
        sd = jax.random.uniform(ks[5], (DIM,)) * (0.02 / np.sqrt(HID)) + 0.0001
        return {'x': jax.random.normal(ks[0], (B, S, DIM), dtype=jnp.float32), 'wq_gate': jax.random.randint(ks[2], (HID, DIM), 0, 64, dtype=jnp.int32), 's_gate': sg, 'wq_up': jax.random.randint(ks[4], (HID, DIM), 0, 64, dtype=jnp.int32), 's_up': su, 'wq_down': jax.random.randint(ks[6], (DIM, HID), 0, 64, dtype=jnp.int32), 's_down': sd}
    _L0_ffn_in = _L0_ffn_setup()
    _d = {'L0_attn_a_x': _L0_attn_a_in['x'], 'L0_attn_a_Wq': _L0_attn_a_in['Wq'], 'L0_attn_a_bq': _L0_attn_a_in['bq'], 'L0_attn_a_Wk': _L0_attn_a_in['Wk'], 'L0_attn_a_bk': _L0_attn_a_in['bk'], 'L0_attn_a_Wv': _L0_attn_a_in['Wv'], 'L0_attn_a_bv': _L0_attn_a_in['bv'], 'L0_attn_a_Wbeta': _L0_attn_a_in['Wbeta'], 'L0_attn_a_bbeta': _L0_attn_a_in['bbeta'], 'L0_attn_a_Walpha': _L0_attn_a_in['Walpha'], 'L0_attn_a_balpha': _L0_attn_a_in['balpha'], 'L0_attn_b_W_q': _L0_attn_b_in['W_q'], 'L0_attn_b_W_k': _L0_attn_b_in['W_k'], 'L0_attn_b_W_v': _L0_attn_b_in['W_v'], 'L0_attn_b_W_o': _L0_attn_b_in['W_o'], 'L0_ffn_wq_gate': _L0_ffn_in['wq_gate'], 'L0_ffn_s_gate': _L0_ffn_in['s_gate'], 'L0_ffn_wq_up': _L0_ffn_in['wq_up'], 'L0_ffn_s_up': _L0_ffn_in['s_up'], 'L0_ffn_wq_down': _L0_ffn_in['wq_down'], 'L0_ffn_s_down': _L0_ffn_in['s_down']}
    _x0 = _d['L0_attn_a_x']
    _d['L0_attn_a_x'] = jax.random.normal(jax.random.fold_in(jax.random.key(seed), 1), (2, 1024, 512), dtype=_x0.dtype)
    del _x0
    return _d

def reference(L0_attn_a_x, L0_attn_a_Wq, L0_attn_a_bq, L0_attn_a_Wk, L0_attn_a_bk, L0_attn_a_Wv, L0_attn_a_bv, L0_attn_a_Wbeta, L0_attn_a_bbeta, L0_attn_a_Walpha, L0_attn_a_balpha, L0_attn_b_W_q, L0_attn_b_W_k, L0_attn_b_W_v, L0_attn_b_W_o, L0_ffn_wq_gate, L0_ffn_s_gate, L0_ffn_wq_up, L0_ffn_s_up, L0_ffn_wq_down, L0_ffn_s_down):

    def _L0_attn_a_ref(x, Wq, bq, Wk, bk, Wv, bv, Wbeta, bbeta, Walpha, balpha):
        import jax, jax.numpy as jnp
        import numpy as np
        DIM = 512
        HEAD_DIM = 128
        NH = DIM // HEAD_DIM
        CHUNK = 128

        def _forward(x, Wq, bq, Wk, bk, Wv, bv, Wbeta, bbeta, Walpha, balpha):
            B, T, D = x.shape
            H, S, C = (NH, HEAD_DIM, CHUNK)
            q = (x @ Wq + bq).reshape(B, T, H, S)
            k = (x @ Wk + bk).reshape(B, T, H, S)
            v = (x @ Wv + bv).reshape(B, T, H, S)
            k = k / jnp.maximum(jnp.linalg.norm(k, axis=-1, keepdims=True), 1e-12)
            alpha_val = jax.nn.sigmoid(x @ Walpha + balpha).reshape(B, T, H, 1)
            beta = jax.nn.softplus(x @ Wbeta + bbeta).reshape(B, T, H, 1)
            pad = -T % C

            def padt(t):
                return jnp.pad(t, ((0, 0), (0, pad), (0, 0), (0, 0))) if pad else t
            qp, kp, vp = (padt(q), padt(k), padt(v))
            ap, bp = (padt(alpha_val), padt(beta))
            Tp = T + pad
            n = Tp // C

            def ch(t):
                return t.reshape(B, n, C, H, t.shape[-1]).transpose(0, 1, 3, 2, 4)
            qc, kc, vc, bc = (ch(qp), ch(kp), ch(vp), ch(bp))
            cla = jnp.cumsum(jnp.log(ch(ap) + 1e-06), axis=3)
            decay = jnp.exp(cla - jnp.swapaxes(cla, -1, -2))
            causal = jnp.tril(jnp.ones((C, C), dtype=bool))
            decay = jnp.where(causal, decay, 0.0)
            attn = jnp.einsum('bnhcd,bnhed->bnhce', qc, kc) * jnp.swapaxes(bc, -1, -2) * decay
            y_local = jnp.einsum('bnhce,bnhed->bnhcd', attn, vc)
            chunk_decay = jnp.exp(cla)
            cla_end = cla[:, :, :, -1:, :]
            total_decay = jnp.exp(cla_end)
            decay_to_end = jnp.exp(cla_end - cla)
            kw = kc * bc * decay_to_end
            delta = jnp.einsum('bnhcd,bnhce->bnhde', vc, kw)
            state0 = jnp.zeros((B, H, S, S), x.dtype)

            def step(state, inp):
                q_i, yloc_i, cd_i, td_i, d_i = inp
                y_glob = jnp.einsum('bhce,bhde->bhcd', q_i, state) * cd_i
                new_state = state * td_i + d_i
                return (new_state, y_glob + yloc_i)
            xs = (jnp.moveaxis(qc, 1, 0), jnp.moveaxis(y_local, 1, 0), jnp.moveaxis(chunk_decay, 1, 0), jnp.moveaxis(total_decay, 1, 0), jnp.moveaxis(delta, 1, 0))
            final_state, y_chunks = jax.lax.scan(step, state0, xs)
            y = jnp.moveaxis(y_chunks, 0, 1)
            y = y.transpose(0, 1, 3, 2, 4).reshape(B, Tp, D)[:, :T, :]
            surprise = jnp.linalg.norm(y_local, axis=-1).mean(axis=-1)
            surprise = surprise.reshape(B, -1, 1).mean(axis=1, keepdims=True)
            return (y, final_state, surprise, alpha_val)

        def _reference_tuple_inner(x, Wq, bq, Wk, bk, Wv, bv, Wbeta, bbeta, Walpha, balpha):
            return _forward(x, Wq, bq, Wk, bk, Wv, bv, Wbeta, bbeta, Walpha, balpha)
        return _reference_tuple_inner(x, Wq, bq, Wk, bk, Wv, bv, Wbeta, bbeta, Walpha, balpha)[0]

    def _L0_attn_b_ref(x, W_q, W_k, W_v, W_o):
        import jax, jax.numpy as jnp
        import numpy as np
        D_MODEL = 512
        B, S = (2, 512)
        scale = 1.0 / jnp.sqrt(jnp.asarray(x.shape[-1], x.dtype))
        Q = jnp.einsum('bsd,de->bse', x, W_q)
        K = jnp.einsum('bsd,de->bse', x, W_k)
        V = jnp.einsum('bsd,de->bse', x, W_v)
        scores = jnp.einsum('bqe,bke->bqk', Q, K) * scale
        attn = jax.nn.softmax(scores, axis=-1)
        out = jnp.einsum('bqk,bke->bqe', attn, V)
        return jnp.einsum('bse,ed->bsd', out, W_o)

    def _L0_ffn_ref(x, wq_gate, s_gate, wq_up, s_up, wq_down, s_down):
        import jax, jax.numpy as jnp
        import numpy as np
        DIM = 512
        HID = 1408
        ZERO_POINT = 128.0

        def _qlinear(x, wq, scale):
            W = (wq.astype(jnp.float32) - ZERO_POINT) * scale[:, None]
            return jnp.einsum('bsd,hd->bsh', x, W)
        gate = _qlinear(x, wq_gate, s_gate)
        gate = jax.nn.silu(gate)
        up = _qlinear(x, wq_up, s_up)
        return _qlinear(gate * up, wq_down, s_down)
    x = L0_attn_a_x
    x = x + _L0_attn_a_ref(_layernorm(x, axis=-1), L0_attn_a_Wq, L0_attn_a_bq, L0_attn_a_Wk, L0_attn_a_bk, L0_attn_a_Wv, L0_attn_a_bv, L0_attn_a_Wbeta, L0_attn_a_bbeta, L0_attn_a_Walpha, L0_attn_a_balpha)
    x = x + _L0_ffn_ref(_layernorm(x, axis=-1), L0_ffn_wq_gate, L0_ffn_s_gate, L0_ffn_wq_up, L0_ffn_s_up, L0_ffn_wq_down, L0_ffn_s_down)
    x = x + _L0_attn_b_ref(_layernorm(x, axis=-1), L0_attn_b_W_q, L0_attn_b_W_k, L0_attn_b_W_v, L0_attn_b_W_o)
    x = x + _L0_ffn_ref(_layernorm(x, axis=-1), L0_ffn_wq_gate, L0_ffn_s_gate, L0_ffn_wq_up, L0_ffn_s_up, L0_ffn_wq_down, L0_ffn_s_down)
    return x

_drawn_inputs = setup_inputs


def setup_inputs(seed=0):
    import zlib

    import numpy as np

    out = dict(_drawn_inputs(seed))
    spreads = {'L0_attn_a_balpha': (2.0, 0.2)}
    factors = {'L0_attn_a_bq': 2.868, 'L0_attn_a_bk': 2.834, 'L0_attn_a_bbeta': 8.0}
    for name, (base, spread) in spreads.items():
        noise = np.random.default_rng([zlib.crc32(name.encode()), seed]).standard_normal(out[name].shape)
        drawn = base * np.exp(spread * noise) if base else spread * noise
        out[name] = jnp.asarray(drawn.astype(out[name].dtype))
    for name, factor in factors.items():
        out[name] = (out[name] * factor).astype(out[name].dtype)
    return out
```

```python
from contextlib import ExitStack

import concourse.bass as bass
from concourse import mybir

F32 = mybir.dt.float32
F32R = mybir.dt.float32r
BF16 = mybir.dt.bfloat16
I32 = mybir.dt.int32
ALU = mybir.AluOpType
ACT = mybir.ActivationFunctionType
AX = mybir.AxisListType

P = 128
BATCHES = 2
TOKENS = 2048
D = 512
KT = D // P
HEADS = D // P
HID = 1408
JT = HID // P
GT = 4
GROUP = GT * P
BT = 2 * GT
BTOK = BT * P
ZERO_POINT = 128.0
LN_EPS = 1e-5
NORM_FLOOR = 1e-12
SCALE = float(D) ** -0.5
MASKED = -30000.0
RING = 2

BODIES = [("start", 1, {2: 4}),
          ("A", 2, {0: 13, 1: 13, 2: 8, 3: 12, 4: 8, 5: 16, 6: 8, 7: 8}),
          ("F1", 2, {0: 22, 1: 22, 2: 4, 3: 4, 4: 2, 5: 2, 6: 2, 7: 2}),
          ("mid", 1, {0: 4, 1: 4}),
          ("B", 2, {0: 12, 1: 12, 2: 8, 4: 8, 6: 4, 7: 4}),
          ("F2", 2, {0: 22, 1: 22, 2: 4, 3: 4, 4: 2, 5: 2, 6: 2, 7: 2})]
LN_BASE = {"start": 0, "A": 4, "F1": 20, "B": 36, "F2": 52}
FFN_BASE = {"F1": 0, "F2": 1}


def fills_before(phase, bank):
    total = 0
    for name, times, uses in BODIES:
        if name == phase:
            return total
        total += times * uses.get(bank, 0)
    raise ValueError(phase)


def turn(phase, bank, b, i):
    per = {name: uses for name, _, uses in BODIES}[phase][bank]
    return b * per + (fills_before(phase, bank) + i + 1)


def hybrid_layer_kernel(nc, x, wq, wk, wv, w_ab, bq, bk, bv, b_ab,
                        wqT, wkT, wvT, wo, gateT, s_gate, upT, s_up, downT, s_down, out):
    base = (nc.sbuf_base + 63) // 64 * 64

    def at(name, offset, cols, dtype=F32):
        return nc.alloc_sbuf_tensor_at(name, [P, cols], dtype, offset=base + offset)

    xres = at("xres", 0, 16 * D)
    codes_gu = at("codes_gu", 32768, 8 * HID, I32)
    w_gu = at("w_gu", 32768, 8 * HID, F32R)
    xt_hi = at("xt_hi", 77824, KT * BTOK, F32R)
    xt_lo = at("xt_lo", 94208, KT * BTOK, F32R)
    R1, W2, CONST = 110592, 143360, 204800
    ident = at("ident", CONST, P)
    sd_rows = at("sd_rows", CONST + 512, D)
    ab_row = at("ab_row", CONST + 512, GROUP)
    xn = at("xn", CONST + 2560, 2 * D)
    sg_col = at("sg_col", CONST + 6656, JT)
    su_col = at("su_col", CONST + 6720, JT)
    ln_bn = at("ln_bn", CONST + 6784, 4 * 6)
    ln_mv = at("ln_mv", CONST + 6912, 4 * 2)
    ln_var = at("ln_var", CONST + 6944, 4)
    ln_rstd = at("ln_rstd", CONST + 6976, 4)
    minus_half = at("minus_half", CONST + 7008, 4)
    smax = at("smax", CONST + 7040, 2)
    nmax = at("nmax", CONST + 7072, 2)
    rowsum = at("rowsum", CONST + 7104, 2)
    rden = at("rden", CONST + 7136, 2)

    wqk_hi = at("wqk_hi", R1, 2 * KT * D, F32R)
    wqk_raw = at("wqk_raw", R1 + 16384, 2 * KT * D)
    wqk_lo = at("wqk_lo", R1 + 16384, 2 * KT * D, F32R)
    wv_hi = at("wv_hi", W2, KT * D, F32R)
    wv_raw = at("wv_raw", W2 + 8192, KT * D)
    wv_lo = at("wv_lo", W2 + 8192, KT * D, F32R)
    bk_rows = at("bk_rows", W2 + 16384, D)
    bv_rows = at("bv_rows", W2 + 18432, D)
    qT = at("qT", W2 + 20480, HEADS * GROUP)
    kn = at("kn", W2 + 28672, 2 * D)
    kT = at("kT", W2 + 32768, D)
    vn = at("vn", W2 + 34816, 2 * D)
    decay = at("decay", W2 + 38912, D)
    attnT = at("attnT", W2 + 40960, D)
    kw = at("kw", W2 + 43008, D)
    steps_hi = at("steps_hi", W2 + 45056, D, F32R)
    steps_lo = at("steps_lo", W2 + 47104, D, F32R)
    state = at("state", W2 + 49152, D)
    g_z = at("g_z", W2 + 51200, 32)
    g_zz = at("g_zz", W2 + 51328, 32)
    g_e = at("g_e", W2 + 51456, 32)
    g_u = at("g_u", W2 + 51584, 32)
    g_r = at("g_r", W2 + 51712, 32)
    g_a = at("g_a", W2 + 51840, 16)
    g_la = at("g_la", W2 + 51904, 16)
    g_lb = at("g_lb", W2 + 51968, 16)
    g_c = at("g_c", W2 + 52032, 16)
    g_c2 = at("g_c2", W2 + 52096, 16)
    g_zm = at("g_zm", W2 + 52160, 16)
    beta = at("beta", W2 + 52224, 32)
    la_hi = at("la_hi", W2 + 52352, 32, F32R)
    la_lo = at("la_lo", W2 + 52480, 32, F32R)
    negcla = at("negcla", W2 + 52608, 32)
    decays = at("decays", W2 + 52736, 64)
    sumsq = at("sumsq", W2 + 52992, 8)
    kscale = at("kscale", W2 + 53024, 8)
    ab_bias = at("ab_bias", W2 + 53056, 8)
    bq_col = at("bq_col", W2 + 53088, 4)
    squares = at("squares", W2 + 53248, P)
    tri = at("tri", W2 + 53760, P)
    tri_r = at("tri_r", W2 + 54272, P, F32R)
    ones = at("ones", W2 + 54784, P)
    ones_r = at("ones_r", W2 + 55296, P, F32R)
    ident_b = at("ident_b", W2 + 55808, P, BF16)
    mask_b = at("mask_b", W2 + 56064, D, BF16)
    wab_hi = at("wab_hi", W2 + 57088, KT * P, F32R)
    wab_raw = at("wab_raw", W2 + 59136, KT * P)
    wab_lo = at("wab_lo", W2 + 59136, KT * P, F32R)

    codes_d = {"F1": at("codes_d1", R1, JT * D, I32), "F2": at("codes_d2", W2, JT * D, I32)}
    w_d = {"F1": at("w_d1", R1, JT * D, F32R), "F2": at("w_d2", W2, JT * D, F32R)}
    silu = at("silu", W2 + 40960, 2 * GROUP)
    hid = at("hid", W2 + 45056, 2 * GROUP)
    hid_hi = at("hid_hi", W2 + 49152, 2 * GROUP, F32R)
    hid_lo = at("hid_lo", W2 + 53248, 2 * GROUP, F32R)
    yt = at("yt", W2 + 57344, 2 * D)

    qk_hi = at("qk_hi", W2, 2 * KT * D, F32R)
    qk_raw = at("qk_raw", W2 + 16384, 2 * KT * D)
    qk_lo = at("qk_lo", W2 + 16384, 2 * KT * D, F32R)
    vo_hi = at("vo_hi", R1, 2 * KT * D, F32R)
    vo_raw = at("vo_raw", R1 + 16384, 2 * KT * D)
    vo_lo = at("vo_lo", R1 + 16384, 2 * KT * D, F32R)
    g_hi = at("g_hi", W2 + 32768, KT * D, F32R)
    g_lo = at("g_lo", W2 + 40960, KT * D, F32R)
    wvo_hi = at("wvo_hi", W2, KT * D, F32R)
    wvo_lo = at("wvo_lo", W2 + 8192, KT * D, F32R)
    aT_hi = at("aT_hi", W2 + 16384, KT * GROUP, F32R)
    aT_lo = at("aT_lo", W2 + 24576, KT * GROUP, F32R)
    v_hi = at("v_hi", R1, BT * D, F32R)
    v_lo = at("v_lo", R1 + 16384, BT * D, F32R)
    probs = at("probs", W2 + 49152, BTOK)
    pT_hi = at("pT_hi", W2 + 53248, BTOK, F32R)
    pT_lo = at("pT_lo", W2 + 57344, BTOK, F32R)

    psum = nc.alloc_psum_tensor("psum", [P, 8 * 512], F32)

    def bank(i, n=1):
        return psum[:, i * 512:(i + n) * 512]

    def sem(name):
        return nc.alloc_semaphore(name)

    filled = [sem(f"psum_filled{i}") for i in range(8)]
    drained = [sem(f"psum_drained{i}") for i in range(8)]
    x_in = sem("x_in")
    x_rest_in = sem("x_rest_in")
    wab_zero = sem("wab_zero")
    wab_in = sem("wab_in")
    wk_in = sem("wk_in")
    wv_in = sem("wv_in")
    wq_in = sem("wq_in")
    rows_in = sem("rows_in")
    gu_in = sem("gu_in")
    qk_in = sem("qk_in")
    vo_in = sem("vo_in")
    d_in = {"F1": sem("d1_in"), "F2": sem("d2_in")}
    sd_in = sem("sd_in")
    x_out = sem("x_out")
    consts_set = sem("consts_set")
    consts_done = sem("consts_done")
    wa_hi = sem("wa_hi")
    wa_lo = sem("wa_lo")
    ln_bn_done = sem("ln_bn_done")
    ln_mv_done = sem("ln_mv_done")
    ln_var_done = sem("ln_var_done")
    ln_rstd_done = sem("ln_rstd_done")
    ln_xn_done = sem("ln_xn_done")
    xt_hi_done = sem("xt_hi_done")
    gate_dve = sem("gate_dve")
    gate_act = sem("gate_act")
    squares_done = sem("squares_done")
    squares_step = sem("squares_step")
    kscale_step = sem("kscale_step")
    k_scaled = sem("k_scaled")
    kw_ready = sem("kw_ready")
    steps_ready = sem("steps_ready")
    state_zero = sem("state_zero")
    gu_ready = sem("gu_ready")
    wd_ready = {"F1": sem("wd1_ready"), "F2": sem("wd2_ready")}
    hid_hi_ready = sem("hid_hi_ready")
    hid_split = sem("hid_split")
    down_done = sem("down_done")
    x_updated = sem("x_updated")
    qk_split = sem("qk_split")
    vo_hi_done = sem("vo_hi_done")
    vo_split = sem("vo_split")
    hi_done = sem("hi_done")
    pT_hi_done = sem("pT_hi_done")
    smax_done = sem("smax_done")
    nmax_done = sem("nmax_done")
    rden_done = sem("rden_done")

    def a_job(s, i):
        n = 13 * s + i
        return n % 2, n // 2

    def k_job(s, c):
        return a_job(s, 1 if c == 0 else 5 + 2 * c)

    def v_job(s, c):
        return a_job(s, 2 if c == 0 else 6 + 2 * c)

    PREP = {"start": lambda l: (2, l), "A": lambda l: (2, l), "F1": lambda l: (2 + l % 2, l // 2),
            "F2": lambda l: (2 + l % 2, l // 2),
            "B": lambda l: ((l if l < 4 else 16 + l) % 2, (l if l < 4 else 16 + l) // 2)}

    def prep_use(phase, l):
        return PREP[phase](l)

    def prep_x(phase, b, l):
        if phase == "start":
            return xres[:, l * D:(l + 1) * D]
        if l < 4:
            return xres[:, bass.ds(b * (BT * D) + (4 + l) * D, D)]
        return xres[:, bass.ds(other_batch[0] + (l - 4) * D, D)]

    def prep_col(phase, l):
        return l * P if phase == "start" else ((l + 4) % 8) * P

    def xt_tile(t, col):
        return t[:, :].rearrange("p (k n) -> p k n", k=KT)[:, :, col:col + P]

    def ln_n(phase, b, l):
        return b * 8 + (LN_BASE[phase] + l)

    waits_alone = sem("waits_alone")

    def alone(eng):
        eng.sem_inc(waits_alone, 1)

    other_batch = [None]

    class Use:

        def __init__(self, eng, phase, b):
            self.eng, self.phase, self.b = eng, phase, b

        def value(self, use):
            return turn(self.phase, use[0], self.b, use[1])

        def free(self, use):
            self.eng.wait_ge(drained[use[0]], self.value(use))

        def full(self, use):
            self.eng.wait_ge(filled[use[0]], self.value(use))

        def read_out(self, use):
            self.eng.wait_ge(drained[use[0]], self.value(use) + 1)

    block = nc.Block()

    def cols(t, i, n=D):
        return t[:, i * n:(i + 1) * n]

    with block as blk:
        @blk.sync
        def _(sp):
            for i in range(8):
                sp.sem_inc(drained[i], 1)
            for s in (hid_split, x_updated):
                sp.sem_inc(s, RING)
            xv = x.rearrange("(g t p) d -> g p t d", p=P, t=GT)
            xs = [xres[:, g * GT * D:(g + 1) * GT * D].rearrange("p (t d) -> p t d", d=D) for g in range(4)]

            def weights(dst, src, s):
                sp.dma_start(dst.rearrange("p (k n) -> p k n", k=src.shape[0] // P),
                             src.rearrange("(k p) n -> p k n", p=P)).then_inc(s, 16)

            sp.dma_start(xs[0], xv[0]).then_inc(x_in, 16)
            sp.wait_ge(wab_zero, 1)
            wab = wab_raw[:, :].rearrange("p (k n) -> p k n", k=KT)
            sp.dma_start(wab[:, :, 0:2 * HEADS], w_ab.rearrange("(k p) n -> p k n", p=P)).then_inc(wab_in, 16)
            weights(wqk_raw[:, KT * D:2 * KT * D], wk, wk_in)
            sp.dma_start(bk_rows[:, :], bk.partition_broadcast(P)).then_inc(rows_in, 16)
            sp.dma_start(bv_rows[:, :], bv.partition_broadcast(P)).then_inc(rows_in, 16)
            sp.dma_start(ab_bias[:, :], b_ab.partition_broadcast(P)).then_inc(rows_in, 16)
            sp.dma_start(bq_col[:, :], bq).then_inc(rows_in, 16)
            weights(wv_raw[:, :], wv, wv_in)
            weights(wqk_raw[:, 0:KT * D], wq, wq_in)
            for g in range(1, 4):
                sp.dma_start(xs[g], xv[g]).then_inc(x_rest_in, 16)
            sp.dma_start(sg_col[:, :], s_gate).then_inc(rows_in, 16)
            sp.dma_start(su_col[:, :], s_up).then_inc(rows_in, 16)
            weights(codes_gu[:, 0:4 * HID], gateT, gu_in)
            weights(codes_gu[:, 4 * HID:8 * HID], upT, gu_in)
            use = Use(sp, "A", 1)
            for bnk in (0, 1):
                use.full((bnk, 12))
            weights(codes_d["F1"][:, :], downT, d_in["F1"])
            use.read_out((7, 7))
            sp.dma_start(sd_rows[:, :], s_down.partition_broadcast(P)).then_inc(sd_in, 16)
            weights(qk_raw[:, 0:KT * D], wqT, qk_in)
            weights(qk_raw[:, KT * D:2 * KT * D], wkT, qk_in)
            use = Use(sp, "F1", 1)
            use.full((7, 1))
            weights(vo_raw[:, 0:KT * D], wvT, vo_in)
            weights(vo_raw[:, KT * D:2 * KT * D], wo, vo_in)
            use = Use(sp, "B", 1)
            use.full((0, 9))
            use.full((1, 9))
            use.full((4, 7))
            weights(codes_d["F2"][:, :], downT, d_in["F2"])
            ov = out.rearrange("(g t p) d -> g p t d", p=P, t=GT)
            for g in range(4):
                sp.wait_ge(x_updated, RING + 16 + 4 * (g + 1))
                sp.dma_start(ov[g], xs[g]).then_inc(x_out, 16)
            sp.wait_ge(x_out, 4 * 16)

        @blk.gpsimd
        def _(pool):
            def rstd(n, slot):
                pool.wait_ge(ln_var_done, n + 1)
                nc.gpsimd.tensor_tensor(ln_rstd[:, slot:slot + 1], ln_var[:, slot:slot + 1],
                                        minus_half[:, 0:1], ALU.pow).then_inc(ln_rstd_done, 1)

            nc.gpsimd.memset(wab_raw[:, :], 0.0).then_inc(wab_zero, 1)
            nc.gpsimd.memset(minus_half[:, :], -0.5).then_inc(consts_set, 1)
            nc.gpsimd.memset(ident[:, :], 0.0).then_inc(consts_set, 1)
            nc.gpsimd.memset(ident_b[:, :], 0.0).then_inc(consts_set, 1)
            nc.gpsimd.memset(tri[:, :], 1.0).then_inc(consts_set, 1)
            nc.gpsimd.memset(ones[:, :], 1.0).then_inc(consts_set, 1)
            nc.gpsimd.memset(ones_r[:, :].bitcast(F32), 1.0).then_inc(consts_set, 1)
            nc.gpsimd.memset(mask_b[:, :], 0.0).then_inc(consts_set, 1)
            pool.wait_ge(consts_set, 7)
            for m in (ident, ident_b):
                nc.gpsimd.affine_select(out=m[:, :], in_=m[:, :], compare_op=ALU.not_equal, fill=1.0,
                                        base=0, pattern=[[-1, P]], channel_multiplier=1).then_inc(consts_done, 1)
            nc.gpsimd.affine_select(out=tri[:, :], in_=tri[:, :], compare_op=ALU.is_ge, fill=0.0,
                                    base=0, pattern=[[1, P]], channel_multiplier=-1).then_inc(consts_done, 1)
            mv = mask_b[:, :].rearrange("p (h c) -> p h c", h=HEADS)
            nc.gpsimd.affine_select(out=mv, in_=mv, compare_op=ALU.is_ge, fill=MASKED,
                                    base=0, pattern=[[0, HEADS], [1, P]], channel_multiplier=-1).then_inc(consts_done, 1)
            pool.wait_ge(consts_done, 4)
            nc.gpsimd.tensor_copy(tri_r[:, :], tri[:, :]).then_inc(consts_done, 1)
            pool.wait_ge(consts_done, 5)
            for l in range(4):
                rstd(l, l)

            with pool.Fori(0, BATCHES) as b:
                def scale_k(s, c):
                    n = b * 8 + (4 * s + c)
                    r = 4 * (c % 2)
                    pool.wait_ge(squares_done, n + 1)
                    alone(pool)
                    nc.gpsimd.tensor_scalar(kscale[:, r:r + 4], sumsq[:, r:r + 4], NORM_FLOOR ** 2, None,
                                            ALU.max).then_inc(kscale_step, 1)
                    pool.wait_ge(kscale_step, n * 3 + 1)
                    nc.gpsimd.tensor_tensor(kscale[:, r:r + 4], kscale[:, r:r + 4], minus_half[:, :],
                                            ALU.pow).then_inc(kscale_step, 1)
                    pool.wait_ge(kscale_step, n * 3 + 2)
                    if c == 0:
                        pool.wait_ge(gate_dve, b * 20 + (10 * s + 8))
                    nc.gpsimd.tensor_tensor(kscale[:, r:r + 4], kscale[:, r:r + 4],
                                            beta[:, 16 * s + 4 * c:16 * s + 4 * c + 4],
                                            ALU.mult).then_inc(kscale_step, 1)
                    pool.wait_ge(kscale_step, n * 3 + 3)
                    kv = cols(kn, c % 2).rearrange("p (h d) -> p h d", h=HEADS)
                    nc.gpsimd.tensor_tensor(kv, kv, kscale[:, r:r + 4].unsqueeze(2).broadcast_to([P, HEADS, P]),
                                            ALU.mult).then_inc(k_scaled, 1)

                def log_steps(s, c):
                    if c == 0:
                        pool.wait_ge(gate_dve, b * 20 + (10 * s + 10))
                    tv = tri_r[:, :].bitcast(F32).unsqueeze(1).broadcast_to([P, HEADS, P])
                    for dst, src in ((steps_hi, la_hi), (steps_lo, la_lo)):
                        sv = src[:, 16 * s + 4 * c:16 * s + 4 * c + 4].bitcast(F32)
                        nc.gpsimd.tensor_tensor(dst[:, :].rearrange("p (h d) -> p h d", h=HEADS),
                                                sv.unsqueeze(2).broadcast_to([P, HEADS, P]), tv,
                                                ALU.mult).then_inc(steps_ready, 1)

                def weight_k(s, c):
                    u = Use(pool, "A", b)
                    u.read_out((4, 4 * s + c))
                    kv = cols(kn, c % 2).rearrange("p (h d) -> p h d", h=HEADS)
                    dv = decay[:, :].rearrange("p (h d) -> p h d", h=HEADS)[:, :, P - 1:P]
                    nc.gpsimd.tensor_tensor(kw[:, :].rearrange("p (h d) -> p h d", h=HEADS), kv,
                                            dv.broadcast_to([P, HEADS, P]), ALU.mult).then_inc(kw_ready, 1)

                for s in range(2):
                    if s == 0:
                        scale_k(0, 0)
                        log_steps(0, 0)
                    for c in range(4):
                        if c < 2:
                            for l in (4 * s + 2 * c, 4 * s + 2 * c + 1):
                                rstd(ln_n("A", b, l), l % 4)
                        if c < 3:
                            scale_k(s, c + 1)
                        weight_k(s, c)
                        if c < 3:
                            log_steps(s, c + 1)
                        elif s == 0:
                            scale_k(1, 0)
                            log_steps(1, 0)

            def ffn(phase):
                nd = 5 if phase == "F1" else 5
                pool.wait_ge(d_in[phase], 16)
                nc.gpsimd.tensor_scalar(w_d[phase][:, (JT - nd) * D:], codes_d[phase][:, (JT - nd) * D:],
                                        -ZERO_POINT, None, ALU.add).then_inc(wd_ready[phase], 1)
                pool.wait_ge(qk_in, 32)
                with pool.Fori(0, BATCHES) as b:
                    def add_y(s, t):
                        n = b * 8 + (16 * FFN_BASE[phase] + 4 * s + t)
                        u = Use(pool, phase, b)
                        u.read_out((4 + t, s))
                        xs = xres[:, bass.ds(b * (BT * D) + (4 * s + t) * D, D)]
                        nc.gpsimd.tensor_tensor(xs, xs, cols(yt, t % 2), ALU.add).then_inc(x_updated, 1)

                    for J in range(2 * JT):
                        s, j = J // JT, J % JT
                        n = b * 22 + (44 * FFN_BASE[phase] + J)
                        pool.wait_ge(hid_hi_ready, n + 1)
                        nc.gpsimd.tensor_tensor(cols(hid_lo, J % 2), cols(hid, J % 2),
                                                cols(hid_hi, J % 2).bitcast(F32),
                                                ALU.subtract).then_inc(hid_split, 1)
                        if j in (1, 3, 5, 7):
                            l = 4 * s + j // 2
                            rstd(ln_n(phase, b, l), l % 4)
                        if phase == "F1" and j in (8, 10):
                            i = 2 * s + (j - 8) // 2
                            m = b * 4 + i
                            piece = bass.ds(b * (KT * D) + i * D, D)
                            nc.gpsimd.tensor_copy(qk_hi[:, piece], qk_raw[:, piece]).then_inc(qk_split, 1)
                            pool.wait_ge(qk_split, m * 2 + 1)
                            alone(pool)
                            nc.gpsimd.tensor_tensor(qk_lo[:, piece], qk_raw[:, piece],
                                                    qk_hi[:, piece].bitcast(F32),
                                                    ALU.subtract).then_inc(qk_split, 1)
                        if J == JT:
                            for t in range(4):
                                add_y(0, t)
                    for t in range(4):
                        add_y(1, t)

            ffn("F1")
            with pool.Fori(0, BATCHES) as b:
                for l in range(8):
                    rstd(ln_n("B", b, l), l % 4)
            ffn("F2")

        @blk.scalar
        def _(act):
            def split_hi(phase, b, l):
                use = prep_use(phase, l)
                Use(act, phase, b).full(use)
                nc.scalar.activation(xt_tile(xt_hi, prep_col(phase, l)),
                                     bank(use[0]).rearrange("p (k n) -> p k n", k=KT),
                                     ACT.Copy).then_inc(xt_hi_done, 1)

            nc.scalar.preload_act_table_set("natural_log_exp_and_others")
            act.wait_ge(wab_in, 16)
            nc.scalar.activation(wab_hi[:, :], wab_raw[:, :], ACT.Copy).then_inc(wa_hi, 1)
            for l in range(4):
                split_hi("start", 0, l)
            act.wait_ge(wk_in, 16)
            nc.scalar.activation(wqk_hi[:, KT * D:], wqk_raw[:, KT * D:], ACT.Copy).then_inc(wa_hi, 1)
            act.wait_ge(wv_in, 16)
            nc.scalar.activation(wv_hi[:, :], wv_raw[:, :], ACT.Copy).then_inc(wa_hi, 1)
            act.wait_ge(wq_in, 16)
            nc.scalar.activation(wqk_hi[:, 0:KT * D], wqk_raw[:, 0:KT * D], ACT.Copy).then_inc(wa_hi, 1)
            act.wait_ge(rows_in, 6 * 16)

            with act.Fori(0, BATCHES) as b:
                u = Use(act, "A", b)

                def logits_row(s):
                    use = a_job(s, 0)
                    u.full(use)
                    nc.scalar.activation(ab_row[0:8, :], bank(use[0])[0:8, :], ACT.Copy).then_inc(drained[use[0]], 1)

                def norms(s, c):
                    u.read_out(k_job(s, c))
                    r = 4 * (c % 2)
                    for h in range(HEADS):
                        last = nc.scalar.activation(squares[:, :], kn[:, (c % 2) * D + h * P:(c % 2) * D + (h + 1) * P],
                                                    ACT.Square, accum_out=sumsq[:, r + h:r + h + 1])
                        last.then_inc(squares_done if h == HEADS - 1 else squares_step, 1)
                        if h < HEADS - 1:
                            act.wait_ge(squares_step, (b * 8 + (4 * s + c)) * 3 + (h + 1))

                def gate_exp(s):
                    act.wait_ge(gate_dve, b * 20 + (10 * s + 1))
                    nc.scalar.activation(g_e[:, :], g_zz[:, :], ACT.Exp, scale=-1.0).then_inc(gate_act, 1)

                def gate_logs(s):
                    act.wait_ge(gate_dve, b * 20 + (10 * s + 4))
                    nc.scalar.activation(g_la[:, :], g_a[:, :], ACT.Ln).then_inc(gate_act, 1)
                    nc.scalar.activation(g_lb[:, :], g_u[:, 16:32], ACT.Ln).then_inc(gate_act, 1)

                def q_out(s, h):
                    use = a_job(s, 3 + h)
                    u.full(use)
                    nc.scalar.activation(qT[:, h * GROUP:(h + 1) * GROUP], bank(use[0]), ACT.Identity,
                                         bias=bq_col[:, h:h + 1]).then_inc(drained[use[0]], 1)

                def gate_decays(s):
                    u.full((3, 6 * s + 1))
                    nc.scalar.activation(decays[:, 32 * s:32 * s + 32], bank(3)[:, 0:32], ACT.Exp).then_inc(gate_act, 1)
                    nc.scalar.activation(negcla[:, 16 * s:16 * s + 16], bank(3)[:, 0:16], ACT.Copy,
                                         scale=-1.0).then_inc(drained[3], 1)

                def kT_out(s, c):
                    use = (3, 6 * s + 2 + c)
                    u.full(use)
                    nc.scalar.activation(kT[:, :], bank(3), ACT.Copy).then_inc(drained[3], 1)

                def decay_out(s, c):
                    use = (4, 4 * s + c)
                    if c == 0:
                        u.read_out((3, 6 * s + 1))
                    u.full(use)
                    for h in range(HEADS):
                        i = 16 * s + 4 * c + h
                        last = nc.scalar.activation(decay[:, h * P:(h + 1) * P], bank(4)[:, h * P:(h + 1) * P],
                                                    ACT.Exp, bias=negcla[:, i:i + 1])
                    last.then_inc(drained[4], 1)

                def head(s):
                    q_out(s, 0)
                    gate_logs(s)
                    q_out(s, 1)
                    q_out(s, 2)
                    gate_decays(s)
                    q_out(s, 3)

                logits_row(0)
                norms(0, 0)
                gate_exp(0)
                head(0)
                for s in range(2):
                    for c in range(4):
                        kT_out(s, c)
                        if c < 3:
                            norms(s, c + 1)
                        elif s == 0:
                            logits_row(1)
                            norms(1, 0)
                            gate_exp(1)
                        if c < 2:
                            split_hi("A", b, 4 * s + 2 * c)
                        decay_out(s, c)
                        if c < 2:
                            split_hi("A", b, 4 * s + 2 * c + 1)
                        if c == 3 and s == 0:
                            head(1)

            def ffn(phase):
                nc.scalar.preload_act_table(ACT.Silu)
                with act.Fori(0, BATCHES) as b:
                    u = Use(act, phase, b)
                    for J in range(2 * JT):
                        s, j = J // JT, J % JT
                        u.full((0, J))
                        act.wait_ge(drained[1], u.value((1, J)) - 1)
                        nc.scalar.activation(cols(silu, J % 2), bank(0), ACT.Silu,
                                             scale=sg_col[:, j:j + 1]).then_inc(drained[0], 1)
                        u.read_out((1, J))
                        if J >= 2 and (J - 2) % JT < JT - 1:
                            act.wait_ge(down_done, b * 20 + (40 * FFN_BASE[phase] + (J - 2) // JT * 10
                                                             + (J - 2) % JT + 1))
                        elif J >= 2:
                            u.full((7, (J - 2) // JT))
                        nc.scalar.activation(cols(hid_hi, J % 2), cols(hid, J % 2),
                                             ACT.Copy).then_inc(hid_hi_ready, 1)
                        if j in (3, 5, 7, 9):
                            split_hi(phase, b, 4 * s + (j - 3) // 2)

            ffn("F1")

            nc.scalar.preload_act_table(ACT.Exp)
            act.wait_ge(vo_in, 32)
            for i in range(8):
                nc.scalar.activation(cols(vo_hi, i), cols(vo_raw, i), ACT.Copy).then_inc(vo_hi_done, 1)
            um = Use(act, "mid", 0)
            for i in range(8):
                um.full((i % 2, i // 2))
                nc.scalar.activation(cols(g_hi if i < 4 else wvo_hi, i % 4), bank(i % 2), ACT.Copy).then_inc(hi_done, 1)

            with act.Fori(0, BATCHES) as b:
                u = Use(act, "B", b)

                def high(dst, job):
                    u.full((job % 2, job // 2))
                    nc.scalar.activation(dst, bank(job % 2), ACT.Copy).then_inc(hi_done, 1)

                def softmax(i):
                    u.full((4, i))
                    act.wait_ge(nmax_done, b * 8 + (i + 1))
                    nc.scalar.activation(probs[:, :], bank(4, 2), ACT.Exp, scale=SCALE,
                                         bias=nmax[:, i % 2:i % 2 + 1],
                                         accum_out=rowsum[:, i % 2:i % 2 + 1]).then_inc(drained[4], 1)

                def pT_high(i):
                    u.full((2, i))
                    nc.scalar.activation(pT_hi[:, :], bank(2, 2), ACT.Copy).then_inc(pT_hi_done, 1)

                for l in range(4):
                    split_hi("B", b, l)
                for i in range(4):
                    high(cols(v_hi, i), 4 + i)
                for i in range(4):
                    high(cols(aT_hi, i), 8 + i)
                softmax(0)
                for i in range(4):
                    high(cols(v_hi, 4 + i), 12 + i)
                pT_high(0)
                for i in range(1, 8):
                    if i == 4:
                        for m in range(4):
                            high(cols(aT_hi, m), 16 + m)
                    softmax(i)
                    if i == 7:
                        for l in range(4, 8):
                            split_hi("B", b, l)
                    pT_high(i)

            ffn("F2")

        @blk.vector
        def _(dve):
            def stats(phase, b, l):
                n, r = ln_n(phase, b, l), l % 4
                nc.vector.bn_stats(ln_bn[:, 6 * r:6 * r + 6], prep_x(phase, b, l)).then_inc(ln_bn_done, 1)
                dve.wait_ge(ln_bn_done, n + 1)
                alone(dve)
                nc.vector.bn_aggr(ln_mv[:, 2 * r:2 * r + 2], ln_bn[:, 6 * r:6 * r + 6]).then_inc(ln_mv_done, 1)
                dve.wait_ge(ln_mv_done, n + 1)
                nc.vector.tensor_scalar(ln_var[:, r:r + 1], ln_mv[:, 2 * r + 1:2 * r + 2], LN_EPS, None,
                                        ALU.add).then_inc(ln_var_done, 1)

            def normalise(phase, b, l):
                n, r = ln_n(phase, b, l), l % 4
                dve.wait_ge(ln_rstd_done, n + 1)
                nc.vector.tensor_scalar(cols(xn, l % 2), prep_x(phase, b, l), ln_mv[:, 2 * r:2 * r + 1],
                                        ln_rstd[:, r:r + 1], ALU.subtract, ALU.mult).then_inc(ln_xn_done, 1)

            def split_lo(phase, b, l):
                use = prep_use(phase, l)
                dve.wait_ge(xt_hi_done, ln_n(phase, b, l) + 1)
                nc.vector.tensor_tensor(xt_tile(xt_lo, prep_col(phase, l)),
                                        bank(use[0]).rearrange("p (k n) -> p k n", k=KT),
                                        xt_tile(xt_hi, prep_col(phase, l)).bitcast(F32),
                                        ALU.subtract).then_inc(drained[use[0]], 1)

            def prep_four(phase, b, l0):
                for l in range(l0, l0 + 4):
                    stats(phase, b, l)
                normalise(phase, b, l0)
                normalise(phase, b, l0 + 1)
                split_lo(phase, b, l0)
                normalise(phase, b, l0 + 2)
                split_lo(phase, b, l0 + 1)
                normalise(phase, b, l0 + 3)
                split_lo(phase, b, l0 + 2)
                split_lo(phase, b, l0 + 3)

            dve.wait_ge(x_in, 16)
            prep_four("start", 0, 0)
            for i, (lo, raw, hi) in enumerate(((wab_lo[:, :], wab_raw[:, :], wab_hi[:, :]),
                                               (wqk_lo[:, KT * D:], wqk_raw[:, KT * D:], wqk_hi[:, KT * D:]),
                                               (wv_lo[:, :], wv_raw[:, :], wv_hi[:, :]),
                                               (wqk_lo[:, 0:KT * D], wqk_raw[:, 0:KT * D], wqk_hi[:, 0:KT * D]))):
                dve.wait_ge(wa_hi, i + 1)
                nc.vector.tensor_tensor(lo, raw, hi.bitcast(F32), ALU.subtract).then_inc(wa_lo, 1)
            dve.wait_ge(rows_in, 6 * 16)
            dve.wait_ge(x_rest_in, 48)
            dve.wait_ge(gu_in, 32)

            with dve.Fori(0, BATCHES) as b:
                row0 = dve.snap(b * (BT * D))
                other_batch[0] = dve.snap(BT * D - row0)
                u = Use(dve, "A", b)
                z3 = g_z[:, :].rearrange("p (c k) -> p c k", c=4)

                def four(ap):
                    return ap.rearrange("p (c h) -> p c h", c=4)

                def k_out(s, c):
                    use = k_job(s, c)
                    u.full(use)
                    nc.vector.tensor_tensor(cols(kn, c % 2), bank(use[0]), bk_rows[:, :],
                                            ALU.add).then_inc(drained[use[0]], 1)

                def v_out(s, c):
                    use = v_job(s, c)
                    u.full(use)
                    nc.vector.tensor_tensor(cols(vn, c % 2), bank(use[0]), bv_rows[:, :],
                                            ALU.add).then_inc(drained[use[0]], 1)

                def gate_a(s):
                    use = (3, 6 * s)
                    u.full(use)
                    nc.vector.tensor_tensor(z3, bank(3)[:, 0:32].rearrange("p (c k) -> p c k", c=4),
                                            ab_bias[:, :].unsqueeze(1).broadcast_to([P, 4, 8]),
                                            ALU.add).then_inc(drained[3], 1)
                    u.read_out(use)
                    nc.vector.tensor_scalar(four(g_zz[:, 0:16]), z3[:, :, 0:4], -80.0, None,
                                            ALU.max)
                    nc.vector.scalar_tensor_tensor(out=four(g_zz[:, 16:32]), in0=z3[:, :, 4:8], scalar=-1.0,
                                                   in1=z3[:, :, 4:8], op0=ALU.mult,
                                                   op1=ALU.max).then_inc(gate_dve, 1)

                def gate_b(s):
                    g = b * 20 + 10 * s
                    dve.wait_ge(gate_act, b * 8 + (4 * s + 1))
                    nc.vector.tensor_scalar(g_u[:, :], g_e[:, :], 1.0, None, ALU.add).then_inc(gate_dve, 1)
                    dve.wait_ge(gate_dve, g + 2)
                    nc.vector.reciprocal(g_r[:, :], g_u[:, :]).then_inc(gate_dve, 1)
                    dve.wait_ge(gate_dve, g + 3)
                    nc.vector.tensor_scalar(g_a[:, :], g_r[:, 0:16], 1e-6, None, ALU.add).then_inc(gate_dve, 1)
                    nc.vector.scalar_tensor_tensor(out=g_c[:, :], in0=g_u[:, 16:32], scalar=1.0, in1=g_e[:, 16:32],
                                                   op0=ALU.subtract, op1=ALU.subtract).then_inc(gate_dve, 1)
                    dve.wait_ge(gate_dve, g + 5)
                    nc.vector.tensor_tensor(g_c2[:, :], g_c[:, :], g_r[:, 16:32], ALU.mult).then_inc(gate_dve, 1)
                    dve.wait_ge(gate_dve, g + 6)
                    nc.vector.scalar_tensor_tensor(out=four(g_zm[:, :]), in0=z3[:, :, 4:8], scalar=0.0,
                                                   in1=four(g_c2[:, :]), op0=ALU.max,
                                                   op1=ALU.subtract).then_inc(gate_dve, 1)

                def gate_c(s):
                    g = b * 20 + 10 * s
                    o = slice(16 * s, 16 * s + 16)
                    dve.wait_ge(gate_act, b * 8 + (4 * s + 3))
                    dve.wait_ge(gate_dve, g + 7)
                    nc.vector.tensor_tensor(beta[:, o], g_zm[:, :], g_lb[:, :], ALU.add).then_inc(gate_dve, 1)
                    nc.vector.tensor_copy(la_hi[:, o], g_la[:, :]).then_inc(gate_dve, 1)
                    dve.wait_ge(gate_dve, g + 9)
                    nc.vector.tensor_tensor(la_lo[:, o], g_la[:, :], la_hi[:, o].bitcast(F32),
                                            ALU.subtract).then_inc(gate_dve, 1)

                def attn_out(s, c):
                    n = 4 * s + c
                    u.full((5, 2 * n))
                    u.read_out((4, n))
                    nc.vector.tensor_tensor(attnT[:, :], bank(5), decay[:, :], ALU.mult).then_inc(drained[5], 1)

                def state_out(s, c):
                    n = 4 * s + c
                    if n == 0:
                        dve.wait_ge(state_zero, b + 1)
                    u.free((5, 2 * n + 1))
                    u.full((5, 2 * n + 1))
                    for h in range(HEADS):
                        i = 32 * s + 16 + 4 * c + h
                        hs = slice(h * P, (h + 1) * P)
                        last = nc.vector.scalar_tensor_tensor(out=state[:, hs], in0=state[:, hs],
                                                              scalar=decays[:, i:i + 1], in1=bank(5)[:, hs],
                                                              op0=ALU.mult, op1=ALU.add)
                    last.then_inc(drained[5], 1)

                def y_out(s, c):
                    n = 4 * s + c
                    u.full((6, n))
                    for h in range(HEADS):
                        i = 32 * s + 4 * c + h
                        xs = xres[:, bass.ds(row0 + (n * D + h * P), P)]
                        last = nc.vector.scalar_tensor_tensor(out=xs, in0=bank(6)[:, h * P:(h + 1) * P],
                                                              scalar=decays[:, i:i + 1], in1=xs,
                                                              op0=ALU.mult, op1=ALU.add)
                    last.then_inc(drained[6], 1)
                    u.read_out((6, n))
                    u.full((7, n))
                    xs = xres[:, bass.ds(row0 + n * D, D)]
                    nc.vector.tensor_tensor(xs, xs, bank(7), ALU.add).then_inc(drained[7], 1)

                nc.vector.memset(state[:, :], 0.0).then_inc(state_zero, 1)
                k_out(0, 0)
                gate_a(0)
                v_out(0, 0)
                gate_b(0)
                stats("A", b, 0)
                stats("A", b, 1)
                gate_c(0)
                for s in range(2):
                    for c in range(4):
                        l = 4 * s + 2 * c
                        if c < 2:
                            normalise("A", b, l)
                            normalise("A", b, l + 1)
                        if c < 3:
                            k_out(s, c + 1)
                        elif s == 0:
                            k_out(1, 0)
                            gate_a(1)
                        if c < 2:
                            split_lo("A", b, l)
                        attn_out(s, c)
                        if c < 3:
                            v_out(s, c + 1)
                        elif s == 0:
                            v_out(1, 0)
                            gate_b(1)
                        if c < 2:
                            split_lo("A", b, l + 1)
                        if c == 0:
                            if s == 1:
                                u.read_out((7, 3))
                                alone(dve)
                            stats("A", b, l + 2)
                            stats("A", b, l + 3)
                        state_out(s, c)
                        y_out(s, c)
                        piece = bass.ds(b * (4 * HID) + (4 * s + c) * (HID // 2), HID // 2)
                        nc.vector.tensor_scalar(w_gu[:, piece], codes_gu[:, piece], -ZERO_POINT, None,
                                                ALU.add).then_inc(gu_ready, 1)
                        if c == 3 and s == 0:
                            gate_c(1)
                            u.read_out((7, 3))
                            alone(dve)
                            stats("A", b, 4)
                            stats("A", b, 5)

            def ffn(phase):
                nd = 6
                dve.wait_ge(d_in[phase], 16)
                nc.vector.tensor_scalar(w_d[phase][:, 0:nd * D], codes_d[phase][:, 0:nd * D], -ZERO_POINT, None,
                                        ALU.add).then_inc(wd_ready[phase], 1)
                dve.wait_ge(sd_in, 16)
                if phase == "F1":
                    Use(dve, "A", 1).read_out((7, 7))
                else:
                    Use(dve, "B", 1).read_out((7, 3))
                with dve.Fori(0, BATCHES) as b:
                    row0 = dve.snap(b * (BT * D))
                    other_batch[0] = dve.snap(BT * D - row0)
                    u = Use(dve, phase, b)

                    def residual(s):
                        for t in range(4):
                            n = b * 8 + (16 * FFN_BASE[phase] + 4 * s + t)
                            u.full((4 + t, s))
                            dve.wait_ge(x_updated, n + 1)
                            nc.vector.tensor_tensor(cols(yt, t % 2), bank(4 + t), sd_rows[:, :],
                                                    ALU.mult).then_inc(drained[4 + t], 1)

                    for J in range(2 * JT):
                        s, j = J // JT, J % JT
                        n = b * 22 + (44 * FFN_BASE[phase] + J)
                        u.full((1, J))
                        u.read_out((0, J))
                        dve.wait_ge(hid_split, n + 1)
                        nc.vector.scalar_tensor_tensor(out=cols(hid, J % 2), in0=bank(1), scalar=su_col[:, j:j + 1],
                                                       in1=cols(silu, J % 2), op0=ALU.mult,
                                                       op1=ALU.mult).then_inc(drained[1], 1)
                        if J == JT:
                            residual(0)
                        if j in (3, 5, 7, 9):
                            split_lo(phase, b, 4 * s + (j - 3) // 2)
                        if j in (1, 3, 5, 7):
                            if j == 1 and s == 1:
                                dve.wait_ge(x_updated, b * 8 + (16 * FFN_BASE[phase] + 4 + RING))
                                alone(dve)
                            stats(phase, b, 4 * s + j // 2)
                        if j in (2, 4, 6, 8):
                            normalise(phase, b, 4 * s + j // 2 - 1)
                    residual(1)

            ffn("F1")

            for i in range(8):
                dve.wait_ge(vo_hi_done, i + 1)
                nc.vector.tensor_tensor(cols(vo_lo, i), cols(vo_raw, i), cols(vo_hi, i).bitcast(F32),
                                        ALU.subtract).then_inc(vo_split, 1)
            for i in range(8):
                dve.wait_ge(hi_done, i + 1)
                nc.vector.tensor_tensor(cols(g_lo if i < 4 else wvo_lo, i % 4), bank(i % 2),
                                        cols(g_hi if i < 4 else wvo_hi, i % 4).bitcast(F32),
                                        ALU.subtract).then_inc(drained[i % 2], 1)
            dve.wait_ge(x_updated, 16 + RING)

            with dve.Fori(0, BATCHES) as b:
                row0 = dve.snap(b * (BT * D))
                other_batch[0] = dve.snap(BT * D - row0)
                u = Use(dve, "B", b)

                def low(dst, hi, job, k):
                    dve.wait_ge(hi_done, b * 16 + (8 + k + 1))
                    nc.vector.tensor_tensor(dst, bank(job % 2), hi.bitcast(F32),
                                            ALU.subtract).then_inc(drained[job % 2], 1)

                def row_max(i):
                    r = slice(i % 2, i % 2 + 1)
                    u.full((4, i))
                    nc.vector.reduce_max(smax[:, r], bank(4, 2), AX.X).then_inc(smax_done, 1)
                    dve.wait_ge(smax_done, b * 8 + (i + 1))
                    nc.vector.tensor_scalar(nmax[:, r], smax[:, r], -SCALE, None, ALU.mult).then_inc(nmax_done, 1)

                def pT_low(i):
                    dve.wait_ge(pT_hi_done, b * 8 + (i + 1))
                    nc.vector.tensor_tensor(pT_lo[:, :], bank(2, 2), pT_hi[:, :].bitcast(F32),
                                            ALU.subtract).then_inc(drained[2], 1)

                def out_add(i):
                    r = slice(i % 2, i % 2 + 1)
                    u.read_out((4, i))
                    nc.vector.reciprocal(rden[:, r], rowsum[:, r]).then_inc(rden_done, 1)
                    dve.wait_ge(rden_done, b * 8 + (i + 1))
                    u.full((6 + i % 2, i // 2))
                    xs = xres[:, bass.ds(row0 + i * D, D)]
                    nc.vector.scalar_tensor_tensor(out=xs, in0=bank(6 + i % 2), scalar=rden[:, r], in1=xs,
                                                   op0=ALU.mult, op1=ALU.add).then_inc(drained[6 + i % 2], 1)

                prep_four("B", b, 0)
                for i in range(4):
                    low(cols(v_lo, i), cols(v_hi, i), 4 + i, i)
                for i in range(4):
                    low(cols(aT_lo, i), cols(aT_hi, i), 8 + i, 4 + i)
                row_max(0)
                for i in range(4):
                    low(cols(v_lo, 4 + i), cols(v_hi, 4 + i), 12 + i, 8 + i)
                pT_low(0)
                for i in range(1, 8):
                    if i == 4:
                        for m in range(4):
                            low(cols(aT_lo, m), cols(aT_hi, m), 16 + m, 12 + m)
                    row_max(i)
                    out_add(i - 1)
                    if i == 7:
                        u.read_out((7, 2))
                        u.read_out((6, 3))
                        alone(dve)
                        prep_four("B", b, 4)
                    pT_low(i)
                out_add(7)

            ffn("F2")

        @blk.tensor
        def _(pe):
            def mm(out, lhsT, rhs, start, stop):
                return nc.tensor.matmul(out, lhsT, rhs, start=start, stop=stop)

            def product(out, left, right, ks=KT):
                for k in range(ks):
                    (lh, ll), (rh, rl) = left(k), right(k)
                    mm(out, lh, rh, k == 0, False)
                    mm(out, lh, rl, False, False)
                    last = mm(out, ll, rh, False, k == ks - 1)
                return last

            def pair(hi, lo, a, n):
                return hi[:, a:a + n], lo[:, a:a + n]

            def turn_tile(phase, b, l):
                use = prep_use(phase, l)
                pe.wait_ge(ln_xn_done, ln_n(phase, b, l) + 1)
                Use(pe, phase, b).free(use)
                for k in range(KT):
                    last = nc.tensor.transpose(bank(use[0])[:, k * P:(k + 1) * P],
                                               xn[:, (l % 2) * D + k * P:(l % 2) * D + (k + 1) * P], ident[:, :])
                last.then_inc(filled[use[0]], 1)

            def xt(k, col, n):
                return pair(xt_hi, xt_lo, k * BTOK + col, n)

            pe.wait_ge(consts_done, 5)
            for l in range(4):
                turn_tile("start", 0, l)
            pe.wait_ge(drained[2], turn("start", 2, 0, 3) + 1)

            with pe.Fori(0, BATCHES) as b:
                u = Use(pe, "A", b)
                u.free((2, 0))

                def logits(s):
                    use = a_job(s, 0)
                    pe.wait_ge(wa_lo, 1)
                    u.free(use)
                    product(bank(use[0]), lambda k: pair(wab_hi, wab_lo, k * P, P),
                            lambda k: xt(k, s * GROUP, GROUP)).then_inc(filled[use[0]], 1)

                def logits_turned(s):
                    u.read_out(a_job(s, 0))
                    u.free((3, 6 * s))
                    alone(pe)
                    for c in range(4):
                        last = nc.tensor.transpose(bank(3)[:, 8 * c:8 * c + 8], ab_row[0:8, c * P:(c + 1) * P],
                                                   ident[0:8, 0:8])
                    last.then_inc(filled[3], 1)

                def k_rows(s, c):
                    use = k_job(s, c)
                    pe.wait_ge(wa_lo, 2)
                    u.free(use)
                    product(bank(use[0]), lambda k: xt(k, s * GROUP + c * P, P),
                            lambda k: pair(wqk_hi, wqk_lo, (KT + k) * D, D)).then_inc(filled[use[0]], 1)

                def v_rows(s, c):
                    use = v_job(s, c)
                    pe.wait_ge(wa_lo, 3)
                    u.free(use)
                    product(bank(use[0]), lambda k: xt(k, s * GROUP + c * P, P),
                            lambda k: pair(wv_hi, wv_lo, k * D, D)).then_inc(filled[use[0]], 1)

                def q_cols(s, h):
                    use = a_job(s, 3 + h)
                    pe.wait_ge(wa_lo, 4)
                    u.free(use)
                    product(bank(use[0]), lambda k: pair(wqk_hi, wqk_lo, k * D + h * P, P),
                            lambda k: xt(k, s * GROUP, GROUP)).then_inc(filled[use[0]], 1)

                def log_sums(s):
                    pe.wait_ge(gate_act, b * 8 + (4 * s + 2))
                    u.free((3, 6 * s + 1))
                    mm(bank(3)[:, 0:16], tri[:, :], g_la[:, :], True, True)
                    mm(bank(3)[:, 16:32], ones[:, :], g_la[:, :], True, True).then_inc(filled[3], 1)

                def k_turned(s, c):
                    pe.wait_ge(k_scaled, b * 8 + (4 * s + c + 1))
                    u.free((3, 6 * s + 2 + c))
                    for h in range(HEADS):
                        last = nc.tensor.transpose(bank(3)[:, h * P:(h + 1) * P],
                                                   kn[:, (c % 2) * D + h * P:(c % 2) * D + (h + 1) * P], ident[:, :])
                    last.then_inc(filled[3], 1)

                def scores(s, c):
                    n = 4 * s + c
                    if c == 0:
                        u.read_out(a_job(s, 5))
                        u.read_out(a_job(s, 6))
                    u.read_out((3, 6 * s + 2 + c))
                    u.free((5, 2 * n))
                    for h in range(HEADS):
                        last = mm(bank(5)[:, h * P:(h + 1) * P], kT[:, h * P:(h + 1) * P],
                                  qT[:, h * GROUP + c * P:h * GROUP + (c + 1) * P], True, True)
                    last.then_inc(filled[5], 1)

                def log_decay(s, c):
                    n = 4 * s + c
                    pe.wait_ge(steps_ready, b * 16 + (2 * n + 2))
                    u.free((4, n))
                    mm(bank(4), ones_r[:, :], steps_hi[:, :], True, False)
                    mm(bank(4), ones_r[:, :], steps_lo[:, :], False, False)
                    mm(bank(4), ident_b[:, :], mask_b[:, :], False, True).then_inc(filled[4], 1)

                def core(s, c):
                    n = 4 * s + c
                    if n == 0:
                        pe.wait_ge(state_zero, b + 1)
                    u.free((6, n))
                    for h in range(HEADS):
                        last = mm(bank(6)[:, h * P:(h + 1) * P], qT[:, h * GROUP + c * P:h * GROUP + (c + 1) * P],
                                  state[:, h * P:(h + 1) * P], True, True)
                    last.then_inc(filled[6], 1)
                    u.read_out((5, 2 * n))
                    u.read_out(v_job(s, c))
                    u.free((7, n))
                    for h in range(HEADS):
                        last = mm(bank(7)[:, h * P:(h + 1) * P], attnT[:, h * P:(h + 1) * P],
                                  vn[:, (c % 2) * D + h * P:(c % 2) * D + (h + 1) * P], True, True)
                    last.then_inc(filled[7], 1)
                    pe.wait_ge(kw_ready, b * 8 + (n + 1))
                    for h in range(HEADS):
                        last = mm(bank(5)[:, h * P:(h + 1) * P], kw[:, h * P:(h + 1) * P],
                                  vn[:, (c % 2) * D + h * P:(c % 2) * D + (h + 1) * P], True, True)
                    last.then_inc(filled[5], 1)

                def head(s):
                    q_cols(s, 0)
                    q_cols(s, 1)
                    q_cols(s, 2)
                    log_sums(s)
                    q_cols(s, 3)

                logits(0)
                k_rows(0, 0)
                logits_turned(0)
                v_rows(0, 0)
                head(0)
                for s in range(2):
                    for c in range(4):
                        k_turned(s, c)
                        if c < 3:
                            k_rows(s, c + 1)
                        elif s == 0:
                            u.free((2, 4))
                            logits(1)
                            k_rows(1, 0)
                            logits_turned(1)
                        if c < 2:
                            turn_tile("A", b, 4 * s + 2 * c)
                        scores(s, c)
                        log_decay(s, c)
                        if c < 3:
                            v_rows(s, c + 1)
                        elif s == 0:
                            v_rows(1, 0)
                        if c < 2:
                            turn_tile("A", b, 4 * s + 2 * c + 1)
                        core(s, c)
                        if c == 3 and s == 0:
                            head(1)

            def ffn(phase):
                pe.wait_ge(gu_ready, 16)
                pe.wait_ge(wd_ready[phase], 2)
                with pe.Fori(0, BATCHES) as b:
                    u = Use(pe, phase, b)
                    u.free((2, 0))
                    u.free((3, 0))

                    def up(J, out, w0):
                        s, j = J // JT, J % JT
                        u.free((out, J))
                        for k in range(KT):
                            w = w_gu[:, (w0 + k) * HID + j * P:(w0 + k) * HID + (j + 1) * P]
                            xh, xl = xt(k, s * GROUP, GROUP)
                            mm(bank(out), w, xh, k == 0, False)
                            last = mm(bank(out), w, xl, False, k == KT - 1)
                        last.then_inc(filled[out], 1)

                    def down(J):
                        s, j = J // JT, J % JT
                        n = b * 22 + (44 * FFN_BASE[phase] + J)
                        pe.wait_ge(hid_split, n + (RING + 1))
                        for t in range(4):
                            if j == 0:
                                u.free((4 + t, s))
                            o = (J % 2) * GROUP + t * P
                            mm(bank(4 + t), hid_hi[:, o:o + P], cols(w_d[phase], j), j == 0, False)
                            last = mm(bank(4 + t), hid_lo[:, o:o + P], cols(w_d[phase], j), False, j == JT - 1)
                            if j == JT - 1:
                                last.then_inc(filled[4 + t], 1)
                        if j < JT - 1:
                            last.then_inc(down_done, 1)

                    for J in range(2 * JT):
                        s, j = J // JT, J % JT
                        if J == JT:
                            u.free((2, 2))
                            u.free((3, 2))
                        up(J, 0, 0)
                        up(J, 1, KT)
                        if J > 0:
                            down(J - 1)
                        if j in (3, 5, 7, 9):
                            turn_tile(phase, b, 4 * s + (j - 3) // 2)
                    down(2 * JT - 1)

            Use(pe, "A", 1).read_out((2, 7))
            ffn("F1")
            for bnk in (2, 3):
                Use(pe, "F1", 1).read_out((bnk, 3))

            um = Use(pe, "mid", 0)
            pe.wait_ge(qk_split, 16)
            for i in range(4):
                um.free((i % 2, i // 2))
                product(bank(i % 2), lambda k: pair(qk_hi, qk_lo, k * D + i * P, P),
                        lambda k: pair(qk_hi, qk_lo, (KT + k) * D, D)).then_inc(filled[i % 2], 1)
            pe.wait_ge(vo_split, 8)
            for i in range(4, 8):
                um.free((i % 2, i // 2))
                product(bank(i % 2), lambda k: pair(vo_hi, vo_lo, k * D + (i - 4) * P, P),
                        lambda k: pair(vo_hi, vo_lo, (KT + k) * D, D)).then_inc(filled[i % 2], 1)
            um.read_out((0, 3))
            um.read_out((1, 3))

            with pe.Fori(0, BATCHES) as b:
                u = Use(pe, "B", b)

                def values(i):
                    job = (4 + i) if i < 4 else (8 + i)
                    u.free((job % 2, job // 2))
                    product(bank(job % 2), lambda k: xt(k, i * P, P),
                            lambda k: pair(wvo_hi, wvo_lo, k * D, D)).then_inc(filled[job % 2], 1)

                def queries(s):
                    for m in range(4):
                        job = (8 if s == 0 else 16) + m
                        u.free((job % 2, job // 2))
                        product(bank(job % 2), lambda k: pair(g_hi, g_lo, k * D + m * P, P),
                                lambda k: xt(k, s * GROUP, GROUP)).then_inc(filled[job % 2], 1)

                def scores(i):
                    if i % 4 == 0:
                        for job in ((10, 11) if i == 0 else (18, 19)):
                            u.read_out((job % 2, job // 2))
                    u.free((4, i))
                    for half in range(2):
                        last = product(bank(4 + half), lambda k: pair(aT_hi, aT_lo, k * GROUP + (i % 4) * P, P),
                                       lambda k: xt(k, half * GROUP, GROUP))
                    last.then_inc(filled[4], 1)

                def turn_probs(i):
                    u.read_out((4, i))
                    u.free((2, i))
                    for t in range(BT):
                        last = nc.tensor.transpose(bank(2, 2)[:, t * P:(t + 1) * P], probs[:, t * P:(t + 1) * P],
                                                   ident[:, :])
                    last.then_inc(filled[2], 1)

                def attend(i):
                    if i == 0:
                        for job in (14, 15):
                            u.read_out((job % 2, job // 2))
                    u.read_out((2, i))
                    u.free((6 + i % 2, i // 2))
                    product(bank(6 + i % 2), lambda t: pair(pT_hi, pT_lo, t * P, P),
                            lambda t: pair(v_hi, v_lo, t * D, D), BT).then_inc(filled[6 + i % 2], 1)

                u.free((0, 0))
                u.free((1, 0))
                for l in range(4):
                    turn_tile("B", b, l)
                for i in range(4):
                    values(i)
                u.read_out((0, 1))
                u.read_out((1, 1))
                queries(0)
                scores(0)
                for i in range(4, 8):
                    values(i)
                turn_probs(0)
                for i in range(1, 8):
                    if i == 4:
                        queries(1)
                    scores(i)
                    attend(i - 1)
                    if i == 7:
                        for l in range(4, 8):
                            turn_tile("B", b, l)
                    turn_probs(i)
                attend(7)

            for bnk in (0, 1):
                Use(pe, "B", 1).read_out((bnk, 11))
            ffn("F2")


def kernel(**inputs):
    import numpy as np
    import concourse.bacc as bacc
    from concourse.bass_utils import run_bass_kernel_spmd

    def a(name):
        return np.asarray(inputs["L0_" + name])

    def t(m):
        return np.ascontiguousarray(m.T)

    def col(v):
        return t(v.reshape(-1, P))

    x = a("attn_a_x")
    arrays = {
        "x": np.ascontiguousarray(x.reshape(-1, x.shape[-1])),
        "wq": a("attn_a_Wq"), "wk": a("attn_a_Wk"), "wv": a("attn_a_Wv"),
        "w_ab": np.concatenate([a("attn_a_Walpha"), a("attn_a_Wbeta")], axis=1),
        "b_ab": np.concatenate([a("attn_a_balpha"), a("attn_a_bbeta")]),
        "bq": col(a("attn_a_bq")), "bk": a("attn_a_bk"), "bv": a("attn_a_bv"),
        "wqT": t(a("attn_b_W_q")), "wkT": t(a("attn_b_W_k")), "wvT": t(a("attn_b_W_v")), "wo": a("attn_b_W_o"),
        "gateT": t(a("ffn_wq_gate")), "s_gate": col(a("ffn_s_gate")),
        "upT": t(a("ffn_wq_up")), "s_up": col(a("ffn_s_up")),
        "downT": t(a("ffn_wq_down")), "s_down": a("ffn_s_down"),
    }
    nc = bacc.Bacc("TRN2", target_bir_lowering=False, num_devices=1)
    args = {n: nc.dram_tensor(n, v.shape, mybir.dt.from_np(v.dtype), kind="ExternalInput").ap()
            for n, v in arrays.items()}
    args["out"] = nc.dram_tensor("out", arrays["x"].shape, F32, kind="ExternalOutput").ap()
    hybrid_layer_kernel(nc, **args)
    got = run_bass_kernel_spmd(nc, [arrays], core_ids=[0])
    return np.asarray(got.results[0]["out"]).reshape(x.shape)
```

```python
from contextlib import ExitStack

import concourse.bass as bass
from concourse import mybir

F32 = mybir.dt.float32
F32R = mybir.dt.float32r
BF16 = mybir.dt.bfloat16
I32 = mybir.dt.int32
ALU = mybir.AluOpType
ACT = mybir.ActivationFunctionType
AX = mybir.AxisListType

P = 128
BATCHES = 2
TOKENS = 2048
D = 512
KT = D // P
HEADS = D // P
HID = 1408
JT = HID // P
GT = 4
GROUP = GT * P
BT = 2 * GT
BTOK = BT * P
ZERO_POINT = 128.0
LN_EPS = 1e-5
NORM_FLOOR = 1e-12
SCALE = float(D) ** -0.5
MASKED = -30000.0
RING = 2

BODIES = [("start", 1, {2: 4}),
          ("A", 2, {0: 13, 1: 13, 2: 8, 3: 12, 4: 8, 5: 16, 6: 8, 7: 8}),
          ("F1", 2, {0: 22, 1: 22, 2: 4, 3: 4, 4: 2, 5: 2, 6: 2, 7: 2}),
          ("mid", 1, {0: 4, 1: 4}),
          ("B", 2, {0: 10, 1: 10, 2: 8, 4: 8, 6: 6, 7: 6}),
          ("F2", 2, {0: 22, 1: 22, 2: 4, 3: 4, 4: 2, 5: 2, 6: 2, 7: 2})]
LN_BASE = {"start": 0, "A": 4, "F1": 20, "B": 36, "F2": 52}
FFN_BASE = {"F1": 0, "F2": 1}


def fills_before(phase, bank):
    total = 0
    for name, times, uses in BODIES:
        if name == phase:
            return total
        total += times * uses.get(bank, 0)
    raise ValueError(phase)


def turn(phase, bank, b, i):
    per = {name: uses for name, _, uses in BODIES}[phase][bank]
    return b * per + (fills_before(phase, bank) + i + 1)


def hybrid_layer_kernel(nc, x, wq, wk, wv, w_ab, bq, bk, bv, b_ab,
                        wqT, wkT, wvT, wo, gateT, s_gate, upT, s_up, downT, s_down, out):
    base = (nc.sbuf_base + 63) // 64 * 64

    def at(name, offset, cols, dtype=F32):
        return nc.alloc_sbuf_tensor_at(name, [P, cols], dtype, offset=base + offset)

    xres = at("xres", 0, 16 * D)
    codes_gu = at("codes_gu", 32768, 8 * HID, I32)
    w_gu = at("w_gu", 32768, 8 * HID, F32R)
    xt_hi = at("xt_hi", 77824, KT * BTOK, F32R)
    xt_lo = at("xt_lo", 94208, KT * BTOK, F32R)
    R1, W2, CONST = 110592, 143360, 204800
    ident = at("ident", CONST, P)
    sd_rows = at("sd_rows", CONST + 512, D)
    ab_row = at("ab_row", CONST + 512, GROUP)
    xn = at("xn", CONST + 2560, 2 * D)
    sg_col = at("sg_col", CONST + 6656, JT)
    su_col = at("su_col", CONST + 6720, JT)
    ln_bn = at("ln_bn", CONST + 6784, 4 * 6)
    ln_mv = at("ln_mv", CONST + 6912, 4 * 2)
    ln_var = at("ln_var", CONST + 6944, 4)
    ln_rstd = at("ln_rstd", CONST + 6976, 4)
    minus_half = at("minus_half", CONST + 7008, 4)
    smax = at("smax", CONST + 7040, 2)
    nmax = at("nmax", CONST + 7072, 2)
    rowsum = at("rowsum", CONST + 7104, 2)
    rden = at("rden", CONST + 7136, 2)

    wqk_hi = at("wqk_hi", R1, 2 * KT * D, F32R)
    wqk_raw = at("wqk_raw", R1 + 16384, 2 * KT * D)
    wqk_lo = at("wqk_lo", R1 + 16384, 2 * KT * D, F32R)
    wv_hi = at("wv_hi", W2, KT * D, F32R)
    wv_raw = at("wv_raw", W2 + 8192, KT * D)
    wv_lo = at("wv_lo", W2 + 8192, KT * D, F32R)
    bk_rows = at("bk_rows", W2 + 16384, D)
    bv_rows = at("bv_rows", W2 + 18432, D)
    qT = at("qT", W2 + 20480, HEADS * GROUP)
    kn = at("kn", W2 + 28672, 2 * D)
    kT = at("kT", W2 + 32768, D)
    vn = at("vn", W2 + 34816, 2 * D)
    decay = at("decay", W2 + 38912, D)
    attnT = at("attnT", W2 + 40960, D)
    kw = at("kw", W2 + 43008, D)
    steps_hi = at("steps_hi", W2 + 45056, D, F32R)
    steps_lo = at("steps_lo", W2 + 47104, D, F32R)
    state = at("state", W2 + 49152, D)
    g_z = at("g_z", W2 + 51200, 32)
    g_zz = at("g_zz", W2 + 51328, 32)
    g_e = at("g_e", W2 + 51456, 32)
    g_u = at("g_u", W2 + 51584, 32)
    g_r = at("g_r", W2 + 51712, 32)
    g_a = at("g_a", W2 + 51840, 16)
    g_la = at("g_la", W2 + 51904, 16)
    g_lb = at("g_lb", W2 + 51968, 16)
    g_c = at("g_c", W2 + 52032, 16)
    g_c2 = at("g_c2", W2 + 52096, 16)
    g_zm = at("g_zm", W2 + 52160, 16)
    beta = at("beta", W2 + 52224, 32)
    la_hi = at("la_hi", W2 + 52352, 32, F32R)
    la_lo = at("la_lo", W2 + 52480, 32, F32R)
    negcla = at("negcla", W2 + 52608, 32)
    decays = at("decays", W2 + 52736, 64)
    sumsq = at("sumsq", W2 + 52992, 8)
    kscale = at("kscale", W2 + 53024, 8)
    ab_bias = at("ab_bias", W2 + 53056, 8)
    bq_col = at("bq_col", W2 + 53088, 4)
    squares = at("squares", W2 + 53248, P)
    tri = at("tri", W2 + 53760, P)
    tri_r = at("tri_r", W2 + 54272, P, F32R)
    ones = at("ones", W2 + 54784, P)
    ones_r = at("ones_r", W2 + 55296, P, F32R)
    ident_b = at("ident_b", W2 + 55808, P, BF16)
    mask_b = at("mask_b", W2 + 56064, D, BF16)
    wab_hi = at("wab_hi", W2 + 57088, KT * P, F32R)
    wab_raw = at("wab_raw", W2 + 59136, KT * P)
    wab_lo = at("wab_lo", W2 + 59136, KT * P, F32R)

    codes_d = {"F1": at("codes_d1", R1, JT * D, I32), "F2": at("codes_d2", W2 + 16384, JT * D, I32)}
    w_d = {"F1": at("w_d1", R1, JT * D, F32R), "F2": at("w_d2", W2 + 16384, JT * D, F32R)}
    silu = at("silu", W2 + 40960, 2 * GROUP)
    hid = at("hid", W2 + 45056, 2 * GROUP)
    hid_hi = {"F1": at("hid_hi1", W2 + 32768, 4 * GROUP, F32R), "F2": at("hid_hi2", W2, 4 * GROUP, F32R)}
    hid_lo = at("hid_lo", W2 + 49152, 4 * GROUP, F32R)
    yt = at("yt", W2 + 57344, 2 * D)

    qk_hi = at("qk_hi", W2, 2 * KT * D, F32R)
    qk_raw = at("qk_raw", W2 + 16384, 2 * KT * D)
    qk_lo = at("qk_lo", W2 + 16384, 2 * KT * D, F32R)
    wvT_raw = at("wvT_raw", R1, KT * D)
    wvT_lo = at("wvT_lo", R1, KT * D, F32R)
    wvT_hi = at("wvT_hi", R1 + 8192, KT * D, F32R)
    wo_hi = at("wo_hi", R1 + 16384, KT * D, F32R)
    wo_raw = at("wo_raw", R1 + 24576, KT * D)
    wo_lo = at("wo_lo", R1 + 24576, KT * D, F32R)
    g_hi = at("g_hi", W2 + 32768, KT * D, F32R)
    g_lo = at("g_lo", W2 + 40960, KT * D, F32R)
    aT_hi = at("aT_hi", W2, KT * GROUP, F32R)
    aT_lo = at("aT_lo", W2 + 8192, KT * GROUP, F32R)
    wvo_hi = at("wvo_hi", W2 + 16384, KT * D, F32R)
    wvo_lo = at("wvo_lo", W2 + 24576, KT * D, F32R)
    v_hi = at("v_hi", R1, BT * D, F32R)
    v_lo = at("v_lo", R1 + 16384, BT * D, F32R)
    probs = at("probs", W2 + 49152, BTOK)
    pT_hi = at("pT_hi", W2 + 53248, BTOK, F32R)
    pT_lo = at("pT_lo", W2 + 57344, BTOK, F32R)

    psum = nc.alloc_psum_tensor("psum", [P, 8 * 512], F32)

    def bank(i, n=1):
        return psum[:, i * 512:(i + n) * 512]

    def sem(name):
        return nc.alloc_semaphore(name)

    filled = [sem(f"psum_filled{i}") for i in range(8)]
    drained = [sem(f"psum_drained{i}") for i in range(8)]
    x_in = [sem(f"x_in{t}") for t in range(GT)]
    x_rest_in = sem("x_rest_in")
    wab_zero = sem("wab_zero")
    wab_in = sem("wab_in")
    wk_in = sem("wk_in")
    wv_in = sem("wv_in")
    wq_in = sem("wq_in")
    rows_in = sem("rows_in")
    cols_in = sem("cols_in")
    gu_in = sem("gu_in")
    qk_in = sem("qk_in")
    wvT_in = sem("wvT_in")
    wo_in = sem("wo_in")
    d_in = {"F1": sem("d1_in"), "F2": sem("d2_in")}
    d1_mid_in = sem("d1_mid_in")
    sd_in = sem("sd_in")
    x_out = sem("x_out")
    consts_set = sem("consts_set")
    consts_done = sem("consts_done")
    wa_hi = sem("wa_hi")
    wa_lo = sem("wa_lo")
    ln_bn_done = sem("ln_bn_done")
    ln_mv_done = sem("ln_mv_done")
    ln_var_done = sem("ln_var_done")
    ln_rstd_done = sem("ln_rstd_done")
    ln_xn_done = sem("ln_xn_done")
    xt_hi_done = sem("xt_hi_done")
    gate_dve = sem("gate_dve")
    gate_act = sem("gate_act")
    squares_done = sem("squares_done")
    squares_step = sem("squares_step")
    kscale_step = sem("kscale_step")
    k_scaled = sem("k_scaled")
    kw_ready = sem("kw_ready")
    steps_ready = sem("steps_ready")
    state_zero = sem("state_zero")
    gu_ready = sem("gu_ready")
    wd_ready = {"F1": sem("wd1_ready"), "F2": sem("wd2_ready")}
    hid_hi_ready = sem("hid_hi_ready")
    hid_split = sem("hid_split")
    down_done = sem("down_done")
    x_updated = sem("x_updated")
    qk_split = sem("qk_split")
    vo_hi_done = sem("vo_hi_done")
    vo_split = sem("vo_split")
    hi_done = sem("hi_done")
    pT_hi_done = sem("pT_hi_done")
    smax_done = sem("smax_done")
    nmax_done = sem("nmax_done")
    rden_done = sem("rden_done")

    def a_job(s, i):
        n = 13 * s + i
        return n % 2, n // 2

    def k_job(s, c):
        return a_job(s, 1 if c == 0 else 5 + 2 * c)

    def v_job(s, c):
        return a_job(s, 2 if c == 0 else 6 + 2 * c)

    PREP = {"start": lambda l: (2, l), "A": lambda l: (2, l), "F1": lambda l: (2 + l % 2, l // 2),
            "F2": lambda l: (2 + l % 2, l // 2),
            "B": lambda l: (6 + l % 2, l // 2) if l < 4 else (l % 2, 6 + l // 2)}

    def prep_use(phase, l):
        return PREP[phase](l)

    def prep_x(phase, b, l):
        if phase == "start":
            return xres[:, l * D:(l + 1) * D]
        if l < 4:
            return xres[:, bass.ds(b * (BT * D) + (4 + l) * D, D)]
        return xres[:, bass.ds(other_batch[0] + (l - 4) * D, D)]

    def prep_col(phase, l):
        return l * P if phase == "start" else ((l + 4) % 8) * P

    def xt_tile(t, col):
        return t[:, :].rearrange("p (k n) -> p k n", k=KT)[:, :, col:col + P]

    def ln_n(phase, b, l):
        return b * 8 + (LN_BASE[phase] + l)

    waits_alone = sem("waits_alone")

    def alone(eng):
        eng.sem_inc(waits_alone, 1)

    def pT(i):
        return (aT_hi[:, 0:BTOK], aT_lo[:, 0:BTOK]) if i == BT - 1 else (pT_hi[:, :], pT_lo[:, :])

    other_batch = [None]

    class Use:

        def __init__(self, eng, phase, b):
            self.eng, self.phase, self.b = eng, phase, b

        def value(self, use):
            return turn(self.phase, use[0], self.b, use[1])

        def free(self, use):
            self.eng.wait_ge(drained[use[0]], self.value(use))

        def full(self, use):
            self.eng.wait_ge(filled[use[0]], self.value(use))

        def read_out(self, use):
            self.eng.wait_ge(drained[use[0]], self.value(use) + 1)

    block = nc.Block()

    def cols(t, i, n=D):
        return t[:, i * n:(i + 1) * n]

    with block as blk:
        @blk.sync
        def _(sp):
            for i in range(8):
                sp.sem_inc(drained[i], 1)
            for s in (hid_split, x_updated):
                sp.sem_inc(s, RING)
            xv = x.rearrange("(g t p) d -> g p t d", p=P, t=GT)
            xs = [xres[:, g * GT * D:(g + 1) * GT * D].rearrange("p (t d) -> p t d", d=D) for g in range(4)]

            def weights(dst, src, s):
                sp.dma_start(dst.rearrange("p (k n) -> p k n", k=src.shape[0] // P),
                             src.rearrange("(k p) n -> p k n", p=P)).then_inc(s, 16)

            for t in range(GT):
                sp.dma_start(xres[:, t * D:(t + 1) * D], x[t * P:(t + 1) * P, :]).then_inc(x_in[t], 16)
            sp.wait_ge(wab_zero, 1)
            wab = wab_raw[:, :].rearrange("p (k n) -> p k n", k=KT)
            sp.dma_start(wab[:, :, 0:2 * HEADS], w_ab.rearrange("(k p) n -> p k n", p=P)).then_inc(wab_in, 16)
            weights(wqk_raw[:, KT * D:2 * KT * D], wk, wk_in)
            sp.dma_start(bk_rows[:, :], bk.partition_broadcast(P)).then_inc(rows_in, 16)
            sp.dma_start(bv_rows[:, :], bv.partition_broadcast(P)).then_inc(rows_in, 16)
            sp.dma_start(ab_bias[:, :], b_ab.partition_broadcast(P)).then_inc(rows_in, 16)
            sp.dma_start(bq_col[:, :], bq).then_inc(rows_in, 16)
            weights(wv_raw[:, :], wv, wv_in)
            weights(wqk_raw[:, 0:KT * D], wq, wq_in)
            for g in range(1, 4):
                sp.dma_start(xs[g], xv[g]).then_inc(x_rest_in, 16)
            sp.dma_start(sg_col[:, :], s_gate).then_inc(cols_in, 16)
            sp.dma_start(su_col[:, :], s_up).then_inc(cols_in, 16)
            weights(codes_gu[:, 0:4 * HID], gateT, gu_in)
            weights(codes_gu[:, 4 * HID:8 * HID], upT, gu_in)
            use = Use(sp, "A", 1)
            for h in (2, 3):
                use.full(a_job(1, 3 + h))
            weights(codes_d["F1"][:, 0:4 * D], downT[0:4 * P, :], d_in["F1"])
            weights(codes_d["F1"][:, 8 * D:JT * D], downT[8 * P:JT * P, :], d_in["F1"])
            use.full(k_job(1, 3))
            weights(codes_d["F1"][:, 4 * D:8 * D], downT[4 * P:8 * P, :], d1_mid_in)
            weights(wo_raw[:, :], wo, wo_in)
            use.read_out((7, 7))
            sp.dma_start(sd_rows[:, :], s_down.partition_broadcast(P)).then_inc(sd_in, 16)
            weights(qk_raw[:, 0:KT * D], wqT, qk_in)
            weights(qk_raw[:, KT * D:2 * KT * D], wkT, qk_in)
            sp.wait_ge(down_done, 20 + 10 + KT)
            weights(wvT_raw[:, :], wvT, wvT_in)
            use = Use(sp, "B", 1)
            use.full((0, 7))
            use.full((1, 7))
            weights(codes_d["F2"][:, :], downT, d_in["F2"])
            for t in range(4 * GT):
                sp.wait_ge(x_updated, RING + 16 + t + 1)
                sp.dma_start(out[t * P:(t + 1) * P, :], xres[:, t * D:(t + 1) * D]).then_inc(x_out, 16)
            sp.wait_ge(x_out, 4 * GT * 16)

        @blk.gpsimd
        def _(pool):
            def rstd(n, slot):
                pool.wait_ge(ln_var_done, n + 1)
                nc.gpsimd.tensor_tensor(ln_rstd[:, slot:slot + 1], ln_var[:, slot:slot + 1],
                                        minus_half[:, 0:1], ALU.pow).then_inc(ln_rstd_done, 1)

            nc.gpsimd.memset(wab_raw[:, :], 0.0).then_inc(wab_zero, 1)
            nc.gpsimd.memset(minus_half[:, :], -0.5).then_inc(consts_set, 1)
            nc.gpsimd.memset(ident[:, :], 0.0).then_inc(consts_set, 1)
            nc.gpsimd.memset(ident_b[:, :], 0.0).then_inc(consts_set, 1)
            nc.gpsimd.memset(tri[:, :], 1.0).then_inc(consts_set, 1)
            nc.gpsimd.memset(ones[:, :], 1.0).then_inc(consts_set, 1)
            nc.gpsimd.memset(ones_r[:, :].bitcast(F32), 1.0).then_inc(consts_set, 1)
            nc.gpsimd.memset(mask_b[:, :], 0.0).then_inc(consts_set, 1)
            pool.wait_ge(consts_set, 7)
            for m in (ident, ident_b):
                nc.gpsimd.affine_select(out=m[:, :], in_=m[:, :], compare_op=ALU.not_equal, fill=1.0,
                                        base=0, pattern=[[-1, P]], channel_multiplier=1).then_inc(consts_done, 1)
            nc.gpsimd.affine_select(out=tri[:, :], in_=tri[:, :], compare_op=ALU.is_ge, fill=0.0,
                                    base=0, pattern=[[1, P]], channel_multiplier=-1).then_inc(consts_done, 1)
            mv = mask_b[:, :].rearrange("p (h c) -> p h c", h=HEADS)
            nc.gpsimd.affine_select(out=mv, in_=mv, compare_op=ALU.is_ge, fill=MASKED,
                                    base=0, pattern=[[0, HEADS], [1, P]], channel_multiplier=-1).then_inc(consts_done, 1)
            pool.wait_ge(consts_done, 4)
            nc.gpsimd.tensor_copy(tri_r[:, :], tri[:, :]).then_inc(consts_done, 1)
            pool.wait_ge(consts_done, 5)
            for l in range(4):
                rstd(l, l)

            with pool.Fori(0, BATCHES) as b:
                def scale_k(s, c):
                    n = b * 8 + (4 * s + c)
                    r = 4 * (c % 2)
                    pool.wait_ge(squares_done, n + 1)
                    alone(pool)
                    nc.gpsimd.tensor_scalar(kscale[:, r:r + 4], sumsq[:, r:r + 4], NORM_FLOOR ** 2, None,
                                            ALU.max).then_inc(kscale_step, 1)
                    pool.wait_ge(kscale_step, n * 3 + 1)
                    nc.gpsimd.tensor_tensor(kscale[:, r:r + 4], kscale[:, r:r + 4], minus_half[:, :],
                                            ALU.pow).then_inc(kscale_step, 1)
                    pool.wait_ge(kscale_step, n * 3 + 2)
                    if c == 0:
                        pool.wait_ge(gate_dve, b * 20 + (10 * s + 8))
                    nc.gpsimd.tensor_tensor(kscale[:, r:r + 4], kscale[:, r:r + 4],
                                            beta[:, 16 * s + 4 * c:16 * s + 4 * c + 4],
                                            ALU.mult).then_inc(kscale_step, 1)
                    pool.wait_ge(kscale_step, n * 3 + 3)
                    kv = cols(kn, c % 2).rearrange("p (h d) -> p h d", h=HEADS)
                    nc.gpsimd.tensor_tensor(kv, kv, kscale[:, r:r + 4].unsqueeze(2).broadcast_to([P, HEADS, P]),
                                            ALU.mult).then_inc(k_scaled, 1)

                def log_steps(s, c):
                    if c == 0:
                        pool.wait_ge(gate_dve, b * 20 + (10 * s + 10))
                    tv = tri_r[:, :].bitcast(F32).unsqueeze(1).broadcast_to([P, HEADS, P])
                    for dst, src in ((steps_hi, la_hi), (steps_lo, la_lo)):
                        sv = src[:, 16 * s + 4 * c:16 * s + 4 * c + 4].bitcast(F32)
                        nc.gpsimd.tensor_tensor(dst[:, :].rearrange("p (h d) -> p h d", h=HEADS),
                                                sv.unsqueeze(2).broadcast_to([P, HEADS, P]), tv,
                                                ALU.mult).then_inc(steps_ready, 1)

                def weight_k(s, c):
                    u = Use(pool, "A", b)
                    u.read_out((4, 4 * s + c))
                    kv = cols(kn, c % 2).rearrange("p (h d) -> p h d", h=HEADS)
                    dv = decay[:, :].rearrange("p (h d) -> p h d", h=HEADS)[:, :, P - 1:P]
                    nc.gpsimd.tensor_tensor(kw[:, :].rearrange("p (h d) -> p h d", h=HEADS), kv,
                                            dv.broadcast_to([P, HEADS, P]), ALU.mult).then_inc(kw_ready, 1)

                for s in range(2):
                    if s == 0:
                        scale_k(0, 0)
                        log_steps(0, 0)
                    for c in range(4):
                        if c < 2:
                            for l in (4 * s + 2 * c, 4 * s + 2 * c + 1):
                                rstd(ln_n("A", b, l), l % 4)
                        if c < 3:
                            scale_k(s, c + 1)
                        weight_k(s, c)
                        if c < 3:
                            log_steps(s, c + 1)
                        elif s == 0:
                            scale_k(1, 0)
                            log_steps(1, 0)

            def ffn(phase):
                pool.wait_ge(d_in[phase], 32 if phase == "F1" else 16)
                for j in range(8 if phase == "F1" else 0, JT):
                    nc.gpsimd.tensor_scalar(cols(w_d[phase], j), cols(codes_d[phase], j),
                                            -ZERO_POINT, None, ALU.add).then_inc(wd_ready[phase], 1)
                with pool.Fori(0, BATCHES) as b:
                    def add_y(s, t):
                        n = b * 8 + (16 * FFN_BASE[phase] + 4 * s + t)
                        u = Use(pool, phase, b)
                        u.read_out((4 + t, s))
                        xs = xres[:, bass.ds(b * (BT * D) + (4 * s + t) * D, D)]
                        nc.gpsimd.tensor_tensor(xs, xs, cols(yt, t % 2), ALU.add).then_inc(x_updated, 1)

                    for J in range(2 * JT):
                        s, j = J // JT, J % JT
                        n = b * 22 + (44 * FFN_BASE[phase] + J)
                        pool.wait_ge(hid_hi_ready, n + 1)
                        nc.gpsimd.tensor_tensor(cols(hid_lo, J % 4), cols(hid, J % 2),
                                                cols(hid_hi[phase], J % 4).bitcast(F32),
                                                ALU.subtract).then_inc(hid_split, 1)
                        if J == JT + 1:
                            for t in range(4):
                                add_y(0, t)
                        if j in (1, 3, 5, 7):
                            l = 4 * s + j // 2
                            rstd(ln_n(phase, b, l), l % 4)
                        if phase == "F1" and j in (8, 10):
                            i = 2 * s + (j - 8) // 2
                            m = b * 4 + i
                            if i == 0:
                                pool.wait_ge(qk_in, 32)
                            piece = bass.ds(b * (KT * D) + i * D, D)
                            nc.gpsimd.tensor_copy(qk_hi[:, piece], qk_raw[:, piece]).then_inc(qk_split, 1)
                            pool.wait_ge(qk_split, m * 2 + 1)
                            alone(pool)
                            nc.gpsimd.tensor_tensor(qk_lo[:, piece], qk_raw[:, piece],
                                                    qk_hi[:, piece].bitcast(F32),
                                                    ALU.subtract).then_inc(qk_split, 1)
                    for t in range(4):
                        add_y(1, t)

            ffn("F1")
            with pool.Fori(0, BATCHES) as b:
                for l in range(8):
                    rstd(ln_n("B", b, l), l % 4)
            ffn("F2")

        @blk.scalar
        def _(act):
            def split_hi(phase, b, l):
                use = prep_use(phase, l)
                Use(act, phase, b).full(use)
                nc.scalar.activation(xt_tile(xt_hi, prep_col(phase, l)),
                                     bank(use[0]).rearrange("p (k n) -> p k n", k=KT),
                                     ACT.Copy).then_inc(xt_hi_done, 1)

            nc.scalar.preload_act_table_set("natural_log_exp_and_others")
            act.wait_ge(wab_in, 16)
            nc.scalar.activation(wab_hi[:, :], wab_raw[:, :], ACT.Copy).then_inc(wa_hi, 1)
            for l in range(4):
                split_hi("start", 0, l)
            for w_in, hi, raw, w0 in ((wk_in, wqk_hi, wqk_raw, KT), (wv_in, wv_hi, wv_raw, 0),
                                      (wq_in, wqk_hi, wqk_raw, 0)):
                act.wait_ge(w_in, 16)
                for k in range(KT):
                    nc.scalar.activation(cols(hi, w0 + k), cols(raw, w0 + k), ACT.Copy).then_inc(wa_hi, 1)
            act.wait_ge(rows_in, 4 * 16)

            with act.Fori(0, BATCHES) as b:
                u = Use(act, "A", b)

                def logits_row(s):
                    use = a_job(s, 0)
                    u.full(use)
                    nc.scalar.activation(ab_row[0:8, :], bank(use[0])[0:8, :], ACT.Copy).then_inc(drained[use[0]], 1)

                def norms(s, c):
                    u.read_out(k_job(s, c))
                    r = 4 * (c % 2)
                    for h in range(HEADS):
                        last = nc.scalar.activation(squares[:, :], kn[:, (c % 2) * D + h * P:(c % 2) * D + (h + 1) * P],
                                                    ACT.Square, accum_out=sumsq[:, r + h:r + h + 1])
                        last.then_inc(squares_done if h == HEADS - 1 else squares_step, 1)
                        if h < HEADS - 1:
                            act.wait_ge(squares_step, (b * 8 + (4 * s + c)) * 3 + (h + 1))

                def gate_exp(s):
                    act.wait_ge(gate_dve, b * 20 + (10 * s + 1))
                    nc.scalar.activation(g_e[:, :], g_zz[:, :], ACT.Exp, scale=-1.0).then_inc(gate_act, 1)

                def gate_logs(s):
                    act.wait_ge(gate_dve, b * 20 + (10 * s + 4))
                    nc.scalar.activation(g_la[:, :], g_a[:, :], ACT.Ln).then_inc(gate_act, 1)
                    nc.scalar.activation(g_lb[:, :], g_u[:, 16:32], ACT.Ln).then_inc(gate_act, 1)

                def q_out(s, h):
                    use = a_job(s, 3 + h)
                    u.full(use)
                    nc.scalar.activation(qT[:, h * GROUP:(h + 1) * GROUP], bank(use[0]), ACT.Identity,
                                         bias=bq_col[:, h:h + 1]).then_inc(drained[use[0]], 1)

                def gate_decays(s):
                    u.full((3, 6 * s + 1))
                    nc.scalar.activation(decays[:, 32 * s:32 * s + 32], bank(3)[:, 0:32], ACT.Exp).then_inc(gate_act, 1)
                    nc.scalar.activation(negcla[:, 16 * s:16 * s + 16], bank(3)[:, 0:16], ACT.Copy,
                                         scale=-1.0).then_inc(drained[3], 1)

                def kT_out(s, c):
                    use = (3, 6 * s + 2 + c)
                    u.full(use)
                    nc.scalar.activation(kT[:, :], bank(3), ACT.Copy).then_inc(drained[3], 1)

                def decay_out(s, c):
                    use = (4, 4 * s + c)
                    if c == 0:
                        u.read_out((3, 6 * s + 1))
                    u.full(use)
                    for h in range(HEADS):
                        i = 16 * s + 4 * c + h
                        last = nc.scalar.activation(decay[:, h * P:(h + 1) * P], bank(4)[:, h * P:(h + 1) * P],
                                                    ACT.Exp, bias=negcla[:, i:i + 1])
                    last.then_inc(drained[4], 1)

                def head(s):
                    q_out(s, 0)
                    gate_logs(s)
                    q_out(s, 1)
                    q_out(s, 2)
                    gate_decays(s)
                    q_out(s, 3)

                logits_row(0)
                norms(0, 0)
                gate_exp(0)
                head(0)
                for s in range(2):
                    for c in range(4):
                        kT_out(s, c)
                        if c < 3:
                            norms(s, c + 1)
                        elif s == 0:
                            logits_row(1)
                            norms(1, 0)
                            gate_exp(1)
                        if c < 2:
                            split_hi("A", b, 4 * s + 2 * c)
                        decay_out(s, c)
                        if c < 2:
                            split_hi("A", b, 4 * s + 2 * c + 1)
                        if c == 3 and s == 0:
                            head(1)

            def ffn(phase):
                nc.scalar.preload_act_table(ACT.Silu)
                act.wait_ge(cols_in, 32)
                with act.Fori(0, BATCHES) as b:
                    u = Use(act, phase, b)
                    for J in range(2 * JT):
                        s, j = J // JT, J % JT
                        u.full((0, J))
                        act.wait_ge(drained[1], u.value((1, J)) - 1)
                        nc.scalar.activation(cols(silu, J % 2), bank(0), ACT.Silu,
                                             scale=sg_col[:, j:j + 1]).then_inc(drained[0], 1)
                        u.read_out((1, J))
                        if J >= 4 and (J - 4) % JT < JT - 1:
                            act.wait_ge(down_done, b * 20 + (40 * FFN_BASE[phase] + (J - 4) // JT * 10
                                                             + (J - 4) % JT + 1))
                        elif J >= 4:
                            u.full((7, (J - 4) // JT))
                        nc.scalar.activation(cols(hid_hi[phase], J % 4), cols(hid, J % 2),
                                             ACT.Copy).then_inc(hid_hi_ready, 1)
                        if j in (3, 5, 7, 9):
                            split_hi(phase, b, 4 * s + (j - 3) // 2)

            ffn("F1")

            nc.scalar.preload_act_table(ACT.Exp)
            act.wait_ge(wo_in, 16)
            act.wait_ge(wvT_in, 16)
            Use(act, "F1", 1).full((7, 1))
            um = Use(act, "mid", 0)
            for i in range(8):
                if i < 4:
                    nc.scalar.activation(cols(wvT_hi, i), cols(wvT_raw, i), ACT.Copy).then_inc(vo_hi_done, 1)
                    nc.scalar.activation(cols(wo_hi, i), cols(wo_raw, i), ACT.Copy).then_inc(vo_hi_done, 1)
                um.full((i % 2, i // 2))
                nc.scalar.activation(cols(g_hi if i < 4 else wvo_hi, i % 4), bank(i % 2), ACT.Copy).then_inc(hi_done, 1)

            with act.Fori(0, BATCHES) as b:
                u = Use(act, "B", b)

                def high(dst, job):
                    u.full((job % 2, job // 2))
                    nc.scalar.activation(dst, bank(job % 2), ACT.Copy).then_inc(hi_done, 1)

                def softmax(i):
                    u.full((4, i))
                    act.wait_ge(nmax_done, b * 8 + (i + 1))
                    nc.scalar.activation(probs[:, :], bank(4, 2), ACT.Exp, scale=SCALE,
                                         bias=nmax[:, i % 2:i % 2 + 1],
                                         accum_out=rowsum[:, i % 2:i % 2 + 1]).then_inc(drained[4], 1)

                def pT_high(i):
                    u.full((2, i))
                    nc.scalar.activation(pT(i)[0], bank(2, 2), ACT.Copy).then_inc(pT_hi_done, 1)

                high(cols(v_hi, 0), 0)
                high(cols(v_hi, 1), 1)
                split_hi("B", b, 0)
                split_hi("B", b, 1)
                high(cols(v_hi, 2), 2)
                high(cols(v_hi, 3), 3)
                split_hi("B", b, 2)
                split_hi("B", b, 3)
                for i in range(4):
                    high(cols(aT_hi, i), 4 + i)
                high(cols(v_hi, 4), 8)
                high(cols(v_hi, 5), 9)
                softmax(0)
                high(cols(v_hi, 6), 10)
                high(cols(v_hi, 7), 11)
                pT_high(0)
                for i in range(1, 8):
                    softmax(i)
                    if i == 3:
                        for m in range(4):
                            high(cols(aT_hi, m), 12 + m)
                    if i == 7:
                        split_hi("B", b, 4)
                        split_hi("B", b, 5)
                    pT_high(i)
                split_hi("B", b, 6)
                split_hi("B", b, 7)

            ffn("F2")

        @blk.vector
        def _(dve):
            def stats(phase, b, l):
                n, r = ln_n(phase, b, l), l % 4
                nc.vector.bn_stats(ln_bn[:, 6 * r:6 * r + 6], prep_x(phase, b, l)).then_inc(ln_bn_done, 1)
                dve.wait_ge(ln_bn_done, n + 1)
                alone(dve)
                nc.vector.bn_aggr(ln_mv[:, 2 * r:2 * r + 2], ln_bn[:, 6 * r:6 * r + 6]).then_inc(ln_mv_done, 1)
                dve.wait_ge(ln_mv_done, n + 1)
                nc.vector.tensor_scalar(ln_var[:, r:r + 1], ln_mv[:, 2 * r + 1:2 * r + 2], LN_EPS, None,
                                        ALU.add).then_inc(ln_var_done, 1)

            def normalise(phase, b, l):
                n, r = ln_n(phase, b, l), l % 4
                dve.wait_ge(ln_rstd_done, n + 1)
                nc.vector.tensor_scalar(cols(xn, l % 2), prep_x(phase, b, l), ln_mv[:, 2 * r:2 * r + 1],
                                        ln_rstd[:, r:r + 1], ALU.subtract, ALU.mult).then_inc(ln_xn_done, 1)

            def split_lo(phase, b, l):
                use = prep_use(phase, l)
                dve.wait_ge(xt_hi_done, ln_n(phase, b, l) + 1)
                nc.vector.tensor_tensor(xt_tile(xt_lo, prep_col(phase, l)),
                                        bank(use[0]).rearrange("p (k n) -> p k n", k=KT),
                                        xt_tile(xt_hi, prep_col(phase, l)).bitcast(F32),
                                        ALU.subtract).then_inc(drained[use[0]], 1)

            def prep_four(phase, b, l0):
                for l in range(l0, l0 + 4):
                    dve.wait_ge(x_in[l], 16)
                    stats(phase, b, l)
                normalise(phase, b, l0)
                normalise(phase, b, l0 + 1)
                split_lo(phase, b, l0)
                normalise(phase, b, l0 + 2)
                split_lo(phase, b, l0 + 1)
                normalise(phase, b, l0 + 3)
                split_lo(phase, b, l0 + 2)
                split_lo(phase, b, l0 + 3)

            prep_four("start", 0, 0)
            dve.wait_ge(wa_hi, 1)
            nc.vector.tensor_tensor(wab_lo[:, :], wab_raw[:, :], wab_hi[:, :].bitcast(F32),
                                    ALU.subtract).then_inc(wa_lo, 1)
            for i, (lo, raw, hi, w0) in enumerate(((wqk_lo, wqk_raw, wqk_hi, KT), (wv_lo, wv_raw, wv_hi, 0),
                                                   (wqk_lo, wqk_raw, wqk_hi, 0))):
                for k in range(KT):
                    dve.wait_ge(wa_hi, KT * i + k + 2)
                    nc.vector.tensor_tensor(cols(lo, w0 + k), cols(raw, w0 + k), cols(hi, w0 + k).bitcast(F32),
                                            ALU.subtract).then_inc(wa_lo, 1)
            dve.wait_ge(rows_in, 4 * 16)

            with dve.Fori(0, BATCHES) as b:
                row0 = dve.snap(b * (BT * D))
                other_batch[0] = dve.snap(BT * D - row0)
                u = Use(dve, "A", b)
                z3 = g_z[:, :].rearrange("p (c k) -> p c k", c=4)

                def four(ap):
                    return ap.rearrange("p (c h) -> p c h", c=4)

                def k_out(s, c):
                    use = k_job(s, c)
                    u.full(use)
                    nc.vector.tensor_tensor(cols(kn, c % 2), bank(use[0]), bk_rows[:, :],
                                            ALU.add).then_inc(drained[use[0]], 1)

                def v_out(s, c):
                    use = v_job(s, c)
                    u.full(use)
                    nc.vector.tensor_tensor(cols(vn, c % 2), bank(use[0]), bv_rows[:, :],
                                            ALU.add).then_inc(drained[use[0]], 1)

                def gate_a(s):
                    use = (3, 6 * s)
                    u.full(use)
                    nc.vector.tensor_tensor(z3, bank(3)[:, 0:32].rearrange("p (c k) -> p c k", c=4),
                                            ab_bias[:, :].unsqueeze(1).broadcast_to([P, 4, 8]),
                                            ALU.add).then_inc(drained[3], 1)
                    u.read_out(use)
                    nc.vector.tensor_scalar(four(g_zz[:, 0:16]), z3[:, :, 0:4], -80.0, None,
                                            ALU.max)
                    nc.vector.scalar_tensor_tensor(out=four(g_zz[:, 16:32]), in0=z3[:, :, 4:8], scalar=-1.0,
                                                   in1=z3[:, :, 4:8], op0=ALU.mult,
                                                   op1=ALU.max).then_inc(gate_dve, 1)

                def gate_b(s):
                    g = b * 20 + 10 * s
                    dve.wait_ge(gate_act, b * 8 + (4 * s + 1))
                    nc.vector.tensor_scalar(g_u[:, :], g_e[:, :], 1.0, None, ALU.add).then_inc(gate_dve, 1)
                    dve.wait_ge(gate_dve, g + 2)
                    nc.vector.reciprocal(g_r[:, :], g_u[:, :]).then_inc(gate_dve, 1)
                    dve.wait_ge(gate_dve, g + 3)
                    nc.vector.tensor_scalar(g_a[:, :], g_r[:, 0:16], 1e-6, None, ALU.add).then_inc(gate_dve, 1)
                    nc.vector.scalar_tensor_tensor(out=g_c[:, :], in0=g_u[:, 16:32], scalar=1.0, in1=g_e[:, 16:32],
                                                   op0=ALU.subtract, op1=ALU.subtract).then_inc(gate_dve, 1)
                    dve.wait_ge(gate_dve, g + 5)
                    nc.vector.tensor_tensor(g_c2[:, :], g_c[:, :], g_r[:, 16:32], ALU.mult).then_inc(gate_dve, 1)
                    dve.wait_ge(gate_dve, g + 6)
                    nc.vector.scalar_tensor_tensor(out=four(g_zm[:, :]), in0=z3[:, :, 4:8], scalar=0.0,
                                                   in1=four(g_c2[:, :]), op0=ALU.max,
                                                   op1=ALU.subtract).then_inc(gate_dve, 1)

                def gate_c(s):
                    g = b * 20 + 10 * s
                    o = slice(16 * s, 16 * s + 16)
                    dve.wait_ge(gate_act, b * 8 + (4 * s + 3))
                    dve.wait_ge(gate_dve, g + 7)
                    nc.vector.tensor_tensor(beta[:, o], g_zm[:, :], g_lb[:, :], ALU.add).then_inc(gate_dve, 1)
                    nc.vector.tensor_copy(la_hi[:, o], g_la[:, :]).then_inc(gate_dve, 1)
                    dve.wait_ge(gate_dve, g + 9)
                    nc.vector.tensor_tensor(la_lo[:, o], g_la[:, :], la_hi[:, o].bitcast(F32),
                                            ALU.subtract).then_inc(gate_dve, 1)

                def attn_out(s, c):
                    n = 4 * s + c
                    u.full((5, 2 * n))
                    u.read_out((4, n))
                    nc.vector.tensor_tensor(attnT[:, :], bank(5), decay[:, :], ALU.mult).then_inc(drained[5], 1)

                def state_out(s, c):
                    n = 4 * s + c
                    if n == 0:
                        dve.wait_ge(state_zero, b + 1)
                    u.free((5, 2 * n + 1))
                    u.full((5, 2 * n + 1))
                    for h in range(HEADS):
                        i = 32 * s + 16 + 4 * c + h
                        hs = slice(h * P, (h + 1) * P)
                        last = nc.vector.scalar_tensor_tensor(out=state[:, hs], in0=state[:, hs],
                                                              scalar=decays[:, i:i + 1], in1=bank(5)[:, hs],
                                                              op0=ALU.mult, op1=ALU.add)
                    last.then_inc(drained[5], 1)

                def y_out(s, c):
                    n = 4 * s + c
                    u.full((6, n))
                    for h in range(HEADS):
                        i = 32 * s + 4 * c + h
                        xs = xres[:, bass.ds(row0 + (n * D + h * P), P)]
                        last = nc.vector.scalar_tensor_tensor(out=xs, in0=bank(6)[:, h * P:(h + 1) * P],
                                                              scalar=decays[:, i:i + 1], in1=xs,
                                                              op0=ALU.mult, op1=ALU.add)
                    last.then_inc(drained[6], 1)
                    u.read_out((6, n))
                    u.full((7, n))
                    xs = xres[:, bass.ds(row0 + n * D, D)]
                    nc.vector.tensor_tensor(xs, xs, bank(7), ALU.add).then_inc(drained[7], 1)

                nc.vector.memset(state[:, :], 0.0).then_inc(state_zero, 1)
                k_out(0, 0)
                gate_a(0)
                v_out(0, 0)
                gate_b(0)
                dve.wait_ge(x_rest_in, 48)
                stats("A", b, 0)
                stats("A", b, 1)
                gate_c(0)
                for s in range(2):
                    for c in range(4):
                        l = 4 * s + 2 * c
                        if c < 2:
                            normalise("A", b, l)
                            normalise("A", b, l + 1)
                        if c < 3:
                            k_out(s, c + 1)
                        elif s == 0:
                            k_out(1, 0)
                            gate_a(1)
                        if c < 2:
                            split_lo("A", b, l)
                        attn_out(s, c)
                        if c < 3:
                            v_out(s, c + 1)
                        elif s == 0:
                            v_out(1, 0)
                            gate_b(1)
                        if c < 2:
                            split_lo("A", b, l + 1)
                        if c == 0:
                            if s == 1:
                                u.read_out((7, 3))
                                alone(dve)
                            stats("A", b, l + 2)
                            stats("A", b, l + 3)
                        state_out(s, c)
                        y_out(s, c)
                        if s == 1:
                            if c == 0:
                                dve.wait_ge(gu_in, 32)
                            piece = bass.ds(b * (4 * HID) + c * HID, HID)
                            nc.vector.tensor_scalar(w_gu[:, piece], codes_gu[:, piece], -ZERO_POINT, None,
                                                    ALU.add).then_inc(gu_ready, 1)
                        if c == 3 and s == 0:
                            gate_c(1)
                            u.read_out((7, 3))
                            alone(dve)
                            stats("A", b, 4)
                            stats("A", b, 5)

            def ffn(phase):
                if phase == "F1":
                    dve.wait_ge(d_in[phase], 32)
                    nc.vector.tensor_scalar(w_d[phase][:, 0:4 * D], codes_d[phase][:, 0:4 * D], -ZERO_POINT, None,
                                            ALU.add).then_inc(wd_ready[phase], 1)
                    dve.wait_ge(d1_mid_in, 16)
                    nc.vector.tensor_scalar(w_d[phase][:, 4 * D:8 * D], codes_d[phase][:, 4 * D:8 * D], -ZERO_POINT,
                                            None, ALU.add).then_inc(wd_ready[phase], 1)
                    Use(dve, "A", 1).read_out((7, 7))
                else:
                    Use(dve, "B", 1).read_out((7, 5))
                    Use(dve, "B", 1).read_out((6, 5))
                dve.wait_ge(cols_in, 32)
                with dve.Fori(0, BATCHES) as b:
                    row0 = dve.snap(b * (BT * D))
                    other_batch[0] = dve.snap(BT * D - row0)
                    u = Use(dve, phase, b)

                    def residual(s):
                        for t in range(4):
                            n = b * 8 + (16 * FFN_BASE[phase] + 4 * s + t)
                            u.full((4 + t, s))
                            if t == 0 and s == 0:
                                dve.wait_ge(sd_in, 16)
                            dve.wait_ge(x_updated, n + 1)
                            nc.vector.tensor_tensor(cols(yt, t % 2), bank(4 + t), sd_rows[:, :],
                                                    ALU.mult).then_inc(drained[4 + t], 1)

                    for J in range(2 * JT):
                        s, j = J // JT, J % JT
                        n = b * 22 + (44 * FFN_BASE[phase] + J)
                        u.full((1, J))
                        u.read_out((0, J))
                        dve.wait_ge(hid_split, n + 1)
                        nc.vector.scalar_tensor_tensor(out=cols(hid, J % 2), in0=bank(1), scalar=su_col[:, j:j + 1],
                                                       in1=cols(silu, J % 2), op0=ALU.mult,
                                                       op1=ALU.mult).then_inc(drained[1], 1)
                        if J == JT + 1:
                            residual(0)
                        if j in (3, 5, 7, 9):
                            split_lo(phase, b, 4 * s + (j - 3) // 2)
                        if j in (1, 3, 5, 7):
                            if j == 1 and s == 1:
                                dve.wait_ge(x_updated, b * 8 + (16 * FFN_BASE[phase] + RING))
                                alone(dve)
                            stats(phase, b, 4 * s + j // 2)
                        if j in (2, 4, 6, 8):
                            normalise(phase, b, 4 * s + j // 2 - 1)
                    residual(1)

            ffn("F1")

            for i in range(8):
                if i < 4:
                    dve.wait_ge(vo_hi_done, 2 * i + 1)
                    nc.vector.tensor_tensor(cols(wvT_lo, i), cols(wvT_raw, i), cols(wvT_hi, i).bitcast(F32),
                                            ALU.subtract).then_inc(vo_split, 1)
                    dve.wait_ge(vo_hi_done, 2 * i + 2)
                    nc.vector.tensor_tensor(cols(wo_lo, i), cols(wo_raw, i), cols(wo_hi, i).bitcast(F32),
                                            ALU.subtract).then_inc(vo_split, 1)
                dve.wait_ge(hi_done, i + 1)
                nc.vector.tensor_tensor(cols(g_lo if i < 4 else wvo_lo, i % 4), bank(i % 2),
                                        cols(g_hi if i < 4 else wvo_hi, i % 4).bitcast(F32),
                                        ALU.subtract).then_inc(drained[i % 2], 1)
            dve.wait_ge(x_updated, 16 + RING)

            with dve.Fori(0, BATCHES) as b:
                row0 = dve.snap(b * (BT * D))
                other_batch[0] = dve.snap(BT * D - row0)
                u = Use(dve, "B", b)

                def low(dst, hi, job, k):
                    dve.wait_ge(hi_done, b * 16 + (8 + k + 1))
                    nc.vector.tensor_tensor(dst, bank(job % 2), hi.bitcast(F32),
                                            ALU.subtract).then_inc(drained[job % 2], 1)

                def row_max(i):
                    r = slice(i % 2, i % 2 + 1)
                    u.full((4, i))
                    nc.vector.reduce_max(smax[:, r], bank(4, 2), AX.X).then_inc(smax_done, 1)
                    dve.wait_ge(smax_done, b * 8 + (i + 1))
                    nc.vector.tensor_scalar(nmax[:, r], smax[:, r], -SCALE, None, ALU.mult).then_inc(nmax_done, 1)

                def pT_low(i):
                    dve.wait_ge(pT_hi_done, b * 8 + (i + 1))
                    nc.vector.tensor_tensor(pT(i)[1], bank(2, 2), pT(i)[0].bitcast(F32),
                                            ALU.subtract).then_inc(drained[2], 1)

                def out_add(i):
                    r = slice(i % 2, i % 2 + 1)
                    u.read_out((4, i))
                    nc.vector.reciprocal(rden[:, r], rowsum[:, r]).then_inc(rden_done, 1)
                    dve.wait_ge(rden_done, b * 8 + (i + 1))
                    u.full((6 + i % 2, 2 + i // 2))
                    xs = xres[:, bass.ds(row0 + i * D, D)]
                    nc.vector.scalar_tensor_tensor(out=xs, in0=bank(6 + i % 2), scalar=rden[:, r], in1=xs,
                                                   op0=ALU.mult, op1=ALU.add).then_inc(drained[6 + i % 2], 1)

                stats("B", b, 0)
                stats("B", b, 1)
                normalise("B", b, 0)
                normalise("B", b, 1)
                low(cols(v_lo, 0), cols(v_hi, 0), 0, 0)
                stats("B", b, 2)
                stats("B", b, 3)
                low(cols(v_lo, 1), cols(v_hi, 1), 1, 1)
                split_lo("B", b, 0)
                normalise("B", b, 2)
                split_lo("B", b, 1)
                normalise("B", b, 3)
                low(cols(v_lo, 2), cols(v_hi, 2), 2, 2)
                low(cols(v_lo, 3), cols(v_hi, 3), 3, 3)
                split_lo("B", b, 2)
                split_lo("B", b, 3)
                for i in range(4):
                    low(cols(aT_lo, i), cols(aT_hi, i), 4 + i, 4 + i)
                low(cols(v_lo, 4), cols(v_hi, 4), 8, 8)
                low(cols(v_lo, 5), cols(v_hi, 5), 9, 9)
                row_max(0)
                low(cols(v_lo, 6), cols(v_hi, 6), 10, 10)
                low(cols(v_lo, 7), cols(v_hi, 7), 11, 11)
                pT_low(0)
                for i in range(1, 7):
                    row_max(i)
                    if i == 3:
                        for m in range(4):
                            low(cols(aT_lo, m), cols(aT_hi, m), 12 + m, 12 + m)
                    out_add(i - 1)
                    pT_low(i)
                    if i in (4, 5):
                        if i == 4:
                            u.free((6, 0))
                            u.free((7, 0))
                            alone(dve)
                        stats("B", b, 2 * i - 4)
                        stats("B", b, 2 * i - 3)
                    if i == 6:
                        normalise("B", b, 4)
                        normalise("B", b, 5)
                row_max(7)
                split_lo("B", b, 4)
                normalise("B", b, 6)
                split_lo("B", b, 5)
                normalise("B", b, 7)
                pT_low(7)
                out_add(6)
                split_lo("B", b, 6)
                split_lo("B", b, 7)
                out_add(7)

            ffn("F2")

        @blk.tensor
        def _(pe):
            def mm(out, lhsT, rhs, start, stop):
                return nc.tensor.matmul(out, lhsT, rhs, start=start, stop=stop)

            def product(out, left, right, ks=KT):
                for k in range(ks):
                    (lh, ll), (rh, rl) = left(k), right(k)
                    mm(out, lh, rh, k == 0, False)
                    mm(out, lh, rl, False, False)
                    last = mm(out, ll, rh, False, k == ks - 1)
                return last

            def pair(hi, lo, a, n):
                return hi[:, a:a + n], lo[:, a:a + n]

            def turn_tile(phase, b, l):
                use = prep_use(phase, l)
                pe.wait_ge(ln_xn_done, ln_n(phase, b, l) + 1)
                Use(pe, phase, b).free(use)
                for k in range(KT):
                    last = nc.tensor.transpose(bank(use[0])[:, k * P:(k + 1) * P],
                                               xn[:, (l % 2) * D + k * P:(l % 2) * D + (k + 1) * P], ident[:, :])
                last.then_inc(filled[use[0]], 1)

            def xt(k, col, n):
                return pair(xt_hi, xt_lo, k * BTOK + col, n)

            pe.wait_ge(consts_done, 5)
            for l in range(4):
                turn_tile("start", 0, l)
            pe.wait_ge(drained[2], turn("start", 2, 0, 3) + 1)

            with pe.Fori(0, BATCHES) as b:
                u = Use(pe, "A", b)
                u.free((2, 0))

                def logits(s):
                    use = a_job(s, 0)
                    pe.wait_ge(wa_lo, 1)
                    u.free(use)
                    product(bank(use[0]), lambda k: pair(wab_hi, wab_lo, k * P, P),
                            lambda k: xt(k, s * GROUP, GROUP)).then_inc(filled[use[0]], 1)

                def logits_turned(s):
                    u.read_out(a_job(s, 0))
                    u.free((3, 6 * s))
                    alone(pe)
                    for c in range(4):
                        last = nc.tensor.transpose(bank(3)[:, 8 * c:8 * c + 8], ab_row[0:8, c * P:(c + 1) * P],
                                                   ident[0:8, 0:8])
                    last.then_inc(filled[3], 1)

                def k_rows(s, c):
                    use = k_job(s, c)
                    pe.wait_ge(wa_lo, 1 + KT)
                    u.free(use)
                    product(bank(use[0]), lambda k: xt(k, s * GROUP + c * P, P),
                            lambda k: pair(wqk_hi, wqk_lo, (KT + k) * D, D)).then_inc(filled[use[0]], 1)

                def v_rows(s, c):
                    use = v_job(s, c)
                    pe.wait_ge(wa_lo, 1 + 2 * KT)
                    u.free(use)
                    product(bank(use[0]), lambda k: xt(k, s * GROUP + c * P, P),
                            lambda k: pair(wv_hi, wv_lo, k * D, D)).then_inc(filled[use[0]], 1)

                def q_cols(s, h):
                    use = a_job(s, 3 + h)
                    pe.wait_ge(wa_lo, 1 + 3 * KT)
                    u.free(use)
                    product(bank(use[0]), lambda k: pair(wqk_hi, wqk_lo, k * D + h * P, P),
                            lambda k: xt(k, s * GROUP, GROUP)).then_inc(filled[use[0]], 1)

                def log_sums(s):
                    pe.wait_ge(gate_act, b * 8 + (4 * s + 2))
                    u.free((3, 6 * s + 1))
                    mm(bank(3)[:, 0:16], tri[:, :], g_la[:, :], True, True)
                    mm(bank(3)[:, 16:32], ones[:, :], g_la[:, :], True, True).then_inc(filled[3], 1)

                def k_turned(s, c):
                    pe.wait_ge(k_scaled, b * 8 + (4 * s + c + 1))
                    u.free((3, 6 * s + 2 + c))
                    for h in range(HEADS):
                        last = nc.tensor.transpose(bank(3)[:, h * P:(h + 1) * P],
                                                   kn[:, (c % 2) * D + h * P:(c % 2) * D + (h + 1) * P], ident[:, :])
                    last.then_inc(filled[3], 1)

                def scores(s, c):
                    n = 4 * s + c
                    if c == 0:
                        u.read_out(a_job(s, 5))
                        u.read_out(a_job(s, 6))
                    u.read_out((3, 6 * s + 2 + c))
                    u.free((5, 2 * n))
                    for h in range(HEADS):
                        last = mm(bank(5)[:, h * P:(h + 1) * P], kT[:, h * P:(h + 1) * P],
                                  qT[:, h * GROUP + c * P:h * GROUP + (c + 1) * P], True, True)
                    last.then_inc(filled[5], 1)

                def log_decay(s, c):
                    n = 4 * s + c
                    pe.wait_ge(steps_ready, b * 16 + (2 * n + 2))
                    u.free((4, n))
                    mm(bank(4), ones_r[:, :], steps_hi[:, :], True, False)
                    mm(bank(4), ones_r[:, :], steps_lo[:, :], False, False)
                    mm(bank(4), ident_b[:, :], mask_b[:, :], False, True).then_inc(filled[4], 1)

                def core(s, c):
                    n = 4 * s + c
                    if n == 0:
                        pe.wait_ge(state_zero, b + 1)
                    u.free((6, n))
                    for h in range(HEADS):
                        last = mm(bank(6)[:, h * P:(h + 1) * P], qT[:, h * GROUP + c * P:h * GROUP + (c + 1) * P],
                                  state[:, h * P:(h + 1) * P], True, True)
                    last.then_inc(filled[6], 1)
                    u.read_out((5, 2 * n))
                    u.read_out(v_job(s, c))
                    u.free((7, n))
                    for h in range(HEADS):
                        last = mm(bank(7)[:, h * P:(h + 1) * P], attnT[:, h * P:(h + 1) * P],
                                  vn[:, (c % 2) * D + h * P:(c % 2) * D + (h + 1) * P], True, True)
                    last.then_inc(filled[7], 1)
                    pe.wait_ge(kw_ready, b * 8 + (n + 1))
                    for h in range(HEADS):
                        last = mm(bank(5)[:, h * P:(h + 1) * P], kw[:, h * P:(h + 1) * P],
                                  vn[:, (c % 2) * D + h * P:(c % 2) * D + (h + 1) * P], True, True)
                    last.then_inc(filled[5], 1)

                def head(s):
                    q_cols(s, 0)
                    q_cols(s, 1)
                    q_cols(s, 2)
                    log_sums(s)
                    q_cols(s, 3)

                logits(0)
                k_rows(0, 0)
                logits_turned(0)
                v_rows(0, 0)
                head(0)
                for s in range(2):
                    for c in range(4):
                        k_turned(s, c)
                        if c < 3:
                            k_rows(s, c + 1)
                        elif s == 0:
                            u.free((2, 4))
                            logits(1)
                            k_rows(1, 0)
                            logits_turned(1)
                        if c < 2:
                            turn_tile("A", b, 4 * s + 2 * c)
                        scores(s, c)
                        log_decay(s, c)
                        if c < 3:
                            v_rows(s, c + 1)
                        elif s == 0:
                            v_rows(1, 0)
                        if c < 2:
                            turn_tile("A", b, 4 * s + 2 * c + 1)
                        core(s, c)
                        if c == 3 and s == 0:
                            head(1)

            def ffn(phase):
                pe.wait_ge(gu_ready, 8)
                with pe.Fori(0, BATCHES) as b:
                    u = Use(pe, phase, b)
                    u.free((2, 0))
                    u.free((3, 0))

                    def up(J, out, w0):
                        s, j = J // JT, J % JT
                        u.free((out, J))
                        for k in range(KT):
                            w = w_gu[:, (w0 + k) * HID + j * P:(w0 + k) * HID + (j + 1) * P]
                            xh, xl = xt(k, s * GROUP, GROUP)
                            mm(bank(out), w, xh, k == 0, False)
                            last = mm(bank(out), w, xl, False, k == KT - 1)
                        last.then_inc(filled[out], 1)

                    def down(J):
                        s, j = J // JT, J % JT
                        n = b * 22 + (44 * FFN_BASE[phase] + J)
                        if J == 0:
                            pe.wait_ge(wd_ready[phase], 5 if phase == "F1" else JT)
                        pe.wait_ge(hid_split, n + (RING + 1))
                        for t in range(4):
                            if j == 0:
                                u.free((4 + t, s))
                            o = (J % 4) * GROUP + t * P
                            mm(bank(4 + t), hid_hi[phase][:, o:o + P], cols(w_d[phase], j), j == 0, False)
                            last = mm(bank(4 + t), hid_lo[:, o:o + P], cols(w_d[phase], j), False, j == JT - 1)
                            if j == JT - 1:
                                last.then_inc(filled[4 + t], 1)
                        if j < JT - 1:
                            last.then_inc(down_done, 1)

                    for J in range(2 * JT):
                        s, j = J // JT, J % JT
                        if J == JT:
                            u.free((2, 2))
                            u.free((3, 2))
                        up(J, 0, 0)
                        up(J, 1, KT)
                        if J > 1:
                            down(J - 2)
                        if j in (3, 5, 7, 9):
                            turn_tile(phase, b, 4 * s + (j - 3) // 2)
                    down(2 * JT - 2)
                    down(2 * JT - 1)

            Use(pe, "A", 1).read_out((2, 7))
            ffn("F1")
            for bnk in (2, 3):
                Use(pe, "F1", 1).read_out((bnk, 3))

            um = Use(pe, "mid", 0)
            pe.wait_ge(qk_split, 16)
            for i in range(4):
                um.free((i % 2, i // 2))
                product(bank(i % 2), lambda k: pair(qk_hi, qk_lo, k * D + i * P, P),
                        lambda k: pair(qk_hi, qk_lo, (KT + k) * D, D)).then_inc(filled[i % 2], 1)
            pe.wait_ge(vo_split, 8)
            for i in range(4, 8):
                um.free((i % 2, i // 2))
                product(bank(i % 2), lambda k: pair(wvT_hi, wvT_lo, k * D + (i - 4) * P, P),
                        lambda k: pair(wo_hi, wo_lo, k * D, D)).then_inc(filled[i % 2], 1)

            with pe.Fori(0, BATCHES) as b:
                u = Use(pe, "B", b)

                def values(i):
                    job = i if i < 4 else 4 + i
                    u.free((job % 2, job // 2))
                    for k in range(KT):
                        if i == 0 and k > 1:
                            um.read_out((k % 2, 3))
                        xh, xl = xt(k, i * P, P)
                        mm(bank(job % 2), xh, cols(wvo_hi, k), k == 0, False)
                        mm(bank(job % 2), xh, cols(wvo_lo, k), False, False)
                        last = mm(bank(job % 2), xl, cols(wvo_hi, k), False, k == KT - 1)
                    last.then_inc(filled[job % 2], 1)

                def queries(s):
                    for m in range(4):
                        job = (4 if s == 0 else 12) + m
                        u.free((job % 2, job // 2))
                        product(bank(job % 2), lambda k: pair(g_hi, g_lo, k * D + m * P, P),
                                lambda k: xt(k, s * GROUP, GROUP)).then_inc(filled[job % 2], 1)

                def scores(i):
                    if i % 4 == 0:
                        for job in ((6, 7) if i == 0 else (14, 15)):
                            u.read_out((job % 2, job // 2))
                    u.free((4, i))
                    for half in range(2):
                        last = product(bank(4 + half), lambda k: pair(aT_hi, aT_lo, k * GROUP + (i % 4) * P, P),
                                       lambda k: xt(k, half * GROUP, GROUP))
                    last.then_inc(filled[4], 1)

                def turn_probs(i):
                    u.read_out((4, i))
                    u.free((2, i))
                    for t in range(BT):
                        last = nc.tensor.transpose(bank(2, 2)[:, t * P:(t + 1) * P], probs[:, t * P:(t + 1) * P],
                                                   ident[:, :])
                    last.then_inc(filled[2], 1)

                def attend(i, t0=0, t1=BT):
                    if i == 0:
                        for job in (10, 11):
                            u.read_out((job % 2, job // 2))
                    use = (6 + i % 2, 2 + i // 2)
                    if t0 == 0:
                        u.read_out((2, i))
                        u.free(use)
                    ph, pl = pT(i)
                    for t in range(t0, t1):
                        left, vh, vl = slice(t * P, (t + 1) * P), cols(v_hi, t), cols(v_lo, t)
                        mm(bank(use[0]), ph[:, left], vh, t == 0, False)
                        mm(bank(use[0]), ph[:, left], vl, False, False)
                        last = mm(bank(use[0]), pl[:, left], vh, False, t == BT - 1)
                    if t1 == BT:
                        last.then_inc(filled[use[0]], 1)

                u.free((0, 0))
                u.free((1, 0))
                values(0)
                values(1)
                turn_tile("B", b, 0)
                turn_tile("B", b, 1)
                values(2)
                values(3)
                turn_tile("B", b, 2)
                turn_tile("B", b, 3)
                queries(0)
                u.read_out((6, 1))
                u.read_out((7, 1))
                values(4)
                values(5)
                scores(0)
                values(6)
                values(7)
                turn_probs(0)
                for i in range(1, 7):
                    scores(i)
                    if i == 3:
                        queries(1)
                    attend(i - 1)
                    turn_probs(i)
                scores(7)
                turn_tile("B", b, 4)
                turn_tile("B", b, 5)
                attend(6, 0, 4)
                turn_probs(7)
                attend(6, 4, 8)
                turn_tile("B", b, 6)
                turn_tile("B", b, 7)
                attend(7)

            for bnk in (0, 1):
                Use(pe, "B", 1).read_out((bnk, 9))
            ffn("F2")


def kernel(**inputs):
    import numpy as np
    import concourse.bacc as bacc
    from concourse.bass_utils import run_bass_kernel_spmd

    def a(name):
        return np.asarray(inputs["L0_" + name])

    def t(m):
        return np.ascontiguousarray(m.T)

    def col(v):
        return t(v.reshape(-1, P))

    x = a("attn_a_x")
    arrays = {
        "x": np.ascontiguousarray(x.reshape(-1, x.shape[-1])),
        "wq": a("attn_a_Wq"), "wk": a("attn_a_Wk"), "wv": a("attn_a_Wv"),
        "w_ab": np.concatenate([a("attn_a_Walpha"), a("attn_a_Wbeta")], axis=1),
        "b_ab": np.concatenate([a("attn_a_balpha"), a("attn_a_bbeta")]),
        "bq": col(a("attn_a_bq")), "bk": a("attn_a_bk"), "bv": a("attn_a_bv"),
        "wqT": t(a("attn_b_W_q")), "wkT": t(a("attn_b_W_k")), "wvT": t(a("attn_b_W_v")), "wo": a("attn_b_W_o"),
        "gateT": t(a("ffn_wq_gate")), "s_gate": col(a("ffn_s_gate")),
        "upT": t(a("ffn_wq_up")), "s_up": col(a("ffn_s_up")),
        "downT": t(a("ffn_wq_down")), "s_down": a("ffn_s_down"),
    }
    nc = bacc.Bacc("TRN2", target_bir_lowering=False, num_devices=1)
    args = {n: nc.dram_tensor(n, v.shape, mybir.dt.from_np(v.dtype), kind="ExternalInput").ap()
            for n, v in arrays.items()}
    args["out"] = nc.dram_tensor("out", arrays["x"].shape, F32, kind="ExternalOutput").ap()
    hybrid_layer_kernel(nc, **args)
    got = run_bass_kernel_spmd(nc, [arrays], core_ids=[0])
    return np.asarray(got.results[0]["out"]).reshape(x.shape)
```

```python
import concourse.bass as bass
from concourse import mybir

F32 = mybir.dt.float32
F32R = mybir.dt.float32r
BF16 = mybir.dt.bfloat16
I32 = mybir.dt.int32
ALU = mybir.AluOpType
ACT = mybir.ActivationFunctionType
AX = mybir.AxisListType

P = 128
BATCHES = 2
TOKENS = 2048
D = 512
KT = D // P
HEADS = D // P
AB = 2 * HEADS
HID = 1408
JT = HID // P
GT = 4
GROUP = GT * P
BT = 2 * GT
BTOK = BT * P
ZERO_POINT = 128.0
LN_EPS = 1e-5
NORM_FLOOR = 1e-12
SCALE = float(D) ** -0.5
MASKED = -30000.0
GU_STEPS = ((0, 1), (0, 2), (0, 3), (1, 1))
RING = 2

BODIES = [("start", 1, {2: 1, 3: 1, 4: 1, 5: 1}),
          ("A", 2, {0: 13, 1: 13, 2: 8, 3: 12, 4: 8, 5: 15, 6: 7, 7: 8}),
          ("F1", 2, {0: 22, 1: 22, 2: 4, 3: 4, 4: 2, 5: 2, 6: 2, 7: 2}),
          ("mid", 1, {0: 4, 1: 4}),
          ("B", 2, {0: 9, 1: 9, 2: 8, 4: 9, 5: 1, 6: 6, 7: 6}),
          ("F2", 2, {0: 22, 1: 22, 2: 4, 3: 4, 4: 2, 5: 2, 6: 2, 7: 2})]
LN_BASE = {"start": 0, "A": 4, "F1": 20, "B": 36, "F2": 52}
FFN_BASE = {"F1": 0, "F2": 1}


def fills_before(phase, bank):
    total = 0
    for name, times, uses in BODIES:
        if name == phase:
            return total
        total += times * uses.get(bank, 0)
    raise ValueError(phase)


def turn(phase, bank, b, i):
    per = {name: uses for name, _, uses in BODIES}[phase][bank]
    return b * per + (fills_before(phase, bank) + i + 1)


def hybrid_layer_kernel(nc, x, wq, wk, wv, w_ab, bq, bk, bv, b_ab,
                        wqT, wkT, wvT, wo, gateT, s_gate, upT, s_up, downT, s_down, out):
    base = (nc.sbuf_base + 63) // 64 * 64

    def at(name, offset, cols, dtype=F32):
        return nc.alloc_sbuf_tensor_at(name, [P, cols], dtype, offset=base + offset)

    xres = at("xres", 0, 16 * D)
    codes_gu = at("codes_gu", 32768, 8 * HID, I32)
    w_gu = at("w_gu", 32768, 8 * HID, F32R)
    xt_hi = at("xt_hi", 77824, KT * BTOK, F32R)
    xt_lo = at("xt_lo", 94208, KT * BTOK, F32R)
    R1, W2, CONST = 110592, 143360, 204800
    ident = at("ident", CONST, P)
    sd_rows = at("sd_rows", CONST + 512, D)
    ab_row = at("ab_row", CONST + 512, GROUP)
    xn = at("xn", CONST + 2560, 2 * D)
    sg_col = at("sg_col", CONST + 6656, JT)
    su_col = at("su_col", CONST + 6720, JT)
    ln_bn = at("ln_bn", CONST + 6784, 4 * 6)
    ln_mv = at("ln_mv", CONST + 6912, 4 * 2)
    ln_var = at("ln_var", CONST + 6944, 4)
    ln_rstd = at("ln_rstd", CONST + 6976, 4)
    minus_half = at("minus_half", CONST + 7008, 4)
    smax = at("smax", CONST + 7040, 2)
    nmax = at("nmax", CONST + 7072, 2)
    rowsum = at("rowsum", CONST + 7104, 2)
    rden = at("rden", CONST + 7136, 2)

    wqk_hi = at("wqk_hi", R1, 2 * KT * D, F32R)
    wqk_raw = at("wqk_raw", R1 + 16384, 2 * KT * D)
    wqk_lo = at("wqk_lo", R1 + 16384, 2 * KT * D, F32R)
    wv_hi = at("wv_hi", W2, KT * D, F32R)
    wv_raw = at("wv_raw", W2 + 8192, KT * D)
    wv_lo = at("wv_lo", W2 + 8192, KT * D, F32R)
    bk_rows = at("bk_rows", W2 + 16384, D)
    bv_rows = at("bv_rows", W2 + 18432, D)
    qT = at("qT", W2 + 20480, HEADS * GROUP)
    kn = at("kn", W2 + 28672, 2 * D)
    kT = at("kT", W2 + 32768, D)
    vn = at("vn", W2 + 34816, 2 * D)
    decay = at("decay", W2 + 38912, D)
    attnT = at("attnT", W2 + 40960, D)
    kw = at("kw", W2 + 43008, D)
    steps_hi = at("steps_hi", W2 + 45056, D, F32R)
    steps_lo = at("steps_lo", W2 + 47104, D, F32R)
    state = at("state", W2 + 49152, D)
    g_z = at("g_z", W2 + 51200, 32)
    g_zz = at("g_zz", W2 + 51328, 32)
    g_e = at("g_e", W2 + 51456, 32)
    g_u = at("g_u", W2 + 51584, 32)
    g_r = at("g_r", W2 + 51712, 32)
    g_a = at("g_a", W2 + 51840, 16)
    g_la = at("g_la", W2 + 51904, 16)
    g_lb = at("g_lb", W2 + 51968, 16)
    g_c = at("g_c", W2 + 52032, 16)
    g_c2 = at("g_c2", W2 + 52096, 16)
    g_zm = at("g_zm", W2 + 52160, 16)
    beta = at("beta", W2 + 52224, 32)
    la_hi = at("la_hi", W2 + 52352, 32, F32R)
    la_lo = at("la_lo", W2 + 52480, 32, F32R)
    decays = at("decays", W2 + 52736, 64)
    sumsq = at("sumsq", W2 + 52992, 8)
    kscale = at("kscale", W2 + 53024, 8)
    ab_bias = at("ab_bias", W2 + 53056, 8)
    bq_col = at("bq_col", W2 + 53088, 4)
    squares = at("squares", W2 + 53248, P)
    tri = at("tri", W2 + 53760, P)
    tri_r = at("tri_r", W2 + 54272, P, F32R)
    ones = at("ones", W2 + 54784, P)
    after_r = at("after_r", W2 + 55296, P, F32R)
    ident_b = at("ident_b", W2 + 55808, P, BF16)
    mask_b = at("mask_b", W2 + 56064, D, BF16)
    wab = at("wab", W2 + 57088, KT * P, F32R)
    wab_raw = at("wab_raw", W2 + 59136, KT * P)

    codes_d = {"F1": at("codes_d1", R1, JT * D, I32), "F2": at("codes_d2", W2 + 16384, JT * D, I32)}
    w_d = {"F1": at("w_d1", R1, JT * D, F32R), "F2": at("w_d2", W2 + 16384, JT * D, F32R)}
    silu = at("silu", W2 + 40960, 2 * GROUP)
    hid = at("hid", W2 + 45056, 2 * GROUP)
    hid_hi = {"F1": at("hid_hi1", W2 + 32768, 4 * GROUP, F32R), "F2": at("hid_hi2", W2, 4 * GROUP, F32R)}
    hid_lo = at("hid_lo", W2 + 49152, 4 * GROUP, F32R)
    yt = at("yt", W2 + 57344, 2 * D)

    qk_hi = at("qk_hi", W2, 2 * KT * D, F32R)
    qk_raw = at("qk_raw", W2 + 16384, 2 * KT * D)
    qk_lo = at("qk_lo", W2 + 16384, 2 * KT * D, F32R)
    wvT_raw = at("wvT_raw", R1, KT * D)
    wvT_lo = at("wvT_lo", R1, KT * D, F32R)
    wvT_hi = at("wvT_hi", R1 + 8192, KT * D, F32R)
    wo_hi = at("wo_hi", R1 + 16384, KT * D, F32R)
    wo_raw = at("wo_raw", R1 + 24576, KT * D)
    wo_lo = at("wo_lo", R1 + 24576, KT * D, F32R)
    g_hi = at("g_hi", W2 + 32768, KT * D, F32R)
    g_lo = at("g_lo", W2 + 40960, KT * D, F32R)
    aT_hi = at("aT_hi", W2, KT * GROUP, F32R)
    aT_lo = at("aT_lo", W2 + 8192, KT * GROUP, F32R)
    wvo_hi = at("wvo_hi", W2 + 16384, KT * D, F32R)
    wvo_lo = at("wvo_lo", W2 + 24576, KT * D, F32R)
    v_hi = at("v_hi", R1, BT * D, F32R)
    v_lo = at("v_lo", R1 + 16384, BT * D, F32R)
    probs = at("probs", W2 + 49152, BTOK)
    pT_hi = at("pT_hi", W2 + 53248, BTOK, F32R)
    pT_lo = at("pT_lo", W2 + 57344, BTOK, F32R)

    psum = nc.alloc_psum_tensor("psum", [P, 8 * 512], F32)

    def bank(i, n=1):
        return psum[:, i * 512:(i + n) * 512]

    def sem(name):
        return nc.alloc_semaphore(name)

    filled = [sem(f"psum_filled{i}") for i in range(8)]
    drained = [sem(f"psum_drained{i}") for i in range(8)]
    x_in = [sem(f"x_in{t}") for t in range(GT)]
    x_rest_in = sem("x_rest_in")
    wab_zero = sem("wab_zero")
    wab_in = sem("wab_in")
    wk_in = sem("wk_in")
    wv_in = sem("wv_in")
    wq_in = sem("wq_in")
    rows_in = sem("rows_in")
    cols_in = sem("cols_in")
    gu_in = sem("gu_in")
    qk_in = sem("qk_in")
    wvT_in = sem("wvT_in")
    wo_in = sem("wo_in")
    d_in = {"F1": sem("d1_in"), "F2": sem("d2_in")}
    d1_mid_in = sem("d1_mid_in")
    sd_in = sem("sd_in")
    x_out = sem("x_out")
    consts_set = sem("consts_set")
    consts_done = sem("consts_done")
    wa_hi = sem("wa_hi")
    wq_hi_done = sem("wq_hi_done")
    wab_lo_done = sem("wab_lo_done")
    wk_lo_done = sem("wk_lo_done")
    wv_lo_done = sem("wv_lo_done")
    wq_lo_done = sem("wq_lo_done")
    ln_bn_done = sem("ln_bn_done")
    ln_mv_done = sem("ln_mv_done")
    ln_var_done = sem("ln_var_done")
    ln_rstd_done = sem("ln_rstd_done")
    ln_xn_done = sem("ln_xn_done")
    xt_hi_done = sem("xt_hi_done")
    z_half = sem("z_half")
    gate_dve = sem("gate_dve")
    gate_act = sem("gate_act")
    squares_done = sem("squares_done")
    squares_step = sem("squares_step")
    kscale_step = sem("kscale_step")
    k_scaled = sem("k_scaled")
    decay_masked = sem("decay_masked")
    kw_ready = sem("kw_ready")
    steps_hi_ready = sem("steps_hi_ready")
    steps_lo_ready = sem("steps_lo_ready")
    gu_ready = sem("gu_ready")
    wd_ready = {"F1": sem("wd1_ready"), "F2": sem("wd2_ready")}
    hid_hi_ready = sem("hid_hi_ready")
    hid_split = sem("hid_split")
    down_done = sem("down_done")
    x_updated = (sem("x_updated_even"), sem("x_updated_odd"))
    qk_split = sem("qk_split")
    vo_hi_done = sem("vo_hi_done")
    vo_split = sem("vo_split")
    hi_done = sem("hi_done")
    pT_hi_done = sem("pT_hi_done")
    smax_done = sem("smax_done")
    nmax_done = sem("nmax_done")
    rden_done = sem("rden_done")

    def a_job(s, i):
        n = 13 * s + i
        return n % 2, n // 2

    def k_job(s, c):
        return a_job(s, 1 if c == 0 else 5 + 2 * c)

    def v_job(s, c):
        return a_job(s, 2 if c == 0 else 6 + 2 * c)

    PREP = {"start": lambda l: (2 + l, 0), "A": lambda l: (2, l), "F1": lambda l: (2 + l % 2, l // 2),
            "F2": lambda l: (2 + l % 2, l // 2),
            "B": lambda l: (6 + l % 2, l // 2) if l < 4 else ((0, 8), (1, 8), (4, 8), (5, 0))[l - 4]}

    def prep_use(phase, l):
        return PREP[phase](l)

    def prep_x(phase, b, l):
        if phase == "start":
            return xres[:, l * D:(l + 1) * D]
        if l < 4:
            return xres[:, bass.ds(b * (BT * D) + (4 + l) * D, D)]
        return xres[:, bass.ds(other_batch[0] + (l - 4) * D, D)]

    def prep_col(phase, l):
        return l * P if phase == "start" else ((l + 4) % 8) * P

    def xt_tile(t, col):
        return t[:, :].rearrange("p (k n) -> p k n", k=KT)[:, :, col:col + P]

    def updates(phase, b, s):
        return b * 4 + (8 * FFN_BASE[phase] + 2 * s + 1)

    def ln_n(phase, b, l):
        return b * 8 + (LN_BASE[phase] + l)

    waits_alone = sem("waits_alone")

    def alone(eng):
        eng.sem_inc(waits_alone, 1)

    def pT(i):
        return (aT_hi[:, 0:BTOK], aT_lo[:, 0:BTOK]) if i == BT - 1 else (pT_hi[:, :], pT_lo[:, :])

    def steps_of(engine, dst, src, s, c):
        return engine.tensor_tensor(dst[:, :].rearrange("p (h d) -> p h d", h=HEADS),
                                    src[:, 16 * s + 4 * c:16 * s + 4 * c + 4].bitcast(F32).unsqueeze(2)
                                    .broadcast_to([P, HEADS, P]),
                                    tri_r[:, :].bitcast(F32).unsqueeze(1).broadcast_to([P, HEADS, P]), ALU.mult)

    other_batch = [None]

    class Use:

        def __init__(self, eng, phase, b):
            self.eng, self.phase, self.b = eng, phase, b

        def value(self, use):
            return turn(self.phase, use[0], self.b, use[1])

        def free(self, use):
            self.eng.wait_ge(drained[use[0]], self.value(use))

        def full(self, use):
            self.eng.wait_ge(filled[use[0]], self.value(use))

        def read_out(self, use):
            self.eng.wait_ge(drained[use[0]], self.value(use) + 1)

    block = nc.Block()

    def cols(t, i, n=D):
        return t[:, i * n:(i + 1) * n]

    with block as blk:
        @blk.sync
        def _(sp):
            for i in range(8):
                sp.sem_inc(drained[i], 1)
            sp.sem_inc(hid_split, RING)
            for s in x_updated:
                sp.sem_inc(s, 1)
            xv = x.rearrange("(g t p) d -> g p t d", p=P, t=GT)
            xs = [xres[:, g * GT * D:(g + 1) * GT * D].rearrange("p (t d) -> p t d", d=D) for g in range(4)]

            def weights(dst, src, s):
                sp.dma_start(dst.rearrange("p (k n) -> p k n", k=src.shape[0] // P),
                             src.rearrange("(k p) n -> p k n", p=P)).then_inc(s, 16)

            for t in range(GT):
                sp.dma_start(xres[:, t * D:(t + 1) * D], x[t * P:(t + 1) * P, :]).then_inc(x_in[t], 16)
            sp.wait_ge(wab_zero, 1)
            raw = wab_raw[:, :].rearrange("p (k n) -> p k n", k=KT)
            sp.dma_start(raw[:, :, 0:2 * AB], w_ab.rearrange("(k p) n -> p k n", p=P)).then_inc(wab_in, 16)
            weights(wqk_raw[:, KT * D:2 * KT * D], wk, wk_in)
            weights(wv_raw[:, :], wv, wv_in)
            weights(wqk_raw[:, 0:KT * D], wq, wq_in)
            sp.dma_start(bk_rows[:, :], bk.partition_broadcast(P)).then_inc(rows_in, 16)
            sp.dma_start(bv_rows[:, :], bv.partition_broadcast(P)).then_inc(rows_in, 16)
            sp.dma_start(ab_bias[:, :], b_ab.partition_broadcast(P)).then_inc(rows_in, 16)
            sp.dma_start(bq_col[:, :], bq).then_inc(rows_in, 16)
            for g in range(1, 4):
                sp.dma_start(xs[g], xv[g]).then_inc(x_rest_in, 16)
            sp.dma_start(sg_col[:, :], s_gate).then_inc(cols_in, 16)
            sp.dma_start(su_col[:, :], s_up).then_inc(cols_in, 16)
            weights(codes_gu[:, 0:4 * HID], gateT, gu_in)
            weights(codes_gu[:, 4 * HID:8 * HID], upT, gu_in)
            use = Use(sp, "A", 1)
            for h in (2, 3):
                use.full(a_job(1, 3 + h))
            weights(codes_d["F1"][:, 0:4 * D], downT[0:4 * P, :], d_in["F1"])
            weights(codes_d["F1"][:, 8 * D:JT * D], downT[8 * P:JT * P, :], d_in["F1"])
            use.full(k_job(1, 3))
            weights(codes_d["F1"][:, 4 * D:8 * D], downT[4 * P:8 * P, :], d1_mid_in)
            weights(wo_raw[:, :], wo, wo_in)
            use.read_out((7, 7))
            sp.dma_start(sd_rows[:, :], s_down.partition_broadcast(P)).then_inc(sd_in, 16)
            weights(qk_raw[:, 0:KT * D], wqT, qk_in)
            weights(qk_raw[:, KT * D:2 * KT * D], wkT, qk_in)
            sp.wait_ge(down_done, 20 + 10 + KT)
            weights(wvT_raw[:, :], wvT, wvT_in)
            use = Use(sp, "B", 1)
            use.full((0, 7))
            use.full((1, 7))
            weights(codes_d["F2"][:, :], downT, d_in["F2"])
            for t in range(4 * GT):
                sp.wait_ge(x_updated[t % 2], 1 + 8 + t // 2 + 1)
                sp.dma_start(out[t * P:(t + 1) * P, :], xres[:, t * D:(t + 1) * D]).then_inc(x_out, 16)
            sp.wait_ge(x_out, 4 * GT * 16)

        @blk.gpsimd
        def _(pool):
            def rstd(n, slot):
                pool.wait_ge(ln_var_done, n + 1)
                nc.gpsimd.tensor_tensor(ln_rstd[:, slot:slot + 1], ln_var[:, slot:slot + 1],
                                        minus_half[:, 0:1], ALU.pow).then_inc(ln_rstd_done, 1)

            nc.gpsimd.memset(wab_raw[:, :], 0.0).then_inc(wab_zero, 1)
            nc.gpsimd.memset(minus_half[:, :], -0.5).then_inc(consts_set, 1)
            nc.gpsimd.memset(ident[:, :], 0.0).then_inc(consts_set, 1)
            nc.gpsimd.memset(ident_b[:, :], 0.0).then_inc(consts_set, 1)
            nc.gpsimd.memset(tri[:, :], 1.0).then_inc(consts_set, 1)
            nc.gpsimd.memset(ones[:, :], 1.0).then_inc(consts_set, 1)
            nc.gpsimd.memset(mask_b[:, :], 0.0).then_inc(consts_set, 1)
            pool.wait_ge(consts_set, 6)
            for m in (ident, ident_b):
                nc.gpsimd.affine_select(out=m[:, :], in_=m[:, :], compare_op=ALU.not_equal, fill=1.0,
                                        base=0, pattern=[[-1, P]], channel_multiplier=1).then_inc(consts_done, 1)
            nc.gpsimd.affine_select(out=tri[:, :], in_=tri[:, :], compare_op=ALU.is_ge, fill=0.0,
                                    base=0, pattern=[[1, P]], channel_multiplier=-1).then_inc(consts_done, 1)
            mv = mask_b[:, :].rearrange("p (h c) -> p h c", h=HEADS)
            nc.gpsimd.affine_select(out=mv, in_=mv, compare_op=ALU.is_ge, fill=MASKED,
                                    base=0, pattern=[[0, HEADS], [1, P]], channel_multiplier=-1).then_inc(consts_done, 1)
            pool.wait_ge(consts_done, 4)
            nc.gpsimd.tensor_copy(tri_r[:, :], tri[:, :]).then_inc(consts_done, 1)
            nc.gpsimd.tensor_scalar(after_r[:, :], tri[:, :], -1.0, 1.0, ALU.mult, ALU.add).then_inc(consts_done, 1)
            for l in (0, 2):
                pool.wait_ge(ln_var_done, l + 2)
                nc.gpsimd.tensor_tensor(ln_rstd[:, l:l + 2], ln_var[:, l:l + 2], minus_half[:, 0:2],
                                        ALU.pow).then_inc(ln_rstd_done, 2)
            pool.wait_ge(wa_hi, 1)
            low, raw = (w[:, :].rearrange("p (k n) -> p k n", k=KT)[:, :, AB:2 * AB] for w in (wab, wab_raw))
            nc.gpsimd.tensor_tensor(low, raw, low.bitcast(F32), ALU.subtract).then_inc(wab_lo_done, 1)
            for w0, ks, hi0, done in ((KT, range(KT - 1), 2, wk_lo_done), (0, range(2, KT), 2 * KT, wq_lo_done)):
                for k in ks:
                    pool.wait_ge(wa_hi, hi0 + k)
                    nc.gpsimd.tensor_tensor(cols(wqk_lo, w0 + k), cols(wqk_raw, w0 + k),
                                            cols(wqk_hi, w0 + k).bitcast(F32), ALU.subtract).then_inc(done, 1)

            with pool.Fori(0, BATCHES) as b:
                def scale_k(s, c):
                    n = b * 8 + (4 * s + c)
                    r = 4 * (c % 2)
                    pool.wait_ge(squares_done, n + 1)
                    alone(pool)
                    nc.gpsimd.tensor_scalar(kscale[:, r:r + 4], sumsq[:, r:r + 4], NORM_FLOOR ** 2, None,
                                            ALU.max).then_inc(kscale_step, 1)
                    pool.wait_ge(kscale_step, n * 3 + 1)
                    nc.gpsimd.tensor_tensor(kscale[:, r:r + 4], kscale[:, r:r + 4], minus_half[:, :],
                                            ALU.pow).then_inc(kscale_step, 1)
                    pool.wait_ge(kscale_step, n * 3 + 2)
                    if c == 0:
                        pool.wait_ge(gate_dve, b * 20 + (10 * s + 8))
                    nc.gpsimd.tensor_tensor(kscale[:, r:r + 4], kscale[:, r:r + 4],
                                            beta[:, 16 * s + 4 * c:16 * s + 4 * c + 4],
                                            ALU.mult).then_inc(kscale_step, 1)
                    pool.wait_ge(kscale_step, n * 3 + 3)
                    kv = cols(kn, c % 2).rearrange("p (h d) -> p h d", h=HEADS)
                    nc.gpsimd.tensor_tensor(kv, kv, kscale[:, r:r + 4].unsqueeze(2).broadcast_to([P, HEADS, P]),
                                            ALU.mult).then_inc(k_scaled, 1)

                def log_steps(s, c):
                    if c == 0:
                        pool.wait_ge(gate_dve, b * 20 + (10 * s + 10))
                    steps_of(nc.gpsimd, steps_hi, la_hi, s, c).then_inc(steps_hi_ready, 1)

                def mask_decay(s, c):
                    u = Use(pool, "A", b)
                    u.read_out((4, 4 * s + c))
                    alone(pool)
                    dv = decay[:, :].rearrange("p (h d) -> p h d", h=HEADS)
                    nc.gpsimd.affine_select(out=dv, in_=dv, compare_op=ALU.is_ge, fill=0.0, base=0,
                                            pattern=[[0, HEADS], [1, P]], channel_multiplier=-1
                                            ).then_inc(decay_masked, 1)

                def weight_k(s, c):
                    pool.wait_ge(decay_masked, b * 7 + (4 * s + c + 1))
                    kv = cols(kn, c % 2).rearrange("p (h d) -> p h d", h=HEADS)
                    dv = decay[:, :].rearrange("p (h d) -> p h d", h=HEADS)[:, :, P - 1:P]
                    nc.gpsimd.tensor_tensor(kw[:, :].rearrange("p (h d) -> p h d", h=HEADS), kv,
                                            dv.broadcast_to([P, HEADS, P]), ALU.mult).then_inc(kw_ready, 1)

                for s in range(2):
                    if s == 0:
                        scale_k(0, 0)
                        log_steps(0, 0)
                    for c in range(4):
                        if c == 0:
                            for l in range(4 * s, 4 * s + 4):
                                rstd(ln_n("A", b, l), l % 4)
                        if (s, c) != (1, 3):
                            mask_decay(s, c)
                            weight_k(s, c)
                        if c < 3:
                            scale_k(s, c + 1)
                            log_steps(s, c + 1)
                        elif s == 0:
                            scale_k(1, 0)
                            log_steps(1, 0)

            def ffn(phase):
                pool.wait_ge(d_in[phase], 32 if phase == "F1" else 16)
                for j in range(8 if phase == "F1" else 0, JT):
                    nc.gpsimd.tensor_scalar(cols(w_d[phase], j), cols(codes_d[phase], j),
                                            -ZERO_POINT, None, ALU.add).then_inc(wd_ready[phase], 1)
                with pool.Fori(0, BATCHES) as b:
                    def add_y(s, t):
                        u = Use(pool, phase, b)
                        u.read_out((4 + t, s))
                        xs = xres[:, bass.ds(b * (BT * D) + (4 * s + t) * D, D)]
                        nc.gpsimd.tensor_tensor(xs, xs, cols(yt, t % 2), ALU.add).then_inc(x_updated[0], 1)

                    for J in range(2 * JT):
                        s, j = J // JT, J % JT
                        n = b * 22 + (44 * FFN_BASE[phase] + J)
                        pool.wait_ge(hid_hi_ready, n + 1)
                        nc.gpsimd.tensor_tensor(cols(hid_lo, J % 4), cols(hid, J % 2),
                                                cols(hid_hi[phase], J % 4).bitcast(F32),
                                                ALU.subtract).then_inc(hid_split, 1)
                        if J == JT + 1:
                            add_y(0, 0)
                            add_y(0, 2)
                        if j in (1, 3, 5, 7):
                            l = 4 * s + j // 2
                            rstd(ln_n(phase, b, l), l % 4)
                        if phase == "F1" and j in (6, 8):
                            i = 2 * s + (j - 6) // 2
                            m = b * 4 + i
                            if i == 0:
                                pool.wait_ge(qk_in, 32)
                            piece = bass.ds(b * (KT * D) + i * D, D)
                            nc.gpsimd.tensor_copy(qk_hi[:, piece], qk_raw[:, piece]).then_inc(qk_split, 1)
                            pool.wait_ge(qk_split, m * 2 + 1)
                            alone(pool)
                            nc.gpsimd.tensor_tensor(qk_lo[:, piece], qk_raw[:, piece],
                                                    qk_hi[:, piece].bitcast(F32),
                                                    ALU.subtract).then_inc(qk_split, 1)
                    add_y(1, 0)
                    add_y(1, 2)

            ffn("F1")
            with pool.Fori(0, BATCHES) as b:
                for l in range(8):
                    rstd(ln_n("B", b, l), l % 4)
            ffn("F2")

        @blk.scalar
        def _(act):
            def split_hi(phase, b, l):
                use = prep_use(phase, l)
                Use(act, phase, b).full(use)
                nc.scalar.activation(xt_tile(xt_hi, prep_col(phase, l)),
                                     bank(use[0]).rearrange("p (k n) -> p k n", k=KT),
                                     ACT.Copy).then_inc(xt_hi_done, 1)

            nc.scalar.preload_act_table_set("natural_log_exp_and_others")
            act.wait_ge(wab_in, 16)
            nc.scalar.activation(wab[:, :], wab_raw[:, :], ACT.Copy).then_inc(wa_hi, 1)

            def weight_hi(w_in, hi, raw, i):
                act.wait_ge(w_in, 16)
                nc.scalar.activation(cols(hi, i), cols(raw, i), ACT.Copy).then_inc(wa_hi, 1)

            split_hi("start", 0, 0)
            split_hi("start", 0, 1)
            weight_hi(wk_in, wqk_hi, wqk_raw, KT)
            split_hi("start", 0, 2)
            split_hi("start", 0, 3)
            weight_hi(wk_in, wqk_hi, wqk_raw, KT + 1)
            weight_hi(wk_in, wqk_hi, wqk_raw, KT + 2)
            weight_hi(wk_in, wqk_hi, wqk_raw, KT + 3)
            for k in range(KT):
                weight_hi(wv_in, wv_hi, wv_raw, k)
            for k in range(2, KT):
                weight_hi(wq_in, wqk_hi, wqk_raw, k)
            act.wait_ge(rows_in, 4 * 16)

            with act.Fori(0, BATCHES) as b:
                u = Use(act, "A", b)

                def logits_row(s):
                    use = a_job(s, 0)
                    u.full(use)
                    nc.scalar.activation(ab_row[0:2 * AB, :], bank(use[0])[0:2 * AB, :], ACT.Copy).then_inc(drained[use[0]], 1)

                def norms(s, c):
                    u.read_out(k_job(s, c))
                    r = 4 * (c % 2)
                    for h in range(HEADS):
                        last = nc.scalar.activation(squares[:, :], kn[:, (c % 2) * D + h * P:(c % 2) * D + (h + 1) * P],
                                                    ACT.Square, accum_out=sumsq[:, r + h:r + h + 1])
                        last.then_inc(squares_done if h == HEADS - 1 else squares_step, 1)
                        if h < HEADS - 1:
                            act.wait_ge(squares_step, (b * 8 + (4 * s + c)) * 3 + (h + 1))

                def gate_exp(s):
                    act.wait_ge(gate_dve, b * 20 + (10 * s + 1))
                    nc.scalar.activation(g_e[:, :], g_zz[:, :], ACT.Exp, scale=-1.0).then_inc(gate_act, 1)

                def gate_logs(s):
                    act.wait_ge(gate_dve, b * 20 + (10 * s + 4))
                    nc.scalar.activation(g_la[:, :], g_a[:, :], ACT.Ln).then_inc(gate_act, 1)
                    nc.scalar.activation(g_lb[:, :], g_u[:, 16:32], ACT.Ln).then_inc(gate_act, 1)

                def q_out(s, h):
                    use = a_job(s, 3 + h)
                    u.full(use)
                    nc.scalar.activation(qT[:, h * GROUP:(h + 1) * GROUP], bank(use[0]), ACT.Identity,
                                         bias=bq_col[:, h:h + 1]).then_inc(drained[use[0]], 1)

                def gate_decays(s):
                    u.full((3, 6 * s + 1))
                    nc.scalar.activation(decays[:, 32 * s:32 * s + 32], bank(3)[:, 0:32], ACT.Exp).then_inc(drained[3], 1)

                def kT_out(s, c):
                    use = (3, 6 * s + 2 + c)
                    u.full(use)
                    nc.scalar.activation(kT[:, :], bank(3), ACT.Copy).then_inc(drained[3], 1)

                def decay_out(s, c):
                    u.full((4, 4 * s + c))
                    nc.scalar.activation(decay[:, :], bank(4), ACT.Exp).then_inc(drained[4], 1)

                def head(s):
                    q_out(s, 0)
                    gate_logs(s)
                    q_out(s, 1)
                    q_out(s, 2)
                    gate_decays(s)
                    q_out(s, 3)

                logits_row(0)
                norms(0, 0)
                gate_exp(0)
                head(0)
                for s in range(2):
                    for c in range(4):
                        kT_out(s, c)
                        decay_out(s, c)
                        if c < 3:
                            norms(s, c + 1)
                        elif s == 0:
                            logits_row(1)
                            norms(1, 0)
                            gate_exp(1)
                        if c < 2:
                            split_hi("A", b, 4 * s + 2 * c)
                        if c < 2 and (s, c) != (1, 1):
                            split_hi("A", b, 4 * s + 2 * c + 1)
                        if (s, c) == (1, 3):
                            split_hi("A", b, 7)
                        if c == 3 and s == 0:
                            head(1)

            def ffn(phase):
                nc.scalar.preload_act_table(ACT.Silu)
                act.wait_ge(cols_in, 32)
                if phase == "F1":
                    act.wait_ge(d_in[phase], 32)
                    for j in range(4):
                        nc.scalar.activation(cols(w_d[phase], j), cols(codes_d[phase], j), ACT.Copy,
                                             bias=-ZERO_POINT).then_inc(wd_ready[phase], 1)
                with act.Fori(0, BATCHES) as b:
                    u = Use(act, phase, b)
                    for J in range(2 * JT):
                        s, j = J // JT, J % JT
                        u.full((0, J))
                        act.wait_ge(drained[1], u.value((1, J)) - 1)
                        nc.scalar.activation(cols(silu, J % 2), bank(0), ACT.Silu,
                                             scale=sg_col[:, j:j + 1]).then_inc(drained[0], 1)
                        u.read_out((1, J))
                        if J >= 4 and (J - 4) % JT < JT - 1:
                            act.wait_ge(down_done, b * 20 + (40 * FFN_BASE[phase] + (J - 4) // JT * 10
                                                             + (J - 4) % JT + 1))
                        elif J >= 4:
                            u.full((7, (J - 4) // JT))
                        nc.scalar.activation(cols(hid_hi[phase], J % 4), cols(hid, J % 2),
                                             ACT.Copy).then_inc(hid_hi_ready, 1)
                        if j in (3, 5, 7, 9):
                            split_hi(phase, b, 4 * s + (j - 3) // 2)

            ffn("F1")

            nc.scalar.preload_act_table(ACT.Exp)
            act.wait_ge(wo_in, 16)
            act.wait_ge(wvT_in, 16)
            Use(act, "F1", 1).full((7, 1))
            um = Use(act, "mid", 0)
            for i in range(8):
                if i < 4:
                    nc.scalar.activation(cols(wvT_hi, i), cols(wvT_raw, i), ACT.Copy).then_inc(vo_hi_done, 1)
                    nc.scalar.activation(cols(wo_hi, i), cols(wo_raw, i), ACT.Copy).then_inc(vo_hi_done, 1)
                um.full((i % 2, i // 2))
                nc.scalar.activation(cols(g_hi if i < 4 else wvo_hi, i % 4), bank(i % 2), ACT.Copy).then_inc(hi_done, 1)

            with act.Fori(0, BATCHES) as b:
                u = Use(act, "B", b)

                def high(dst, job):
                    u.full((job % 2, job // 2))
                    nc.scalar.activation(dst, bank(job % 2), ACT.Copy).then_inc(hi_done, 1)

                def softmax(i):
                    u.full((4, i))
                    act.wait_ge(nmax_done, b * 8 + (i + 1))
                    nc.scalar.activation(probs[:, :], bank(4, 2), ACT.Exp, scale=SCALE,
                                         bias=nmax[:, i % 2:i % 2 + 1],
                                         accum_out=rowsum[:, i % 2:i % 2 + 1]).then_inc(drained[4], 1)

                def pT_high(i):
                    u.full((2, i))
                    nc.scalar.activation(pT(i)[0], bank(2, 2), ACT.Copy).then_inc(pT_hi_done, 1)

                high(cols(v_hi, 0), 0)
                high(cols(v_hi, 1), 1)
                split_hi("B", b, 0)
                split_hi("B", b, 1)
                high(cols(v_hi, 2), 2)
                high(cols(v_hi, 3), 3)
                split_hi("B", b, 2)
                split_hi("B", b, 3)
                for i in range(4):
                    high(cols(aT_hi, i), 4 + i)
                high(cols(v_hi, 4), 8)
                high(cols(v_hi, 5), 9)
                softmax(0)
                high(cols(v_hi, 6), 10)
                high(cols(v_hi, 7), 11)
                pT_high(0)
                for i in range(1, 8):
                    softmax(i)
                    if i == 3:
                        for m in range(4):
                            high(cols(aT_hi, m), 12 + m)
                    if i == 7:
                        split_hi("B", b, 4)
                        split_hi("B", b, 5)
                    pT_high(i)
                split_hi("B", b, 6)
                split_hi("B", b, 7)

            ffn("F2")

        @blk.vector
        def _(dve):
            def stats(phase, b, l):
                n, r = ln_n(phase, b, l), l % 4
                nc.vector.bn_stats(ln_bn[:, 6 * r:6 * r + 6], prep_x(phase, b, l)).then_inc(ln_bn_done, 1)
                dve.wait_ge(ln_bn_done, n + 1)
                alone(dve)
                nc.vector.bn_aggr(ln_mv[:, 2 * r:2 * r + 2], ln_bn[:, 6 * r:6 * r + 6]).then_inc(ln_mv_done, 1)
                dve.wait_ge(ln_mv_done, n + 1)
                nc.vector.tensor_scalar(ln_var[:, r:r + 1], ln_mv[:, 2 * r + 1:2 * r + 2], LN_EPS, None,
                                        ALU.add).then_inc(ln_var_done, 1)

            def normalise(phase, b, l):
                n, r = ln_n(phase, b, l), l % 4
                dve.wait_ge(ln_rstd_done, n + 1)
                nc.vector.tensor_scalar(cols(xn, l % 2), prep_x(phase, b, l), ln_mv[:, 2 * r:2 * r + 1],
                                        ln_rstd[:, r:r + 1], ALU.subtract, ALU.mult).then_inc(ln_xn_done, 1)

            def split_lo(phase, b, l):
                use = prep_use(phase, l)
                dve.wait_ge(xt_hi_done, ln_n(phase, b, l) + 1)
                nc.vector.tensor_tensor(xt_tile(xt_lo, prep_col(phase, l)),
                                        bank(use[0]).rearrange("p (k n) -> p k n", k=KT),
                                        xt_tile(xt_hi, prep_col(phase, l)).bitcast(F32),
                                        ALU.subtract).then_inc(drained[use[0]], 1)

            def stats_pair(l):
                for r in (l, l + 1):
                    dve.wait_ge(x_in[r], 16)
                    nc.vector.bn_stats(ln_bn[:, 6 * r:6 * r + 6], xres[:, r * D:(r + 1) * D]).then_inc(ln_bn_done, 1)
                for r in (l, l + 1):
                    dve.wait_ge(ln_bn_done, r + 1)
                    nc.vector.bn_aggr(ln_mv[:, 2 * r:2 * r + 2], ln_bn[:, 6 * r:6 * r + 6]).then_inc(ln_mv_done, 1)
                dve.wait_ge(ln_mv_done, l + 2)
                var = ln_mv[:, 2 * l:2 * l + 4].rearrange("p (r two) -> p r two", two=2)[:, :, 1]
                nc.vector.tensor_scalar(ln_var[:, l:l + 2], var, LN_EPS, None, ALU.add).then_inc(ln_var_done, 2)

            stats_pair(0)
            stats_pair(2)
            normalise("start", 0, 0)
            normalise("start", 0, 1)
            for l in (2, 3):
                Use(dve, "start", 0).full((l, 0))
                normalise("start", 0, l)
            for l in range(4):
                split_lo("start", 0, l)
            dve.wait_ge(wa_hi, 1 + KT)
            nc.vector.tensor_tensor(cols(wqk_lo, 2 * KT - 1), cols(wqk_raw, 2 * KT - 1),
                                    cols(wqk_hi, 2 * KT - 1).bitcast(F32), ALU.subtract).then_inc(wk_lo_done, 1)
            for k in range(KT):
                dve.wait_ge(wa_hi, 2 + KT + k)
                nc.vector.tensor_tensor(cols(wv_lo, k), cols(wv_raw, k), cols(wv_hi, k).bitcast(F32),
                                        ALU.subtract).then_inc(wv_lo_done, 1)
            dve.wait_ge(wq_in, 16)
            nc.vector.tensor_copy(wqk_hi[:, 0:2 * D], wqk_raw[:, 0:2 * D]).then_inc(wq_hi_done, 1)
            dve.wait_ge(wq_hi_done, 1)
            for k in range(2):
                nc.vector.tensor_tensor(cols(wqk_lo, k), cols(wqk_raw, k), cols(wqk_hi, k).bitcast(F32),
                                        ALU.subtract).then_inc(wq_lo_done, 1)
            dve.wait_ge(rows_in, 4 * 16)

            with dve.Fori(0, BATCHES) as b:
                row0 = dve.snap(b * (BT * D))
                other_batch[0] = dve.snap(BT * D - row0)
                u = Use(dve, "A", b)
                z3 = g_z[:, :].rearrange("p (c k) -> p c k", c=4)

                def four(ap):
                    return ap.rearrange("p (c h) -> p c h", c=4)

                def k_out(s, c):
                    use = k_job(s, c)
                    u.full(use)
                    nc.vector.tensor_tensor(cols(kn, c % 2), bank(use[0]), bk_rows[:, :],
                                            ALU.add).then_inc(drained[use[0]], 1)

                def v_out(s, c):
                    use = v_job(s, c)
                    u.full(use)
                    nc.vector.tensor_tensor(cols(vn, c % 2), bank(use[0]), bv_rows[:, :],
                                            ALU.add).then_inc(drained[use[0]], 1)

                def gate_a(s):
                    use = (3, 6 * s)
                    u.full(use)
                    parts = bank(3)[:, 0:8 * AB].rearrange("p (c k) -> p c k", c=4)
                    nc.vector.tensor_tensor(z3, parts[:, :, 0:AB], ab_bias[:, :].unsqueeze(1).broadcast_to([P, 4, AB]),
                                            ALU.add).then_inc(z_half, 1)
                    dve.wait_ge(z_half, b * 2 + (s + 1))
                    nc.vector.tensor_tensor(z3, parts[:, :, AB:2 * AB], z3, ALU.add).then_inc(drained[3], 1)
                    u.read_out(use)
                    nc.vector.tensor_scalar(four(g_zz[:, 0:16]), z3[:, :, 0:4], -80.0, None,
                                            ALU.max)
                    nc.vector.scalar_tensor_tensor(out=four(g_zz[:, 16:32]), in0=z3[:, :, 4:8], scalar=-1.0,
                                                   in1=z3[:, :, 4:8], op0=ALU.mult,
                                                   op1=ALU.max).then_inc(gate_dve, 1)

                def gate_b(s):
                    g = b * 20 + 10 * s
                    dve.wait_ge(gate_act, b * 6 + (3 * s + 1))
                    nc.vector.tensor_scalar(g_u[:, :], g_e[:, :], 1.0, None, ALU.add).then_inc(gate_dve, 1)
                    dve.wait_ge(gate_dve, g + 2)
                    nc.vector.reciprocal(g_r[:, :], g_u[:, :]).then_inc(gate_dve, 1)
                    dve.wait_ge(gate_dve, g + 3)
                    nc.vector.tensor_scalar(g_a[:, :], g_r[:, 0:16], 1e-6, None, ALU.add).then_inc(gate_dve, 1)
                    nc.vector.scalar_tensor_tensor(out=g_c[:, :], in0=g_u[:, 16:32], scalar=1.0, in1=g_e[:, 16:32],
                                                   op0=ALU.subtract, op1=ALU.subtract).then_inc(gate_dve, 1)
                    dve.wait_ge(gate_dve, g + 5)
                    nc.vector.tensor_tensor(g_c2[:, :], g_c[:, :], g_r[:, 16:32], ALU.mult).then_inc(gate_dve, 1)
                    dve.wait_ge(gate_dve, g + 6)
                    nc.vector.scalar_tensor_tensor(out=four(g_zm[:, :]), in0=z3[:, :, 4:8], scalar=0.0,
                                                   in1=four(g_c2[:, :]), op0=ALU.max,
                                                   op1=ALU.subtract).then_inc(gate_dve, 1)

                def gate_c(s):
                    g = b * 20 + 10 * s
                    o = slice(16 * s, 16 * s + 16)
                    dve.wait_ge(gate_act, b * 6 + (3 * s + 3))
                    dve.wait_ge(gate_dve, g + 7)
                    nc.vector.tensor_tensor(beta[:, o], g_zm[:, :], g_lb[:, :], ALU.add).then_inc(gate_dve, 1)
                    nc.vector.tensor_copy(la_hi[:, o], g_la[:, :]).then_inc(gate_dve, 1)
                    dve.wait_ge(gate_dve, g + 9)
                    nc.vector.tensor_tensor(la_lo[:, o], g_la[:, :], la_hi[:, o].bitcast(F32),
                                            ALU.subtract).then_inc(gate_dve, 1)

                def log_steps(s, c):
                    if c == 0:
                        dve.wait_ge(gate_dve, b * 20 + (10 * s + 10))
                    steps_of(nc.vector, steps_lo, la_lo, s, c).then_inc(steps_lo_ready, 1)

                def attn_out(s, c):
                    n = 4 * s + c
                    u.full((5, 2 * n))
                    if n < BT - 1:
                        dve.wait_ge(decay_masked, b * 7 + (n + 1))
                    else:
                        u.read_out((4, n))
                    nc.vector.tensor_tensor(attnT[:, :], bank(5), decay[:, :], ALU.mult).then_inc(drained[5], 1)

                def state_out(s, c):
                    n = 4 * s + c
                    u.free((5, 2 * n + 1))
                    u.full((5, 2 * n + 1))
                    if n == 0:
                        nc.vector.tensor_copy(state[:, :], bank(5)).then_inc(drained[5], 1)
                        return
                    for h in range(HEADS):
                        i = 32 * s + 16 + 4 * c + h
                        hs = slice(h * P, (h + 1) * P)
                        last = nc.vector.scalar_tensor_tensor(out=state[:, hs], in0=state[:, hs],
                                                              scalar=decays[:, i:i + 1], in1=bank(5)[:, hs],
                                                              op0=ALU.mult, op1=ALU.add)
                    last.then_inc(drained[5], 1)

                def y_out(s, c):
                    n = 4 * s + c
                    if n > 0:
                        u.full((6, n - 1))
                        for h in range(HEADS):
                            i = 32 * s + 4 * c + h
                            xs = xres[:, bass.ds(row0 + (n * D + h * P), P)]
                            last = nc.vector.scalar_tensor_tensor(out=xs, in0=bank(6)[:, h * P:(h + 1) * P],
                                                                  scalar=decays[:, i:i + 1], in1=xs,
                                                                  op0=ALU.mult, op1=ALU.add)
                        last.then_inc(drained[6], 1)
                        u.read_out((6, n - 1))
                    u.full((7, n))
                    xs = xres[:, bass.ds(row0 + n * D, D)]
                    nc.vector.tensor_tensor(xs, xs, bank(7), ALU.add).then_inc(drained[7], 1)

                k_out(0, 0)
                gate_a(0)
                v_out(0, 0)
                gate_b(0)
                gate_c(0)
                log_steps(0, 0)
                dve.wait_ge(x_rest_in, 48)
                for l in range(4):
                    stats("A", b, l)
                for s in range(2):
                    for c in range(4):
                        l = 4 * s + 2 * c
                        if c == 0:
                            normalise("A", b, l)
                        if c < 2:
                            normalise("A", b, l + 1)
                        if c < 3:
                            k_out(s, c + 1)
                        elif s == 0:
                            k_out(1, 0)
                            gate_a(1)
                        if c < 2:
                            split_lo("A", b, l)
                        attn_out(s, c)
                        if c < 3:
                            v_out(s, c + 1)
                            log_steps(s, c + 1)
                        elif s == 0:
                            v_out(1, 0)
                            gate_b(1)
                        if c < 2 and (s, c) != (1, 1):
                            split_lo("A", b, l + 1)
                        if (s, c) == (1, 3):
                            split_lo("A", b, 7)
                        if c == 0:
                            normalise("A", b, l + 2)
                        if (s, c) != (1, 3):
                            state_out(s, c)
                        y_out(s, c)
                        if (s, c) in GU_STEPS:
                            i = GU_STEPS.index((s, c))
                            if i == 0:
                                dve.wait_ge(gu_in, 32)
                            piece = bass.ds(b * (4 * HID) + i * HID, HID)
                            nc.vector.tensor_scalar(w_gu[:, piece], codes_gu[:, piece], -ZERO_POINT, None,
                                                    ALU.add).then_inc(gu_ready, 1)
                        if c == 3 and s == 0:
                            gate_c(1)
                            log_steps(1, 0)
                            u.read_out((7, 3))
                            alone(dve)
                            for l in range(4, 8):
                                stats("A", b, l)

            def ffn(phase):
                if phase == "F1":
                    dve.wait_ge(d1_mid_in, 16)
                    nc.vector.tensor_scalar(w_d[phase][:, 4 * D:8 * D], codes_d[phase][:, 4 * D:8 * D], -ZERO_POINT,
                                            None, ALU.add).then_inc(wd_ready[phase], 1)
                    Use(dve, "A", 1).read_out((7, 7))
                else:
                    Use(dve, "B", 1).read_out((7, 5))
                    Use(dve, "B", 1).read_out((6, 5))
                dve.wait_ge(cols_in, 32)
                with dve.Fori(0, BATCHES) as b:
                    row0 = dve.snap(b * (BT * D))
                    other_batch[0] = dve.snap(BT * D - row0)
                    u = Use(dve, phase, b)

                    def residual(s):
                        for t in range(4):
                            n = updates(phase, b, s)
                            u.full((4 + t, s))
                            if t == 0 and s == 0:
                                dve.wait_ge(sd_in, 16)
                            dve.wait_ge(x_updated[t % 2], n + t // 2)
                            nc.vector.tensor_tensor(cols(yt, t % 2), bank(4 + t), sd_rows[:, :],
                                                    ALU.mult).then_inc(drained[4 + t], 1)
                            if t % 2 == 1:
                                u.read_out((4 + t, s))
                                xs = xres[:, bass.ds(row0 + (4 * s + t) * D, D)]
                                nc.vector.tensor_tensor(xs, xs, yt[:, D:2 * D], ALU.add).then_inc(x_updated[1], 1)

                    for J in range(2 * JT):
                        s, j = J // JT, J % JT
                        n = b * 22 + (44 * FFN_BASE[phase] + J)
                        u.full((1, J))
                        u.read_out((0, J))
                        dve.wait_ge(hid_split, n + 1)
                        nc.vector.scalar_tensor_tensor(out=cols(hid, J % 2), in0=bank(1), scalar=su_col[:, j:j + 1],
                                                       in1=cols(silu, J % 2), op0=ALU.mult,
                                                       op1=ALU.mult).then_inc(drained[1], 1)
                        if J == JT + 1:
                            residual(0)
                        if j in (3, 5, 7, 9):
                            split_lo(phase, b, 4 * s + (j - 3) // 2)
                        if j in (1, 3, 5, 7):
                            if j == 1 and s == 1:
                                for parity in range(2):
                                    dve.wait_ge(x_updated[parity], updates(phase, b, 0))
                                alone(dve)
                            stats(phase, b, 4 * s + j // 2)
                        if j in (2, 4, 6, 8):
                            normalise(phase, b, 4 * s + j // 2 - 1)
                    residual(1)

            ffn("F1")

            for i in range(8):
                if i < 4:
                    dve.wait_ge(vo_hi_done, 2 * i + 1)
                    nc.vector.tensor_tensor(cols(wvT_lo, i), cols(wvT_raw, i), cols(wvT_hi, i).bitcast(F32),
                                            ALU.subtract).then_inc(vo_split, 1)
                    dve.wait_ge(vo_hi_done, 2 * i + 2)
                    nc.vector.tensor_tensor(cols(wo_lo, i), cols(wo_raw, i), cols(wo_hi, i).bitcast(F32),
                                            ALU.subtract).then_inc(vo_split, 1)
                dve.wait_ge(hi_done, i + 1)
                nc.vector.tensor_tensor(cols(g_lo if i < 4 else wvo_lo, i % 4), bank(i % 2),
                                        cols(g_hi if i < 4 else wvo_hi, i % 4).bitcast(F32),
                                        ALU.subtract).then_inc(drained[i % 2], 1)
            for parity in range(2):
                dve.wait_ge(x_updated[parity], 8 + 1)

            with dve.Fori(0, BATCHES) as b:
                row0 = dve.snap(b * (BT * D))
                other_batch[0] = dve.snap(BT * D - row0)
                u = Use(dve, "B", b)

                def low(dst, hi, job, k):
                    dve.wait_ge(hi_done, b * 16 + (8 + k + 1))
                    nc.vector.tensor_tensor(dst, bank(job % 2), hi.bitcast(F32),
                                            ALU.subtract).then_inc(drained[job % 2], 1)

                def row_max(i):
                    r = slice(i % 2, i % 2 + 1)
                    u.full((4, i))
                    nc.vector.reduce_max(smax[:, r], bank(4, 2), AX.X).then_inc(smax_done, 1)
                    dve.wait_ge(smax_done, b * 8 + (i + 1))
                    nc.vector.tensor_scalar(nmax[:, r], smax[:, r], -SCALE, None, ALU.mult).then_inc(nmax_done, 1)

                def pT_low(i):
                    dve.wait_ge(pT_hi_done, b * 8 + (i + 1))
                    nc.vector.tensor_tensor(pT(i)[1], bank(2, 2), pT(i)[0].bitcast(F32),
                                            ALU.subtract).then_inc(drained[2], 1)

                def out_add(i):
                    r = slice(i % 2, i % 2 + 1)
                    u.read_out((4, i))
                    nc.vector.reciprocal(rden[:, r], rowsum[:, r]).then_inc(rden_done, 1)
                    dve.wait_ge(rden_done, b * 8 + (i + 1))
                    u.full((6 + i % 2, 2 + i // 2))
                    xs = xres[:, bass.ds(row0 + i * D, D)]
                    nc.vector.scalar_tensor_tensor(out=xs, in0=bank(6 + i % 2), scalar=rden[:, r], in1=xs,
                                                   op0=ALU.mult, op1=ALU.add).then_inc(drained[6 + i % 2], 1)

                stats("B", b, 0)
                stats("B", b, 1)
                normalise("B", b, 0)
                normalise("B", b, 1)
                low(cols(v_lo, 0), cols(v_hi, 0), 0, 0)
                stats("B", b, 2)
                stats("B", b, 3)
                low(cols(v_lo, 1), cols(v_hi, 1), 1, 1)
                split_lo("B", b, 0)
                normalise("B", b, 2)
                split_lo("B", b, 1)
                normalise("B", b, 3)
                low(cols(v_lo, 2), cols(v_hi, 2), 2, 2)
                low(cols(v_lo, 3), cols(v_hi, 3), 3, 3)
                split_lo("B", b, 2)
                split_lo("B", b, 3)
                for i in range(4):
                    low(cols(aT_lo, i), cols(aT_hi, i), 4 + i, 4 + i)
                low(cols(v_lo, 4), cols(v_hi, 4), 8, 8)
                low(cols(v_lo, 5), cols(v_hi, 5), 9, 9)
                row_max(0)
                low(cols(v_lo, 6), cols(v_hi, 6), 10, 10)
                low(cols(v_lo, 7), cols(v_hi, 7), 11, 11)
                pT_low(0)
                for i in range(1, 7):
                    row_max(i)
                    if i == 3:
                        for m in range(4):
                            low(cols(aT_lo, m), cols(aT_hi, m), 12 + m, 12 + m)
                    out_add(i - 1)
                    pT_low(i)
                    if i in (4, 5):
                        if i == 4:
                            u.free((6, 0))
                            u.free((7, 0))
                            alone(dve)
                        stats("B", b, 2 * i - 4)
                        stats("B", b, 2 * i - 3)
                    if i == 6:
                        normalise("B", b, 4)
                        normalise("B", b, 5)
                row_max(7)
                split_lo("B", b, 4)
                normalise("B", b, 6)
                split_lo("B", b, 5)
                normalise("B", b, 7)
                pT_low(7)
                out_add(6)
                split_lo("B", b, 6)
                split_lo("B", b, 7)
                out_add(7)

            ffn("F2")

        @blk.tensor
        def _(pe):
            def mm(out, lhsT, rhs, start, stop):
                return nc.tensor.matmul(out, lhsT, rhs, start=start, stop=stop)

            def product(out, left, right, ks=KT):
                for k in range(ks):
                    (lh, ll), (rh, rl) = left(k), right(k)
                    mm(out, lh, rh, k == 0, False)
                    mm(out, lh, rl, False, False)
                    last = mm(out, ll, rh, False, k == ks - 1)
                return last

            def pair(hi, lo, a, n):
                return hi[:, a:a + n], lo[:, a:a + n]

            def turn_tile(phase, b, l):
                use = prep_use(phase, l)
                pe.wait_ge(ln_xn_done, ln_n(phase, b, l) + 1)
                Use(pe, phase, b).free(use)
                for k in range(KT):
                    last = nc.tensor.transpose(bank(use[0])[:, k * P:(k + 1) * P],
                                               xn[:, (l % 2) * D + k * P:(l % 2) * D + (k + 1) * P], ident[:, :])
                last.then_inc(filled[use[0]], 1)

            def xt(k, col, n):
                return pair(xt_hi, xt_lo, k * BTOK + col, n)

            def warm_up(times):
                for _ in range(times):
                    mm(bank(0), ident_b[:, :], mask_b[:, :], True, True)

            pe.wait_ge(consts_done, 4)
            warm_up(10)
            for l in range(4):
                turn_tile("start", 0, l)
            warm_up(6)

            with pe.Fori(0, BATCHES) as b:
                u = Use(pe, "A", b)
                u.free((2, 0))
                for l in range(4):
                    Use(pe, "start", 0).read_out(prep_use("start", l))

                def logits(s):
                    use = a_job(s, 0)
                    pe.wait_ge(wab_lo_done, 1)
                    u.free(use)
                    for k in range(KT):
                        xh, xl = xt(k, s * GROUP, GROUP)
                        mm(bank(use[0]), cols(wab, k, P), xh, k == 0, False)
                        last = mm(bank(use[0]), cols(wab, k, P), xl, False, k == KT - 1)
                    last.then_inc(filled[use[0]], 1)

                def logits_turned(s):
                    u.read_out(a_job(s, 0))
                    u.free((3, 6 * s))
                    alone(pe)
                    for c in range(4):
                        last = nc.tensor.transpose(bank(3)[:, 2 * AB * c:2 * AB * (c + 1)],
                                                   ab_row[0:2 * AB, c * P:(c + 1) * P], ident[0:2 * AB, 0:2 * AB])
                    last.then_inc(filled[3], 1)

                def k_rows(s, c):
                    use = k_job(s, c)
                    pe.wait_ge(wk_lo_done, KT)
                    u.free(use)
                    product(bank(use[0]), lambda k: xt(k, s * GROUP + c * P, P),
                            lambda k: pair(wqk_hi, wqk_lo, (KT + k) * D, D)).then_inc(filled[use[0]], 1)

                def v_rows(s, c):
                    use = v_job(s, c)
                    pe.wait_ge(wv_lo_done, KT)
                    u.free(use)
                    product(bank(use[0]), lambda k: xt(k, s * GROUP + c * P, P),
                            lambda k: pair(wv_hi, wv_lo, k * D, D)).then_inc(filled[use[0]], 1)

                def q_cols(s, h):
                    use = a_job(s, 3 + h)
                    pe.wait_ge(wq_lo_done, KT)
                    u.free(use)
                    product(bank(use[0]), lambda k: pair(wqk_hi, wqk_lo, k * D + h * P, P),
                            lambda k: xt(k, s * GROUP, GROUP)).then_inc(filled[use[0]], 1)

                def log_sums(s):
                    pe.wait_ge(gate_act, b * 6 + (3 * s + 2))
                    u.free((3, 6 * s + 1))
                    mm(bank(3)[:, 0:16], tri[:, :], g_la[:, :], True, True)
                    mm(bank(3)[:, 16:32], ones[:, :], g_la[:, :], True, True).then_inc(filled[3], 1)

                def k_turned(s, c):
                    pe.wait_ge(k_scaled, b * 8 + (4 * s + c + 1))
                    u.free((3, 6 * s + 2 + c))
                    for h in range(HEADS):
                        last = nc.tensor.transpose(bank(3)[:, h * P:(h + 1) * P],
                                                   kn[:, (c % 2) * D + h * P:(c % 2) * D + (h + 1) * P], ident[:, :])
                    last.then_inc(filled[3], 1)

                def scores(s, c):
                    n = 4 * s + c
                    if c == 0:
                        u.read_out(a_job(s, 5))
                        u.read_out(a_job(s, 6))
                    u.read_out((3, 6 * s + 2 + c))
                    u.free((5, 2 * n))
                    for h in range(HEADS):
                        last = mm(bank(5)[:, h * P:(h + 1) * P], kT[:, h * P:(h + 1) * P],
                                  qT[:, h * GROUP + c * P:h * GROUP + (c + 1) * P], True, True)
                    last.then_inc(filled[5], 1)

                def log_decay(s, c):
                    n = 4 * s + c
                    pe.wait_ge(steps_hi_ready, b * 8 + (n + 1))
                    pe.wait_ge(steps_lo_ready, b * 8 + (n + 1))
                    u.free((4, n))
                    mm(bank(4), after_r[:, :], steps_hi[:, :], True, False)
                    last = mm(bank(4), after_r[:, :], steps_lo[:, :], False, n < BT - 1)
                    if n == BT - 1:
                        last = mm(bank(4), ident_b[:, :], mask_b[:, :], False, True)
                    last.then_inc(filled[4], 1)

                def core(s, c):
                    n = 4 * s + c
                    if n > 0:
                        u.free((6, n - 1))
                        for h in range(HEADS):
                            last = mm(bank(6)[:, h * P:(h + 1) * P], qT[:, h * GROUP + c * P:h * GROUP + (c + 1) * P],
                                      state[:, h * P:(h + 1) * P], True, True)
                        last.then_inc(filled[6], 1)
                    u.read_out((5, 2 * n))
                    u.read_out(v_job(s, c))
                    u.free((7, n))
                    for h in range(HEADS):
                        last = mm(bank(7)[:, h * P:(h + 1) * P], attnT[:, h * P:(h + 1) * P],
                                  vn[:, (c % 2) * D + h * P:(c % 2) * D + (h + 1) * P], True, True)
                    last.then_inc(filled[7], 1)
                    if n == BT - 1:
                        return
                    pe.wait_ge(kw_ready, b * 7 + (n + 1))
                    for h in range(HEADS):
                        last = mm(bank(5)[:, h * P:(h + 1) * P], kw[:, h * P:(h + 1) * P],
                                  vn[:, (c % 2) * D + h * P:(c % 2) * D + (h + 1) * P], True, True)
                    last.then_inc(filled[5], 1)

                def head(s):
                    q_cols(s, 0)
                    q_cols(s, 1)
                    q_cols(s, 2)
                    log_sums(s)
                    q_cols(s, 3)

                logits(0)
                k_rows(0, 0)
                logits_turned(0)
                v_rows(0, 0)
                head(0)
                for s in range(2):
                    for c in range(4):
                        k_turned(s, c)
                        log_decay(s, c)
                        if c < 3:
                            k_rows(s, c + 1)
                        elif s == 0:
                            u.free((2, 4))
                            logits(1)
                            k_rows(1, 0)
                            logits_turned(1)
                        if c < 2:
                            turn_tile("A", b, 4 * s + 2 * c)
                        scores(s, c)
                        if c < 3:
                            v_rows(s, c + 1)
                        elif s == 0:
                            v_rows(1, 0)
                        if c < 2 and (s, c) != (1, 1):
                            turn_tile("A", b, 4 * s + 2 * c + 1)
                        if (s, c) == (1, 3):
                            turn_tile("A", b, 7)
                        core(s, c)
                        if c == 3 and s == 0:
                            head(1)

            def ffn(phase):
                pe.wait_ge(gu_ready, 8)
                with pe.Fori(0, BATCHES) as b:
                    u = Use(pe, phase, b)
                    u.free((2, 0))
                    u.free((3, 0))

                    def up(J, out, w0):
                        s, j = J // JT, J % JT
                        u.free((out, J))
                        for k in range(KT):
                            w = w_gu[:, (w0 + k) * HID + j * P:(w0 + k) * HID + (j + 1) * P]
                            xh, xl = xt(k, s * GROUP, GROUP)
                            mm(bank(out), w, xh, k == 0, False)
                            last = mm(bank(out), w, xl, False, k == KT - 1)
                        last.then_inc(filled[out], 1)

                    def down(J):
                        s, j = J // JT, J % JT
                        n = b * 22 + (44 * FFN_BASE[phase] + J)
                        if J == 0:
                            pe.wait_ge(wd_ready[phase], 8 if phase == "F1" else JT)
                        pe.wait_ge(hid_split, n + (RING + 1))
                        for t in range(4):
                            if j == 0:
                                u.free((4 + t, s))
                            o = (J % 4) * GROUP + t * P
                            mm(bank(4 + t), hid_hi[phase][:, o:o + P], cols(w_d[phase], j), j == 0, False)
                            last = mm(bank(4 + t), hid_lo[:, o:o + P], cols(w_d[phase], j), False, j == JT - 1)
                            if j == JT - 1:
                                last.then_inc(filled[4 + t], 1)
                        if j < JT - 1:
                            last.then_inc(down_done, 1)

                    for J in range(2 * JT):
                        s, j = J // JT, J % JT
                        if J == JT:
                            u.free((2, 2))
                            u.free((3, 2))
                        up(J, 0, 0)
                        up(J, 1, KT)
                        if J > 1:
                            down(J - 2)
                        if j in (3, 5, 7, 9):
                            turn_tile(phase, b, 4 * s + (j - 3) // 2)
                    down(2 * JT - 2)
                    down(2 * JT - 1)

            Use(pe, "A", 1).read_out((2, 7))
            ffn("F1")
            for bnk in (2, 3):
                Use(pe, "F1", 1).read_out((bnk, 3))

            um = Use(pe, "mid", 0)
            pe.wait_ge(qk_split, 16)
            for i in range(4):
                um.free((i % 2, i // 2))
                product(bank(i % 2), lambda k: pair(qk_hi, qk_lo, k * D + i * P, P),
                        lambda k: pair(qk_hi, qk_lo, (KT + k) * D, D)).then_inc(filled[i % 2], 1)
            pe.wait_ge(vo_split, 8)
            for i in range(4, 8):
                um.free((i % 2, i // 2))
                product(bank(i % 2), lambda k: pair(wvT_hi, wvT_lo, k * D + (i - 4) * P, P),
                        lambda k: pair(wo_hi, wo_lo, k * D, D)).then_inc(filled[i % 2], 1)

            with pe.Fori(0, BATCHES) as b:
                u = Use(pe, "B", b)

                def values(i):
                    job = i if i < 4 else 4 + i
                    u.free((job % 2, job // 2))
                    for k in range(KT):
                        if i == 0 and k > 1:
                            um.read_out((k % 2, 3))
                        xh, xl = xt(k, i * P, P)
                        mm(bank(job % 2), xh, cols(wvo_hi, k), k == 0, False)
                        mm(bank(job % 2), xh, cols(wvo_lo, k), False, False)
                        last = mm(bank(job % 2), xl, cols(wvo_hi, k), False, k == KT - 1)
                    last.then_inc(filled[job % 2], 1)

                def queries(s):
                    for m in range(4):
                        job = (4 if s == 0 else 12) + m
                        u.free((job % 2, job // 2))
                        product(bank(job % 2), lambda k: pair(g_hi, g_lo, k * D + m * P, P),
                                lambda k: xt(k, s * GROUP, GROUP)).then_inc(filled[job % 2], 1)

                def scores(i):
                    if i % 4 == 0:
                        for job in ((6, 7) if i == 0 else (14, 15)):
                            u.read_out((job % 2, job // 2))
                    u.free((4, i))
                    for half in range(2):
                        last = product(bank(4 + half), lambda k: pair(aT_hi, aT_lo, k * GROUP + (i % 4) * P, P),
                                       lambda k: xt(k, half * GROUP, GROUP))
                    last.then_inc(filled[4], 1)

                def turn_probs(i):
                    u.read_out((4, i))
                    u.free((2, i))
                    for t in range(BT):
                        last = nc.tensor.transpose(bank(2, 2)[:, t * P:(t + 1) * P], probs[:, t * P:(t + 1) * P],
                                                   ident[:, :])
                    last.then_inc(filled[2], 1)

                def attend(i, t0=0, t1=BT):
                    if i == 0:
                        for job in (10, 11):
                            u.read_out((job % 2, job // 2))
                    use = (6 + i % 2, 2 + i // 2)
                    if t0 == 0:
                        u.read_out((2, i))
                        u.free(use)
                    ph, pl = pT(i)
                    for t in range(t0, t1):
                        left, vh, vl = slice(t * P, (t + 1) * P), cols(v_hi, t), cols(v_lo, t)
                        mm(bank(use[0]), ph[:, left], vh, t == 0, False)
                        mm(bank(use[0]), ph[:, left], vl, False, False)
                        last = mm(bank(use[0]), pl[:, left], vh, False, t == BT - 1)
                    if t1 == BT:
                        last.then_inc(filled[use[0]], 1)

                values(0)
                values(1)
                turn_tile("B", b, 0)
                turn_tile("B", b, 1)
                u.free((4, 0))
                values(2)
                u.free((5, 0))
                values(3)
                turn_tile("B", b, 2)
                turn_tile("B", b, 3)
                queries(0)
                u.read_out((6, 1))
                u.read_out((7, 1))
                values(4)
                values(5)
                scores(0)
                values(6)
                values(7)
                turn_probs(0)
                for i in range(1, 7):
                    scores(i)
                    if i == 3:
                        queries(1)
                    attend(i - 1)
                    turn_probs(i)
                scores(7)
                turn_tile("B", b, 4)
                turn_tile("B", b, 5)
                attend(6, 0, 4)
                turn_probs(7)
                attend(6, 4, 8)
                turn_tile("B", b, 6)
                turn_tile("B", b, 7)
                attend(7)

            for l in range(4, 8):
                Use(pe, "B", 1).read_out(prep_use("B", l))
            ffn("F2")


def kernel(**inputs):
    import numpy as np
    import concourse.bacc as bacc
    from concourse.bass_utils import run_bass_kernel_spmd

    def a(name):
        return np.asarray(inputs["L0_" + name])

    def t(m):
        return np.ascontiguousarray(m.T)

    def col(v):
        return t(v.reshape(-1, P))

    x = a("attn_a_x")
    arrays = {
        "x": np.ascontiguousarray(x.reshape(-1, x.shape[-1])),
        "wq": a("attn_a_Wq"), "wk": a("attn_a_Wk"), "wv": a("attn_a_Wv"),
        "w_ab": np.concatenate([a("attn_a_Walpha"), a("attn_a_Wbeta")] * 2, axis=1),
        "b_ab": np.concatenate([a("attn_a_balpha"), a("attn_a_bbeta")]),
        "bq": col(a("attn_a_bq")), "bk": a("attn_a_bk"), "bv": a("attn_a_bv"),
        "wqT": t(a("attn_b_W_q")), "wkT": t(a("attn_b_W_k")), "wvT": t(a("attn_b_W_v")), "wo": a("attn_b_W_o"),
        "gateT": t(a("ffn_wq_gate")), "s_gate": col(a("ffn_s_gate")),
        "upT": t(a("ffn_wq_up")), "s_up": col(a("ffn_s_up")),
        "downT": t(a("ffn_wq_down")), "s_down": a("ffn_s_down"),
    }
    nc = bacc.Bacc("TRN2", target_bir_lowering=False, num_devices=1)
    args = {n: nc.dram_tensor(n, v.shape, mybir.dt.from_np(v.dtype), kind="ExternalInput").ap()
            for n, v in arrays.items()}
    args["out"] = nc.dram_tensor("out", arrays["x"].shape, F32, kind="ExternalOutput").ap()
    hybrid_layer_kernel(nc, **args)
    got = run_bass_kernel_spmd(nc, [arrays], core_ids=[0])
    return np.asarray(got.results[0]["out"]).reshape(x.shape)
```
